# Optimizing a Trainium2 kernel written in Bass

```python
import numpy as np
import jax
import jax.numpy as jnp

def _softmax(x, axis=-1):
    return jax.nn.softmax(x, axis=axis)

def _gelu(x):
    return jax.nn.gelu(x, approximate=True)

def _silu(x):
    return jax.nn.silu(x)

def _sigmoid(x):
    return jax.nn.sigmoid(x)

def _layernorm(x, axis=-1, eps=1e-05):
    m = jnp.mean(x, axis=axis, keepdims=True)
    v = jnp.var(x, axis=axis, keepdims=True)
    return (x - m) / jnp.sqrt(v + eps)

def _scatter_add(tgt, idx, src, axis=0):
    return tgt.at[idx].add(src)

def _segment_sum(src, seg, n):
    return jax.ops.segment_sum(src, seg, n)
kernel_name = 'mk_adaln_d2_jaxref_r8_929940'

def setup_inputs(seed: int=0):
    np.random.seed(seed)
    _w = jnp.asarray

    def _L0_attn_setup():
        import jax, jax.numpy as jnp
        import numpy as np
        SCALE = 0.04
        key = jax.random.key(seed)
        ks = jax.random.split(key, 6)
        B, S, D, H, DK = (8, 128, 128, 16, 64)
        std = 1.0 / np.sqrt(D)
        return {'x': jax.random.normal(ks[0], (B, S, D), dtype=jnp.float32), 'Wq': jax.random.normal(ks[1], (H, DK, D), dtype=jnp.float32) * std, 'Wk': jax.random.normal(ks[2], (H, DK, D), dtype=jnp.float32) * std, 'Wv': jax.random.normal(ks[3], (H, DK, D), dtype=jnp.float32) * std, 'Wo': jax.random.normal(ks[4], (D, H * DK), dtype=jnp.float32) * std, 'bo': jnp.zeros((D,), dtype=jnp.float32)}
    _L0_attn_in = _L0_attn_setup()

    def _L0_ffn_setup():
        import jax, jax.numpy as jnp
        import numpy as np
        DIM = 128
        DEPTH = 6
        HEADS = 16
        DIM_HEAD = 64
        WINDOW = 32
        INNER = HEADS * DIM_HEAD
        DIM_INNER = int(DIM * 4 * 2 / 3)
        QK_SCALE = 8.0

        def shift_tokens(t):
            a, s = jnp.split(t, 2, -1)
            s = jnp.pad(s, ((0, 0), (1, 0), (0, 0)))[:, :-1]
            return jnp.concatenate([a, s], -1)

        def l2norm(t):
            return t / jnp.maximum(jnp.linalg.norm(t, axis=-1, keepdims=True), 1e-12)

        def rotate_half(x):
            x1, x2 = jnp.split(x, 2, -1)
            return jnp.concatenate([-x2, x1], -1)

        def rotary_tables(n):
            half = jnp.arange(0, DIM_HEAD, 2, dtype=jnp.float32)
            inv_freq = 1.0 / 10000.0 ** (half / DIM_HEAD)
            t = jnp.arange(n, dtype=jnp.float32)
            freqs = t[:, None] * inv_freq[None, :]
            freqs = jnp.concatenate([freqs, freqs], -1)
            base_scale = (half + 0.4 * DIM_HEAD) / (1.4 * DIM_HEAD)
            power = (t - n // 2) / (WINDOW // 2)
            scale = base_scale[None, :] ** power[:, None]
            scale = jnp.concatenate([scale, scale], -1)
            return (freqs, scale)

        def local_attention(q, k, v):
            b, h, n, d = q.shape
            w = WINDOW
            nw = n // w
            bq = q.reshape(b, h, nw, w, d)
            bk = k.reshape(b, h, nw, w, d)
            bv = v.reshape(b, h, nw, w, d)

            def look(t):
                p = jnp.pad(t, ((0, 0), (0, 0), (1, 0), (0, 0), (0, 0)))
                return jnp.concatenate([p[:, :, :nw], p[:, :, 1:]], axis=3)
            bk2, bv2 = (look(bk), look(bv))
            seq = jnp.arange(n).reshape(nw, w)
            seq_p = jnp.pad(seq, ((1, 0), (0, 0)), constant_values=-1)
            jt = jnp.concatenate([seq_p[:nw], seq_p[1:]], axis=1)
            it = seq[:, :, None]
            jb = jt[:, None, :]
            mask = (it < jb) | (it > jb + w) | (jb == -1)
            sim = jnp.einsum('bhwie,bhwje->bhwij', bq, bk2) * QK_SCALE
            sim = jnp.where(mask, -jnp.finfo(sim.dtype).max, sim)
            attn = jax.nn.softmax(sim, -1)
            out = jnp.einsum('bhwij,bhwje->bhwie', attn, bv2)
            return out.reshape(b, h, n, d)

        def attn_layer(x, Wqkv, qs, ksc, Wo):
            b, n, _ = x.shape
            qkv = x @ Wqkv
            q, k, v = jnp.split(qkv, 3, -1)
            sh = lambda t: t.reshape(b, n, HEADS, DIM_HEAD).transpose(0, 2, 1, 3)
            q, k, v = (sh(q), sh(k), sh(v))
            q = l2norm(q) * qs
            k = l2norm(k) * ksc
            freqs, scale = rotary_tables(n)
            cos, sin = (jnp.cos(freqs), jnp.sin(freqs))
            q = q * cos * scale + rotate_half(q) * sin * scale
            inv = 1.0 / scale
            k = k * cos * inv + rotate_half(k) * sin * inv
            out = local_attention(q, k, v)
            out = out.transpose(0, 2, 1, 3).reshape(b, n, INNER)
            return out @ Wo

        def ffn_layer(x, g, bln, W1, b1, W2, b2):
            mu = x.mean(-1, keepdims=True)
            var = ((x - mu) ** 2).mean(-1, keepdims=True)
            xn = (x - mu) / jnp.sqrt(var + 1e-05) * g + bln
            hg = xn @ W1 + b1
            a, gate = jnp.split(hg, 2, -1)
            return a * jax.nn.gelu(gate, approximate=False) @ W2 + b2
        key = jax.random.key(seed)
        ks = jax.random.split(key, 8)
        B, N = (2, 256)
        init = lambda k, shape: jax.random.normal(k, shape, jnp.float32) * 0.02
        return {'x': jax.random.normal(ks[0], (B, N, DIM), jnp.float32), 'Wqkv': init(ks[1], (DEPTH, DIM, 3 * INNER)), 'q_scale': jnp.ones((DEPTH, DIM_HEAD), jnp.float32), 'k_scale': jnp.ones((DEPTH, DIM_HEAD), jnp.float32), 'Wo': init(ks[2], (DEPTH, INNER, DIM)), 'ln_g': jnp.ones((DEPTH, DIM), jnp.float32), 'ln_b': jnp.zeros((DEPTH, DIM), jnp.float32), 'W1': init(ks[3], (DEPTH, DIM, 2 * DIM_INNER)), 'b1': jnp.zeros((DEPTH, 2 * DIM_INNER), jnp.float32), 'W2': init(ks[4], (DEPTH, DIM_INNER, DIM)), 'b2': jnp.zeros((DEPTH, DIM), jnp.float32)}
    _L0_ffn_in = _L0_ffn_setup()
    _L0_c = _w((lambda *s: np.random.randn(*s).astype(np.float32) * 0.05)(8, 128))
    _L0_wmod = _w((lambda *s: np.random.randn(*s).astype(np.float32) * 0.05)(128, 6 * 128) * 128 ** (-0.5))

    def _L1_attn_setup():
        import jax, jax.numpy as jnp
        import numpy as np
        H = 16
        D = 64
        BQ = 64
        BKV = 64

        def _flash_tiled(q, k, v, scale):
            B, nh, S, d = q.shape
            nq, nkv = (S // BQ, S // BKV)
            qb = q.reshape(B, nh, nq, BQ, d)
            kb = k.reshape(B, nh, nkv, BKV, d).transpose(2, 0, 1, 3, 4)
            vb = v.reshape(B, nh, nkv, BKV, d).transpose(2, 0, 1, 3, 4)
            o0 = jnp.zeros((B, nh, nq, BQ, d), q.dtype)
            m0 = jnp.full((B, nh, nq, BQ), -jnp.inf, q.dtype)
            l0 = jnp.zeros((B, nh, nq, BQ), q.dtype)

            def step(carry, kv):
                o, m, l = carry
                kj, vj = kv
                s = jnp.einsum('bhnqd,bhkd->bhnqk', qb, kj) * scale
                m_new = jnp.maximum(m, s.max(axis=-1))
                p = jnp.exp(s - m_new[..., None])
                alpha = jnp.exp(m - m_new)
                l_new = alpha * l + p.sum(axis=-1)
                o_new = (alpha[..., None] * o + jnp.einsum('bhnqk,bhkd->bhnqd', p, vj)) / l_new[..., None]
                return ((o_new, m_new, l_new), None)
            (o, _, _), _ = jax.lax.scan(step, (o0, m0, l0), (kb, vb))
            return o.reshape(B, nh, S, d)
        key = jax.random.key(seed)
        ks = jax.random.split(key, 5)
        B, S, dim = (2, 256, 128)
        x = jax.random.normal(ks[0], (B, S, dim), dtype=jnp.float32)
        Wq = jax.random.normal(ks[1], (dim, H * D), dtype=jnp.float32) * 0.02
        Wk = jax.random.normal(ks[2], (dim, H * D), dtype=jnp.float32) * 0.02
        Wv = jax.random.normal(ks[3], (dim, H * D), dtype=jnp.float32) * 0.02
        Wo = jax.random.normal(ks[4], (H * D, dim), dtype=jnp.float32) * 0.02
        return {'x': x, 'Wq': Wq, 'Wk': Wk, 'Wv': Wv, 'Wo': Wo}
    _L1_attn_in = _L1_attn_setup()

    def _L1_ffn_setup():
        import jax, jax.numpy as jnp
        import numpy as np
        BLOCK = 16
        _GRID = jnp.array([0.0, 0.5, 1.0, 1.5, 2.0, 3.0, 4.0, 6.0], dtype=jnp.float32)
        _MID = jnp.array([0.25, 0.75, 1.25, 1.75, 2.5, 3.5, 5.0], dtype=jnp.float32)

        def fp4_quant_dequant(x):
            shape = x.shape
            xb = x.reshape(shape[:-1] + (shape[-1] // BLOCK, BLOCK))
            scale = jnp.max(jnp.abs(xb), axis=-1, keepdims=True) / 6.0
            scale = jnp.maximum(scale, jnp.float32(1e-12))
            xn = xb / scale
            idx = jnp.searchsorted(_MID, jnp.abs(xn))
            q = _GRID[idx] * jnp.sign(xn) * scale
            return q.reshape(shape)

        def fp4_linear(x, w):
            xq = fp4_quant_dequant(x)
            wq = fp4_quant_dequant(w)
            return jnp.einsum('bsk,nk->bsn', xq, wq)
        key = jax.random.key(seed)
        k1, k2, k3, k4 = jax.random.split(key, 4)
        H, I = (128, 352)
        x = jax.random.normal(k1, (4, 512, H), dtype=jnp.float32)
        w_gate = jax.random.normal(k2, (I, H), dtype=jnp.float32) * 0.02
        w_up = jax.random.normal(k3, (I, H), dtype=jnp.float32) * 0.02
        w_down = jax.random.normal(k4, (H, I), dtype=jnp.float32) * 0.02
        return {'x': x, 'w_gate': w_gate, 'w_up': w_up, 'w_down': w_down}
    _L1_ffn_in = _L1_ffn_setup()
    _L1_c = _w((lambda *s: np.random.randn(*s).astype(np.float32) * 0.05)(8, 128))
    _L1_wmod = _w((lambda *s: np.random.randn(*s).astype(np.float32) * 0.05)(128, 6 * 128) * 128 ** (-0.5))
    _d = {'L0_attn_x': _L0_attn_in['x'], 'L0_attn_Wq': _L0_attn_in['Wq'], 'L0_attn_Wk': _L0_attn_in['Wk'], 'L0_attn_Wv': _L0_attn_in['Wv'], 'L0_attn_Wo': _L0_attn_in['Wo'], 'L0_attn_bo': _L0_attn_in['bo'], 'L0_ffn_Wqkv': _L0_ffn_in['Wqkv'], 'L0_ffn_q_scale': _L0_ffn_in['q_scale'], 'L0_ffn_k_scale': _L0_ffn_in['k_scale'], 'L0_ffn_Wo': _L0_ffn_in['Wo'], 'L0_ffn_ln_g': _L0_ffn_in['ln_g'], 'L0_ffn_ln_b': _L0_ffn_in['ln_b'], 'L0_ffn_W1': _L0_ffn_in['W1'], 'L0_ffn_b1': _L0_ffn_in['b1'], 'L0_ffn_W2': _L0_ffn_in['W2'], 'L0_ffn_b2': _L0_ffn_in['b2'], 'L0_c': _L0_c, 'L0_wmod': _L0_wmod, 'L1_attn_Wq': _L1_attn_in['Wq'], 'L1_attn_Wk': _L1_attn_in['Wk'], 'L1_attn_Wv': _L1_attn_in['Wv'], 'L1_attn_Wo': _L1_attn_in['Wo'], 'L1_ffn_w_gate': _L1_ffn_in['w_gate'], 'L1_ffn_w_up': _L1_ffn_in['w_up'], 'L1_ffn_w_down': _L1_ffn_in['w_down'], 'L1_c': _L1_c, 'L1_wmod': _L1_wmod}
    _x0 = _d['L0_attn_x']
    _d['L0_attn_x'] = jax.random.normal(jax.random.fold_in(jax.random.key(seed), 1), (8, 256, 128), dtype=_x0.dtype)
    del _x0
    return _d

def reference(L0_attn_x, L0_attn_Wq, L0_attn_Wk, L0_attn_Wv, L0_attn_Wo, L0_attn_bo, L0_ffn_Wqkv, L0_ffn_q_scale, L0_ffn_k_scale, L0_ffn_Wo, L0_ffn_ln_g, L0_ffn_ln_b, L0_ffn_W1, L0_ffn_b1, L0_ffn_W2, L0_ffn_b2, L0_c, L0_wmod, L1_attn_Wq, L1_attn_Wk, L1_attn_Wv, L1_attn_Wo, L1_ffn_w_gate, L1_ffn_w_up, L1_ffn_w_down, L1_c, L1_wmod):

    def _L0_attn_ref(x, Wq, Wk, Wv, Wo, bo):
        import jax, jax.numpy as jnp
        import numpy as np
        SCALE = 0.04
        B, S, D = x.shape
        H, DK, _ = Wq.shape
        q = jnp.einsum('bsd,hkd->bhsk', x, Wq)
        k = jnp.einsum('bsd,hkd->bhsk', x, Wk)
        v = jnp.einsum('bsd,hkd->bhsk', x, Wv)
        scores = jnp.einsum('bhsk,bhtk->bhst', q, k)
        scores = jnp.where(scores == 0, jnp.float32(-1000000000.0), scores)
        attn = jax.nn.softmax(scores / SCALE, axis=-1)
        z = jnp.einsum('bhst,bhtk->bhsk', attn, v)
        z = z.transpose(0, 2, 1, 3).reshape(B, S, H * DK)
        return z @ Wo.T + bo

    def _L0_ffn_ref(x, Wqkv, q_scale, k_scale, Wo, ln_g, ln_b, W1, b1, W2, b2):
        import jax, jax.numpy as jnp
        import numpy as np
        DIM = 128
        DEPTH = 6
        HEADS = 16
        DIM_HEAD = 64
        WINDOW = 32
        INNER = HEADS * DIM_HEAD
        DIM_INNER = int(DIM * 4 * 2 / 3)
        QK_SCALE = 8.0

        def shift_tokens(t):
            a, s = jnp.split(t, 2, -1)
            s = jnp.pad(s, ((0, 0), (1, 0), (0, 0)))[:, :-1]
            return jnp.concatenate([a, s], -1)

        def l2norm(t):
            return t / jnp.maximum(jnp.linalg.norm(t, axis=-1, keepdims=True), 1e-12)

        def rotate_half(x):
            x1, x2 = jnp.split(x, 2, -1)
            return jnp.concatenate([-x2, x1], -1)

        def rotary_tables(n):
            half = jnp.arange(0, DIM_HEAD, 2, dtype=jnp.float32)
            inv_freq = 1.0 / 10000.0 ** (half / DIM_HEAD)
            t = jnp.arange(n, dtype=jnp.float32)
            freqs = t[:, None] * inv_freq[None, :]
            freqs = jnp.concatenate([freqs, freqs], -1)
            base_scale = (half + 0.4 * DIM_HEAD) / (1.4 * DIM_HEAD)
            power = (t - n // 2) / (WINDOW // 2)
            scale = base_scale[None, :] ** power[:, None]
            scale = jnp.concatenate([scale, scale], -1)
            return (freqs, scale)

        def local_attention(q, k, v):
            b, h, n, d = q.shape
            w = WINDOW
            nw = n // w
            bq = q.reshape(b, h, nw, w, d)
            bk = k.reshape(b, h, nw, w, d)
            bv = v.reshape(b, h, nw, w, d)

            def look(t):
                p = jnp.pad(t, ((0, 0), (0, 0), (1, 0), (0, 0), (0, 0)))
                return jnp.concatenate([p[:, :, :nw], p[:, :, 1:]], axis=3)
            bk2, bv2 = (look(bk), look(bv))
            seq = jnp.arange(n).reshape(nw, w)
            seq_p = jnp.pad(seq, ((1, 0), (0, 0)), constant_values=-1)
            jt = jnp.concatenate([seq_p[:nw], seq_p[1:]], axis=1)
            it = seq[:, :, None]
            jb = jt[:, None, :]
            mask = (it < jb) | (it > jb + w) | (jb == -1)
            sim = jnp.einsum('bhwie,bhwje->bhwij', bq, bk2) * QK_SCALE
            sim = jnp.where(mask, -jnp.finfo(sim.dtype).max, sim)
            attn = jax.nn.softmax(sim, -1)
            out = jnp.einsum('bhwij,bhwje->bhwie', attn, bv2)
            return out.reshape(b, h, n, d)

        def attn_layer(x, Wqkv, qs, ksc, Wo):
            b, n, _ = x.shape
            qkv = x @ Wqkv
            q, k, v = jnp.split(qkv, 3, -1)
            sh = lambda t: t.reshape(b, n, HEADS, DIM_HEAD).transpose(0, 2, 1, 3)
            q, k, v = (sh(q), sh(k), sh(v))
            q = l2norm(q) * qs
            k = l2norm(k) * ksc
            freqs, scale = rotary_tables(n)
            cos, sin = (jnp.cos(freqs), jnp.sin(freqs))
            q = q * cos * scale + rotate_half(q) * sin * scale
            inv = 1.0 / scale
            k = k * cos * inv + rotate_half(k) * sin * inv
            out = local_attention(q, k, v)
            out = out.transpose(0, 2, 1, 3).reshape(b, n, INNER)
            return out @ Wo

        def ffn_layer(x, g, bln, W1, b1, W2, b2):
            mu = x.mean(-1, keepdims=True)
            var = ((x - mu) ** 2).mean(-1, keepdims=True)
            xn = (x - mu) / jnp.sqrt(var + 1e-05) * g + bln
            hg = xn @ W1 + b1
            a, gate = jnp.split(hg, 2, -1)
            return a * jax.nn.gelu(gate, approximate=False) @ W2 + b2
        for i in range(DEPTH):
            x = attn_layer(shift_tokens(x), Wqkv[i], q_scale[i], k_scale[i], Wo[i]) + x
            x = ffn_layer(shift_tokens(x), ln_g[i], ln_b[i], W1[i], b1[i], W2[i], b2[i]) + x
        return x

    def _L1_attn_ref(x, Wq, Wk, Wv, Wo):
        import jax, jax.numpy as jnp
        import numpy as np
        H = 16
        D = 64
        BQ = 64
        BKV = 64

        def _flash_tiled(q, k, v, scale):
            B, nh, S, d = q.shape
            nq, nkv = (S // BQ, S // BKV)
            qb = q.reshape(B, nh, nq, BQ, d)
            kb = k.reshape(B, nh, nkv, BKV, d).transpose(2, 0, 1, 3, 4)
            vb = v.reshape(B, nh, nkv, BKV, d).transpose(2, 0, 1, 3, 4)
            o0 = jnp.zeros((B, nh, nq, BQ, d), q.dtype)
            m0 = jnp.full((B, nh, nq, BQ), -jnp.inf, q.dtype)
            l0 = jnp.zeros((B, nh, nq, BQ), q.dtype)

            def step(carry, kv):
                o, m, l = carry
                kj, vj = kv
                s = jnp.einsum('bhnqd,bhkd->bhnqk', qb, kj) * scale
                m_new = jnp.maximum(m, s.max(axis=-1))
                p = jnp.exp(s - m_new[..., None])
                alpha = jnp.exp(m - m_new)
                l_new = alpha * l + p.sum(axis=-1)
                o_new = (alpha[..., None] * o + jnp.einsum('bhnqk,bhkd->bhnqd', p, vj)) / l_new[..., None]
                return ((o_new, m_new, l_new), None)
            (o, _, _), _ = jax.lax.scan(step, (o0, m0, l0), (kb, vb))
            return o.reshape(B, nh, S, d)
        B, S, dim = x.shape
        scale = D ** (-0.5)
        q = (x @ Wq).reshape(B, S, H, D).transpose(0, 2, 1, 3)
        k = (x @ Wk).reshape(B, S, H, D).transpose(0, 2, 1, 3)
        v = (x @ Wv).reshape(B, S, H, D).transpose(0, 2, 1, 3)
        o = _flash_tiled(q, k, v, scale)
        out = o.transpose(0, 2, 1, 3).reshape(B, S, H * D)
        return out @ Wo

    def _L1_ffn_ref(x, w_gate, w_up, w_down):
        import jax, jax.numpy as jnp
        import numpy as np
        BLOCK = 16
        _GRID = jnp.array([0.0, 0.5, 1.0, 1.5, 2.0, 3.0, 4.0, 6.0], dtype=jnp.float32)
        _MID = jnp.array([0.25, 0.75, 1.25, 1.75, 2.5, 3.5, 5.0], dtype=jnp.float32)

        def fp4_quant_dequant(x):
            shape = x.shape
            xb = x.reshape(shape[:-1] + (shape[-1] // BLOCK, BLOCK))
            scale = jnp.max(jnp.abs(xb), axis=-1, keepdims=True) / 6.0
            scale = jnp.maximum(scale, jnp.float32(1e-12))
            xn = xb / scale
            idx = jnp.searchsorted(_MID, jnp.abs(xn))
            q = _GRID[idx] * jnp.sign(xn) * scale
            return q.reshape(shape)

        def fp4_linear(x, w):
            xq = fp4_quant_dequant(x)
            wq = fp4_quant_dequant(w)
            return jnp.einsum('bsk,nk->bsn', xq, wq)
        gate = fp4_linear(x, w_gate)
        y = fp4_linear(x, w_up)
        h = jax.nn.silu(gate) * y
        return fp4_linear(h, w_down)
    x = L0_attn_x
    mod = (_silu(L0_c) @ L0_wmod).reshape(L0_c.shape[0], 6, 1, -1)
    sa, ca, ga, sb, cb, gb = (mod[:, 0], mod[:, 1], mod[:, 2], mod[:, 3], mod[:, 4], mod[:, 5])
    ga = (2 * (ga >= 0) - 1) * jnp.maximum(jnp.abs(ga), 0.25)
    gb = (2 * (gb >= 0) - 1) * jnp.maximum(jnp.abs(gb), 0.25)
    h = _layernorm(x, axis=-1) * (1 + ca) + sa
    x = x + ga * _L0_attn_ref(h, L0_attn_Wq, L0_attn_Wk, L0_attn_Wv, L0_attn_Wo, L0_attn_bo)
    h = _layernorm(x, axis=-1) * (1 + cb) + sb
    x = x + gb * _L0_ffn_ref(h, L0_ffn_Wqkv, L0_ffn_q_scale, L0_ffn_k_scale, L0_ffn_Wo, L0_ffn_ln_g, L0_ffn_ln_b, L0_ffn_W1, L0_ffn_b1, L0_ffn_W2, L0_ffn_b2)
    mod = (_silu(L1_c) @ L1_wmod).reshape(L1_c.shape[0], 6, 1, -1)
    sa, ca, ga, sb, cb, gb = (mod[:, 0], mod[:, 1], mod[:, 2], mod[:, 3], mod[:, 4], mod[:, 5])
    ga = (2 * (ga >= 0) - 1) * jnp.maximum(jnp.abs(ga), 0.25)
    gb = (2 * (gb >= 0) - 1) * jnp.maximum(jnp.abs(gb), 0.25)
    h = _layernorm(x, axis=-1) * (1 + ca) + sa
    x = x + ga * _L1_attn_ref(h, L1_attn_Wq, L1_attn_Wk, L1_attn_Wv, L1_attn_Wo)
    h = _layernorm(x, axis=-1) * (1 + cb) + sb
    x = x + gb * _L1_ffn_ref(h, L1_ffn_w_gate, L1_ffn_w_up, L1_ffn_w_down)
    return x

_drawn_inputs = setup_inputs


def setup_inputs(seed=0):
    import zlib

    import numpy as np

    out = dict(_drawn_inputs(seed))
    spreads = {'L0_attn_bo': (0.0, 0.396),
     'L0_ffn_q_scale': (1.0, 0.6),
     'L0_ffn_k_scale': (1.0, 0.6),
     'L0_ffn_ln_g': (1.0, 0.6),
     'L0_ffn_ln_b': (0.0, 0.8),
     'L0_ffn_b1': (0.0, 0.8),
     'L0_ffn_b2': (0.0, 0.444)}
    factors = {'L0_ffn_W1': 8.0,
     'L0_ffn_W2': 8.0,
     'L1_attn_Wq': 8.0,
     'L1_attn_Wk': 8.0,
     'L1_attn_Wv': 8.0,
     'L1_attn_Wo': 8.0,
     'L1_ffn_w_gate': 8.0,
     'L1_ffn_w_up': 8.0,
     'L1_ffn_w_down': 8.0,
     'L1_c': 8.0,
     'L1_wmod': 8.0}
    for name, (base, spread) in spreads.items():
        noise = np.random.default_rng([zlib.crc32(name.encode()), seed]).standard_normal(out[name].shape)
        drawn = base * np.exp(spread * noise) if base else spread * noise
        out[name] = jnp.asarray(drawn.astype(out[name].dtype))
    for name, factor in factors.items():
        out[name] = (out[name] * factor).astype(out[name].dtype)
    return out
```

```python
from contextlib import ExitStack

import numpy as np

import concourse.bass as bass
from concourse import mybir

ALU = mybir.AluOpType
ACT = mybir.ActivationFunctionType
AX = mybir.AxisListType
F32 = mybir.dt.float32
BF16 = mybir.dt.bfloat16

P = 128
B, S = 8, 256
T = B * S
DH = 64
PAIRS = 8
INNER = PAIRS * P
DEPTH = 6
WIN = 32
FI = 341
FCH = [(0, 128), (128, 128), (256, FI - 256)]
QI = 352
QCH = [(0, 128), (128, 128), (256, QI - 256)]
CH = 512
NCH = T // CH
SC0 = float(np.float32(1.0) / np.float32(0.04))
LN_EPS = 1e-5
NSCALE, NFLOOR, NBIAS = float(2.0 ** 24), float(2.0 ** -62), float(12 * np.log(2.0))
MASKED = -1.0e30

C_G, C_B, C_B2, C_B1A, C_B1G, C_QS, C_QSR, C_KS, C_KSR, NV = 0, 1, 2, 3, 6, 9, 10, 11, 12, 13


class Chain:

    def __init__(self, e, sem, base):
        self.e, self.sem, self.base, self.n = e, sem, base, 0

    def __call__(self, instruction):
        self.n += 1
        instruction.then_inc(self.sem, 1)
        self.e.wait_ge(self.sem, self.base + self.n)


def build(nc, xT, cT, wmod, bo, w0, w1, wl, f1, f2, cols, tabs, mask, mats, wgu, wd, out):
    ctx = ExitStack()
    with ctx:
        def sb(name, shape, dt=F32):
            return ctx.enter_context(nc.sbuf_tensor(name, shape, dt))

        def sem(name):
            return ctx.enter_context(nc.semaphore(name))

        X = sb("X", [P, T])
        R = sb("R", [P, T])
        H = sb("H", [P, T])
        WB = sb("WB", [P, 4 * INNER])
        WA = sb("WA", [P, 6 * INNER])
        W1 = sb("W1", [P, 2 * FI])
        W2 = sb("W2", [P, 3, P])
        CO = sb("CO", [P, DEPTH * NV])
        TAB = sb("TAB", [P, 4, S])
        LT = sb("LT", [P, 4, S])
        MSK = sb("MSK", [P, 256])
        MSKB = sb("MSKB", [P, 256], BF16)
        MAT = sb("MAT", [P, 3, P])
        IDB = sb("IDB", [P, P], BF16)
        CT = sb("CT", [P, 2, B])
        CE = sb("CE", [P, 2, B])
        CR = sb("CR", [P, 2, B])
        WM = sb("WM", [P, 2, 6 * P])
        MOD = sb("MOD", [P, 2, 6, B])
        MT = sb("MT", [P, 2, 2, 2, B])
        BO = sb("BO", [P, 2])
        KC = sb("KC", [P, 4])
        xs = sb("xs", [P, S])
        sq = sb("sq", [P, 2, 512])
        t1 = sb("t1", [P, 2, 512])
        t2 = sb("t2", [P, 2, 512])
        rl = sb("rl", [P, 2, 260])
        rn = sb("rn", [P, 2, 260])
        k1 = sb("k1", [P, 2, S])
        qz = sb("qz", [P, 2, 2, S])
        kT = sb("kT", [P, 2, WIN + S])
        vb = sb("vb", [P, 4, 2, P])
        mx = sb("mx", [P, 2, 16])
        sm = sb("sm", [P, 2, 16])
        rq = sb("rq", [P, 2, 4])
        nb = sb("nb", [P, 2, 4])
        rs = sb("rs", [P, 2, 16])
        al = sb("al", [P, 2, 16])
        dl = sb("dl", [P, 2, 16])
        ls = sb("ls", [P, 2, 16])
        wt = sb("wt", [P, 2, 16])
        s1 = sb("s1", [P, 2, 1024])
        pe_ = sb("pe_", [P, 2, 1024])
        pn = sb("pn", [P, 2, 1024])
        pt = sb("pt", [P, 2, 2, 2, S])
        ot = sb("ot", [P, 2, S])
        yr = sb("yr", [P, S])
        xc = sb("xc", [P, T])
        xq = sb("xq", [P, T])
        hg = sb("hg", [P, 2, 3, CH])
        ga = sb("ga", [P, 3, CH])
        WG = sb("WG", [P, 2, 3, P])
        WD = sb("WD", [P, QI])
        WGT = sb("WGT", [P, 2, QI])
        WDT = sb("WDT", [P, 3, P])
        NQ = 2 * QI
        fa, fsn, fx, fc, ft, fh, fg = (WA[:, i * NQ:(i + 1) * NQ] for i in range(7))
        fs = sb("fs", [P, NQ // 16])
        fr = sb("fr", [P, NQ // 16])
        hT = sb("hT", [P, S])
        h3 = sb("h3", [P, 3, S])

        PS = ctx.enter_context(nc.psum_tensor("PS", [P, 8, 512], F32))

        s_in = sem("s_in")
        s_wb = sem("s_wb")
        s_wa = sem("s_wa")
        s_wf = sem("s_wf")
        s_wq = sem("s_wq")
        s_out = sem("s_out")
        s_pass = sem("s_pass")
        s_bar = sem("s_bar")
        s_v = sem("s_v")
        s_c = sem("s_c")
        s_m = sem("s_m")
        s_xs = sem("s_xs")
        s_qk = sem("s_qk")
        s_rot = sem("s_rot")
        s_vp = sem("s_vp")
        s_sq = sem("s_sq")
        s_ssq = sem("s_ssq")
        s_t1 = sem("s_t1")
        s_t2 = sem("s_t2")
        s_ln = sem("s_ln")
        s_rn = sem("s_rn")
        s_add = sem("s_add")
        s_pl = sem("s_pl")
        s_pz = sem("s_pz")
        s_kn = sem("s_kn")
        s_vev = sem("s_vev")
        s_sc = sem("s_sc")
        s_mx = sem("s_mx")
        s_nb = sem("s_nb")
        s_exp = sem("s_exp")
        s_rs = sem("s_rs")
        s_pn = sem("s_pn")
        s_pt = sem("s_pt")
        s_av = sem("s_av")
        s_oev = sem("s_oev")
        s_wo = sem("s_wo")
        s_y = sem("s_y")
        s_res = sem("s_res")
        g_xs = sem("g_xs")
        g_qk = sem("g_qk")
        g_vp = sem("g_vp")
        g_qev = sem("g_qev")
        g_vev = sem("g_vev")
        g_sc = sem("g_sc")
        g_d = sem("g_d")
        g_mx = sem("g_mx")
        g_exp = sem("g_exp")
        g_w = sem("g_w")
        g_pn = sem("g_pn")
        g_tp = sem("g_tp")
        g_pta = sem("g_pta")
        g_ptv = sem("g_ptv")
        g_av = sem("g_av")
        g_oev = sem("g_oev")
        g_wo = sem("g_wo")
        g_y = sem("g_y")
        g_res = sem("g_res")
        n_x = sem("n_x")
        n_mu = sem("n_mu")
        n_xc = sem("n_xc")
        n_sq = sem("n_sq")
        n_var = sem("n_var")
        n_ln = sem("n_ln")
        n_rs = sem("n_rs")
        n_xn = sem("n_xn")
        f_hg = sem("f_hg")
        f_ge = sem("f_ge")
        f_gu = sem("f_gu")
        f_y = sem("f_y")
        f_res = sem("f_res")
        q_pe = sem("q_pe")
        q_act = sem("q_act")
        q_dve = sem("q_dve")

        FROM_ONE = [f_ge, f_gu, f_hg, f_res, f_y, g_av, g_d, g_exp, g_mx,
                    g_oev, g_pn, g_pta, g_ptv, g_qev, g_qk, g_res, g_sc, g_tp,
                    g_vev, g_vp, g_w, g_wo, g_xs, n_ln, n_mu, n_rs, n_sq,
                    n_var, n_x, n_xc, n_xn, q_act, q_dve, q_pe, s_add, s_av,
                    s_exp, s_kn, s_ln, s_mx, s_nb, s_oev, s_pl, s_pn, s_pt,
                    s_qk, s_res, s_rn, s_rot, s_rs, s_sc, s_sq, s_ssq, s_t1,
                    s_t2, s_vev, s_vp, s_wo, s_xs]

        ONES, MEAN, IDN = MAT[:, 0, :], MAT[:, 1, :], MAT[:, 2, :]

        def wait_apart(e, sem, value):
            e.wait_ge(sem, value)
            e.sem_inc(s_pass, 1)

        def barrier(e, k):
            e.drain().then_inc(s_bar, 1)
            wait_apart(e, s_bar, (k + 1) * 5)

        LAYER0 = 4
        AFTER = LAYER0 + 3 * DEPTH

        def ln_dve(e, call, src, dst, shift, affine):
            c0 = call * NCH
            if shift:
                for c in range(NCH):
                    for hb in range(2):
                        a = c * CH + hb * S
                        e.tensor_copy(xq[0:DH, a:a + S], src[0:DH, a:a + S])
                        e.memset(xq[DH:P, a:a + 1], 0.0)
                        i = e.tensor_copy(xq[DH:P, a + 1:a + S], src[DH:P, a:a + S - 1])
                    i.then_inc(n_x, 1)
            for c in range(NCH):
                a = c * CH
                e.wait_ge(n_mu, 1 + c0 + (c + 1))
                e.tensor_tensor(xc[:, a:a + CH], (xq if shift else src)[:, a:a + CH], PS[:, c, :],
                                ALU.subtract).then_inc(n_xc, 1)
            for c in range(NCH):
                a = c * CH
                e.wait_ge(n_rs, 1 + c0 + (c + 1))
                e.tensor_tensor(xc[:, a:a + CH], xc[:, a:a + CH], xq[:, a:a + CH],
                                ALU.mult).then_inc(n_xn, 1)
                e.wait_ge(n_xn, 1 + c0 + (c + 1))
                for hb in range(2):
                    g, o = affine(2 * c + hb)
                    e.tensor_scalar(dst[:, a + hb * S:a + hb * S + S], xc[:, a + hb * S:a + hb * S + S],
                                    g, o, ALU.mult, ALU.add)

        def ln_pe(e, call, src, shift, shifts):
            c0 = call * NCH
            for c in range(NCH):
                a = c * CH
                if shift:
                    e.wait_ge(n_x, 1 + shifts * NCH + (c + 1))
                e.matmul(PS[:, c, :], MEAN, (xq if shift else src)[:, a:a + CH],
                         start=True, stop=True).then_inc(n_mu, 1)
            for c in range(NCH):
                e.wait_ge(n_sq, 1 + c0 + (c + 1))
                e.matmul(PS[:, 4 + c, :], MEAN, xq[:, c * CH:(c + 1) * CH],
                         start=True, stop=True).then_inc(n_var, 1)

        def ln_act(e, call):
            c0 = call * NCH
            for c in range(NCH):
                a = c * CH
                e.wait_ge(n_xc, 1 + c0 + (c + 1))
                e.activation(xq[:, a:a + CH], xc[:, a:a + CH], ACT.Square).then_inc(n_sq, 1)
            for c in range(NCH):
                a = c * CH
                e.wait_ge(n_var, 1 + c0 + (c + 1))
                e.activation(xq[:, a:a + CH], PS[:, 4 + c, :], ACT.Ln, bias=KC[:, 2:3]).then_inc(n_ln, 1)
                e.wait_ge(n_ln, 1 + c0 + (c + 1))
                e.activation(xq[:, a:a + CH], xq[:, a:a + CH], ACT.Exp, scale=-0.5).then_inc(n_rs, 1)

        NS = PAIRS
        HPV = 5 * INNER

        def local_pe(e, l):
            wait_apart(e, s_wa, (l + 1) * 16)
            with e.Fori(0, B) as b:
                n0 = l * (B * NS) + b * NS

                def project(t):
                    n, p = n0 + t, t % 2
                    if t == 0:
                        e.wait_ge(s_xs, 1 + (l * B + b + 1) * 2)
                        e.wait_ge(s_t1, 1 + n)
                    else:
                        e.wait_ge(s_t1, 1 + n - 1)
                    w = t * 512
                    e.matmul(PS[:, p, 0:S], WA[:, w:w + P], xs[:, :], start=True, stop=True)
                    e.matmul(PS[:, p, S:2 * S], WA[:, w + P:w + 2 * P], xs[:, :],
                             start=True, stop=True).then_inc(s_qk, 1)
                    e.wait_ge(s_t2, 1 + n)
                    e.matmul(PS[:, 2, 0:S], WA[:, w + 2 * P:w + 3 * P], xs[:, :], start=True, stop=True)
                    e.matmul(PS[:, 2, S:2 * S], WA[:, w + 3 * P:w + 4 * P], xs[:, :],
                             start=True, stop=True).then_inc(s_rot, 1)
                    e.wait_ge(s_vev, 1 + n)
                    for j in range(2):
                        i = e.matmul(PS[:, 5, j * P:(j + 1) * P], xs[:, j * P:(j + 1) * P],
                                     WA[:, 4 * INNER + t * P:4 * INNER + (t + 1) * P],
                                     start=True, stop=True)
                    i.then_inc(s_vp, 1)

                def norms(t):
                    n, p = n0 + t, t % 2
                    e.wait_ge(s_sq, 1 + n + 1)
                    e.wait_ge(s_ln, 1 + n)
                    e.matmul(PS[:, 3, 0:S], ONES, sq[:, p, S:2 * S], start=True, stop=True)
                    for j in range(2):
                        i = e.matmul(PS[:, 3, S + 2 * j:S + 2 * j + 2], sq[:, p, j * P:(j + 1) * P],
                                     MAT[:, 0, 0:P:DH], start=True, stop=True)
                    i.then_inc(s_ssq, 1)

                def scores(t):
                    n, p = n0 + t, t % 2
                    e.wait_ge(s_exp, 1 + n)
                    e.wait_ge(s_add, 1 + n + 1)
                    e.wait_ge(s_kn, 1 + n + 1)
                    e.matmul(PS[:, 4, 0:256], IDB[:, :], MSKB[:, :], start=True, stop=False,
                             skip_group_check=True)
                    for j in range(2):
                        for h in range(2):
                            for u in range(4):
                                w = j * P + u * WIN
                                o = (2 * j + h) * 64
                                i = e.matmul(PS[u * WIN:(u + 1) * WIN, 4, o:o + 64],
                                             qz[:, p, h, w:w + WIN], kT[:, p, w:w + 64],
                                             start=False, stop=(j == h == 1), skip_group_check=True)
                    i.then_inc(s_sc, 1)

                def values(t):
                    n, p = n0 + t, t % 2
                    e.wait_ge(s_pt, 1 + n + 1)
                    e.wait_ge(s_oev, 1 + n)
                    for h in range(2):
                        o = PS[h * DH:(h + 1) * DH, 6, :]
                        e.matmul(o[:, 0:S], vb[:, t % 4, 0, h * DH:(h + 1) * DH], pt[:, p, 0, h, :],
                                 start=True, stop=False, skip_group_check=True)
                        i = e.matmul(o[:, P:S], vb[:, t % 4, 1, h * DH:(h + 1) * DH],
                                     pt[:, p, 1, h, 0:P], start=False, stop=True, skip_group_check=True)
                    i.then_inc(s_av, 1)

                def project_out(t):
                    n, p = n0 + t, t % 2
                    e.wait_ge(s_oev, 1 + n + 1)
                    if t == 0:
                        e.wait_ge(s_res, 1 + l * B + b)
                    i = e.matmul(PS[:, 7, 0:S], WA[:, HPV + t * P:HPV + (t + 1) * P], ot[:, p, :],
                                 start=(t == 0), stop=(t == NS - 1))
                    i.then_inc(s_wo, 1)

                for s in range(NS + 3):
                    if s < NS:
                        project(s)
                    if s >= 3:
                        project_out(s - 3)
                    if s < NS:
                        norms(s)
                    if 1 <= s <= NS:
                        scores(s - 1)
                    if 2 <= s <= NS + 1:
                        values(s - 2)

        def local_act(e, l):
            with e.Fori(0, B) as b:
                n0 = l * (B * NS) + b * NS

                def squares(t):
                    n, p = n0 + t, t % 2
                    e.wait_ge(s_qk, 1 + n + 1)
                    e.wait_ge(s_ssq, 1 + (n if t == 0 else n - 1))
                    e.activation(sq[:, p, :], PS[:, p, :], ACT.Square).then_inc(s_sq, 1)
                    e.wait_ge(s_vp, 1 + n + 1)
                    e.wait_ge(s_av, 1 + (n0 if t < 4 else n - 3))
                    e.activation(vb[:, t % 4, :, :], PS[:, 5, 0:2 * P].rearrange("p (j d) -> p j d", j=2),
                                 ACT.Copy).then_inc(s_vev, 1)

                def norms(t):
                    n, p = n0 + t, t % 2
                    e.wait_ge(s_ssq, 1 + n + 1)
                    e.wait_ge(s_rn, 1 + n)
                    e.activation(rl[:, p, :], PS[:, 3, 0:260], ACT.Ln, bias=KC[:, 0:1],
                                 scale=NSCALE).then_inc(s_ln, 1)
                    e.wait_ge(s_ln, 1 + n + 1)
                    e.wait_ge(s_kn, 1 + (n if t == 0 else n - 1))
                    e.wait_ge(s_nb, 1 + (n if t == 0 else n - 1))
                    e.activation(rn[:, p, :], rl[:, p, :], ACT.Exp, bias=KC[:, 1:2],
                                 scale=-0.5).then_inc(s_rn, 1)

                def exps(t):
                    n, p = n0 + t, t % 2
                    e.wait_ge(s_nb, 1 + n + 1)
                    e.wait_ge(s_pn, 1 + (n if t == 0 else n - 1))
                    e.wait_ge(s_rs, 1 + (n if t == 0 else n - 1))
                    for g in range(4):
                        i = e.activation(pe_[:, p, g * 64:(g + 1) * 64], PS[:, 4, g * 64:(g + 1) * 64],
                                         ACT.Exp, bias=nb[:, p, g:g + 1], scale=rq[:, p, g:g + 1],
                                         accum_out=sm[:, p, g:g + 1])
                    i.then_inc(s_exp, 1)

                def evac(t):
                    n, p = n0 + t, t % 2
                    e.wait_ge(s_av, 1 + n + 1)
                    e.wait_ge(s_wo, 1 + (n if t == 0 else n - 1))
                    e.activation(ot[:, p, :], PS[:, 6, 0:S], ACT.Copy).then_inc(s_oev, 1)

                for s in range(NS + 2):
                    if s < NS:
                        squares(s)
                    if s >= 2:
                        evac(s - 2)
                    if s < NS:
                        norms(s)
                    if 1 <= s <= NS:
                        exps(s - 1)

        def local_dve(e, l, lv, lt_base):
            for i, col in enumerate((C_QS, C_KS, C_QSR, C_KSR)):
                k = e.tensor_scalar(LT[:, i, :], TAB[:, i, :], CO[:, bass.ds(lv + col, 1)], None, ALU.mult)
            k.then_inc(s_v, 1)
            wait_apart(e, s_v, lt_base + l + 1)
            with e.Fori(0, B) as b:
                n0 = l * (B * NS) + b * NS
                e.wait_ge(s_vp, 1 + n0)
                e.tensor_copy(xs[0:DH, :], R[0:DH, bass.ds(b * S, S)]).then_inc(s_xs, 1)
                e.tensor_copy(xs[DH:P, 1:S], R[DH:P, bass.ds(b * S, S - 1)]).then_inc(s_xs, 1)

                def rotary(t):
                    n, p = n0 + t, t % 2
                    e.wait_ge(s_sq, 1 + n + 1)
                    e.wait_ge(s_add, 1 + (n if t == 0 else n - 1))
                    e.tensor_tensor(t1[:, p, :], PS[:, p, :], LT[:, 0:2, :].rearrange("p a n -> p (a n)"),
                                    ALU.mult).then_inc(s_t1, 1)
                    e.wait_ge(s_rot, 1 + n + 1)
                    e.tensor_tensor(t2[:, p, :], PS[:, 2, :], LT[:, 2:4, :].rearrange("p a n -> p (a n)"),
                                    ALU.mult).then_inc(s_t2, 1)

                def keys(t):
                    n, p = n0 + t, t % 2
                    e.wait_ge(s_rn, 1 + n + 1)
                    e.wait_ge(s_add, 1 + n + 1)
                    e.wait_ge(s_sc, 1 + (n if t == 0 else n - 1))
                    e.scalar_tensor_tensor(out=kT[:, p, WIN:], in0=rn[:, p, 0:S], scalar=1e12,
                                           in1=k1[:, p, :], op0=ALU.min, op1=ALU.mult).then_inc(s_kn, 1)

                def maxima(t):
                    n, p = n0 + t, t % 2
                    e.wait_ge(s_exp, 1 + (n if t == 0 else n - 1))
                    e.tensor_scalar(rq[:, p, :], rn[:, p, S:S + 4], 1e12, None, ALU.min)
                    e.wait_ge(s_sc, 1 + n + 1)
                    e.tensor_reduce(mx[:, p, 0:4], PS[:, 4, 0:256].rearrange("p (g k) -> p g k", g=4),
                                    AX.X, ALU.max).then_inc(s_mx, 1)
                    e.wait_ge(s_mx, 1 + n + 1)
                    e.scalar_tensor_tensor(out=nb[:, p, :], in0=mx[:, p, 0:4], scalar=-1.0,
                                           in1=rq[:, p, :], op0=ALU.mult, op1=ALU.mult).then_inc(s_nb, 1)

                def sums(t):
                    n, p = n0 + t, t % 2
                    e.wait_ge(s_exp, 1 + n + 1)
                    e.wait_ge(s_pn, 1 + (n if t == 0 else n - 1))
                    e.reciprocal(rs[:, p, 0:4], sm[:, p, 0:4]).then_inc(s_rs, 1)

                def turn(t):
                    n, p = n0 + t, t % 2
                    e.wait_ge(s_pn, 1 + n + 1)
                    e.wait_ge(s_av, 1 + (n if t == 0 else n - 1))
                    v = pn[:, p, 0:256].rearrange("p (j h f k) -> p j h f k", j=2, h=2, f=2)
                    for u in range(4):
                        a = u * WIN
                        e.transpose(pt[a:a + WIN, p, :, :, a:a + WIN], v[a:a + WIN, :, :, 1, :])
                        if u:
                            e.transpose(pt[a - WIN:a, p, :, :, a:a + WIN], v[a:a + WIN, :, :, 0, :])
                    e.transpose(pt[P - WIN:P, p, 0, :, P:P + WIN],
                                v[0:WIN, 1, :, 0, :]).then_inc(s_pt, 1)

                for s in range(NS + 2):
                    if s < NS:
                        rotary(s)
                    if 1 <= s <= NS:
                        maxima(s - 1)
                    if s >= 2:
                        turn(s - 2)
                    if s < NS:
                        keys(s)
                    if 1 <= s <= NS:
                        sums(s - 1)
                e.wait_ge(s_wo, 1 + n0 + NS)
                e.tensor_tensor(R[:, bass.ds(b * S, S)], PS[:, 7, 0:S], R[:, bass.ds(b * S, S)],
                                ALU.add).then_inc(s_res, 1)

        def local_pool(e, l):
            with e.Fori(0, B) as b:
                n0 = l * (B * NS) + b * NS
                for s in range(NS + 1):
                    if s < NS:
                        n, p = n0 + s, s % 2
                        e.wait_ge(s_t1, 1 + n + 1)
                        e.wait_ge(s_t2, 1 + n + 1)
                        e.wait_ge(s_kn, 1 + (n if s == 0 else n - 1))
                        e.wait_ge(s_sc, 1 + (n if s == 0 else n - 1))
                        e.tensor_tensor(k1[:, p, :], t1[:, p, S:], t2[:, p, S:],
                                        ALU.add).then_inc(s_pl, 1)
                        for h in range(2):
                            r = slice(h * DH, (h + 1) * DH)
                            i = e.tensor_tensor(qz[r, p, h, :], t1[r, p, 0:S], t2[r, p, 0:S], ALU.add)
                            if h == 0:
                                i.then_inc(s_pl, 1)
                                e.wait_ge(s_pl, 1 + 2 * n + 2)
                        i.then_inc(s_add, 1)
                        e.wait_ge(s_add, 1 + n + 1)
                    if s >= 1:
                        n, p = n0 + s - 1, (s - 1) % 2
                        e.wait_ge(s_rs, 1 + n + 1)
                        e.wait_ge(s_pt, 1 + (n if s == 1 else n - 1))
                        e.tensor_tensor(pn[:, p, 0:256].rearrange("p (g k) -> p g k", g=4),
                                        pe_[:, p, 0:256].rearrange("p (g k) -> p g k", g=4),
                                        rs[:, p, 0:4].rearrange("p (g o) -> p g o", o=1)
                                        .broadcast_to([P, 4, 64]), ALU.mult).then_inc(s_pn, 1)

        def block_pe(e, k):
            e.wait_ge(s_wb, (k + 1) * 16)
            with e.Fori(0, B) as b:
                n0 = k * (B * NS) + b * NS

                def project(t):
                    n = n0 + t
                    if t == 0:
                        e.wait_ge(g_xs, 1 + k * B + b + 1)
                    e.wait_ge(g_qev, 1 + n)
                    e.matmul(PS[:, 0, 0:S], WB[:, t * P:(t + 1) * P], xs[:, :], start=True, stop=True)
                    e.matmul(PS[:, 0, S:2 * S], WB[:, INNER + t * P:INNER + (t + 1) * P], xs[:, :],
                             start=True, stop=True).then_inc(g_qk, 1)
                    e.wait_ge(g_vev, 1 + n)
                    for j in range(2):
                        i = e.matmul(PS[:, 1, j * P:(j + 1) * P], xs[:, j * P:(j + 1) * P],
                                     WB[:, 2 * INNER + t * P:2 * INNER + (t + 1) * P],
                                     start=True, stop=True)
                    i.then_inc(g_vp, 1)

                def scores(t):
                    n, p = n0 + t, t % 2
                    e.wait_ge(g_qev, 1 + n + 1)
                    e.wait_ge(g_d, 1 + n)
                    for j in range(2):
                        for h in range(2):
                            i = e.matmul(PS[:, 2 + j, h * S:(h + 1) * S], qz[:, p, h, j * P:(j + 1) * P],
                                         kT[:, p, WIN:], start=True, stop=True)
                    i.then_inc(g_sc, 1)

                def turn(t):
                    n, p = n0 + t, t % 2
                    e.wait_ge(g_pn, 1 + n + 1)
                    e.wait_ge(g_pta, 1 + n)
                    e.wait_ge(g_ptv, 1 + n)
                    for h in range(2):
                        for kt in range(2):
                            for j in range(2):
                                o = kt * S + j * P
                                c = (2 * j + h) * S + kt * P
                                i = e.transpose(PS[:, 4 + h, o:o + P], pn[:, p, c:c + P], IDN)
                    i.then_inc(g_tp, 1)

                def values(t):
                    n, p = n0 + t, t % 2
                    e.wait_ge(g_pta, 1 + n + 1)
                    e.wait_ge(g_ptv, 1 + n + 1)
                    e.wait_ge(g_oev, 1 + n)
                    for h in range(2):
                        for kt in range(2):
                            i = e.matmul(PS[h * DH:(h + 1) * DH, 6, 0:S],
                                         vb[:, t % 4, kt, h * DH:(h + 1) * DH], pt[:, p, h, kt, :],
                                         start=(kt == 0), stop=(kt == 1), skip_group_check=True)
                    i.then_inc(g_av, 1)

                def project_out(t):
                    n, p = n0 + t, t % 2
                    e.wait_ge(g_oev, 1 + n + 1)
                    if t == 0:
                        e.wait_ge(g_res, 1 + k * B + b)
                    i = e.matmul(PS[:, 7, 0:S], WB[:, 3 * INNER + t * P:3 * INNER + (t + 1) * P],
                                 ot[:, p, :], start=(t == 0), stop=(t == NS - 1))
                    i.then_inc(g_wo, 1)

                for s in range(NS + 4):
                    if s < NS:
                        project(s)
                    if 1 <= s <= NS:
                        scores(s - 1)
                    if 2 <= s <= NS + 1:
                        turn(s - 2)
                    if 3 <= s <= NS + 2:
                        values(s - 3)
                    if s >= 4:
                        project_out(s - 4)

        def block_act(e, k):
            with e.Fori(0, B) as b:
                n0 = k * (B * NS) + b * NS

                def evac_qkv(t):
                    n, p = n0 + t, t % 2
                    e.wait_ge(g_qk, 1 + n + 1)
                    e.wait_ge(g_sc, 1 + (n if t == 0 else n - 1))
                    for h in range(2):
                        r = slice(h * DH, (h + 1) * DH)
                        e.activation(qz[r, p, h, :], PS[r, 0, 0:S], ACT.Copy)
                    e.activation(kT[:, p, WIN:], PS[:, 0, S:2 * S], ACT.Copy).then_inc(g_qev, 1)
                    e.wait_ge(g_vp, 1 + n + 1)
                    e.wait_ge(g_av, 1 + (n0 if t < 4 else n - 3))
                    e.activation(vb[:, t % 4, :, :], PS[:, 1, 0:2 * P].rearrange("p (j d) -> p j d", j=2),
                                 ACT.Copy).then_inc(g_vev, 1)

                def exps(t):
                    n, p = n0 + t, t % 2
                    e.wait_ge(g_d if k else g_mx, 1 + n + 1)
                    e.wait_ge(g_pn, 1 + (n if t == 0 else n - 1))
                    e.wait_ge(g_w, 1 + (n if t == 0 else n - 1))
                    if k == 0:
                        for g in range(4):
                            i = e.activation(pe_[:, p, g * S:(g + 1) * S], s1[:, p, g * S:(g + 1) * S],
                                             ACT.Exp, bias=nb[:, p, g:g + 1], scale=SC0,
                                             accum_out=sm[:, p, g:g + 1])
                        i.then_inc(g_exp, 1)
                    else:
                        e.activation(al[:, p, 4:16], dl[:, p, 4:16], ACT.Exp, scale=DH ** -0.5)
                        e.activation(pe_[:, p, :], s1[:, p, :], ACT.Exp,
                                     scale=DH ** -0.5).then_inc(g_exp, 1)

                def evac_pt(t):
                    n, p = n0 + t, t % 2
                    e.wait_ge(g_tp, 1 + n + 1)
                    e.wait_ge(g_av, 1 + (n if t == 0 else n - 1))
                    e.activation(pt[:, p, 0, :, :].rearrange("p a n -> p (a n)"), PS[:, 4, :],
                                 ACT.Copy).then_inc(g_pta, 1)

                def evac_o(t):
                    n, p = n0 + t, t % 2
                    e.wait_ge(g_av, 1 + n + 1)
                    e.wait_ge(g_wo, 1 + (n if t == 0 else n - 1))
                    e.activation(ot[:, p, :], PS[:, 6, 0:S], ACT.Copy).then_inc(g_oev, 1)

                for s in range(NS + 4):
                    if s < NS:
                        evac_qkv(s)
                    if 1 <= s <= NS:
                        exps(s - 1)
                    if 2 <= s <= NS + 1:
                        evac_pt(s - 2)
                    if 3 <= s <= NS + 2:
                        evac_o(s - 3)

        def block_dve(e, k):
            with e.Fori(0, B) as b:
                n0 = k * (B * NS) + b * NS
                chain = Chain(e, s_v, B_CHAIN0[k] + b * B_CHAIN[k])
                e.wait_ge(g_vp, 1 + n0)
                e.tensor_copy(xs[:, :], H[:, bass.ds(b * S, S)]).then_inc(g_xs, 1)

                def soft(t):
                    n, p = n0 + t, t % 2
                    e.wait_ge(g_sc, 1 + n + 1)
                    e.wait_ge(g_exp, 1 + (n if t == 0 else n - 1))
                    if k == 0:
                        sv = PS[:, 2:4, :]
                        s1v = s1[:, p, :].rearrange("p (a n) -> p a n", a=2)
                        chain(e.tensor_scalar(s1v, sv, 0.0, -1.0e9, ALU.is_equal, ALU.mult))
                        e.tensor_tensor(s1v, sv, s1v, ALU.add).then_inc(g_d, 1)
                        e.wait_ge(g_d, 1 + n + 1)
                        chain(e.tensor_reduce(mx[:, p, 0:4], s1[:, p, :].rearrange("p (g q) -> p g q", g=4),
                                              AX.X, ALU.max))
                        e.tensor_scalar(nb[:, p, :], mx[:, p, 0:4], -SC0, None, ALU.mult).then_inc(g_mx, 1)
                    else:
                        for j in range(2):
                            i = e.tensor_reduce(
                                mx[:, p, :].rearrange("p (k g) -> p g k", k=4)[:, 2 * j:2 * j + 2, :],
                                PS[:, 2 + j, :].rearrange("p (h k q) -> p h k q", h=2, k=4),
                                AX.X, ALU.max)
                        chain(i)
                        for i in range(1, 4):
                            chain(e.tensor_tensor(mx[:, p, 4 * i:4 * i + 4], mx[:, p, 4 * i - 4:4 * i],
                                                  mx[:, p, 4 * i:4 * i + 4], ALU.max))
                        e.tensor_tensor(dl[:, p, 4:16], mx[:, p, 0:12], mx[:, p, 4:16], ALU.subtract)
                        for j in range(2):
                            m = mx[:, p, :].rearrange("p (k g o) -> p g k o", k=4, o=1)
                            i = e.tensor_tensor(
                                s1[:, p, j * 512:(j + 1) * 512].rearrange("p (h k q) -> p h k q", h=2, k=4),
                                PS[:, 2 + j, :].rearrange("p (h k q) -> p h k q", h=2, k=4),
                                m[:, 2 * j:2 * j + 2, :, :].broadcast_to([P, 2, 4, 64]), ALU.subtract)
                        i.then_inc(g_d, 1)

                def weights(t):
                    n, p = n0 + t, t % 2
                    e.wait_ge(g_exp, 1 + n + 1)
                    e.wait_ge(g_pn, 1 + (n if t == 0 else n - 1))
                    if k == 0:
                        e.reciprocal(rs[:, p, 0:4], sm[:, p, 0:4]).then_inc(g_w, 1)
                        return
                    chain(e.tensor_reduce(ls[:, p, :].rearrange("p (k g) -> p g k", k=4),
                                          pe_[:, p, :].rearrange("p (g k q) -> p g k q", g=4, k=4),
                                          AX.X, ALU.add))
                    for i in range(1, 4):
                        c, c1 = slice(4 * i, 4 * i + 4), slice(4 * i - 4, 4 * i)
                        chain(e.tensor_tensor(sm[:, p, c], al[:, p, c], ls[:, p, c1], ALU.mult))
                        chain(e.tensor_tensor(ls[:, p, c], ls[:, p, c], sm[:, p, c], ALU.add))
                    chain(e.reciprocal(wt[:, p, :], ls[:, p, :]))
                    for i in (2, 1, 0):
                        c, c1 = slice(4 * i, 4 * i + 4), slice(4 * i + 4, 4 * i + 8)
                        chain(e.tensor_tensor(rs[:, p, c], wt[:, p, c1], al[:, p, c1], ALU.mult))
                        j = e.tensor_tensor(wt[:, p, c], wt[:, p, c], rs[:, p, c], ALU.mult)
                        if i:
                            chain(j)
                        else:
                            j.then_inc(g_w, 1)

                def evac_pt(t):
                    n, p = n0 + t, t % 2
                    e.wait_ge(g_tp, 1 + n + 1)
                    e.wait_ge(g_av, 1 + (n if t == 0 else n - 1))
                    e.tensor_copy(pt[:, p, 1, :, :].rearrange("p a n -> p (a n)"),
                                  PS[:, 5, :]).then_inc(g_ptv, 1)

                for s in range(NS + 2):
                    if s < NS:
                        soft(s)
                    if s >= 2:
                        evac_pt(s - 2)
                    if 1 <= s <= NS:
                        weights(s - 1)
                e.wait_ge(g_wo, 1 + n0 + NS)
                chain(e.tensor_scalar(yr[:, :], PS[:, 7, 0:S], BO[:, k:k + 1], MOD[:, k, 2, bass.ds(b, 1)],
                                      ALU.add, ALU.mult))
                e.tensor_tensor(X[:, bass.ds(b * S, S)], X[:, bass.ds(b * S, S)], yr[:, :],
                                ALU.add).then_inc(g_res, 1)
                assert chain.n == B_CHAIN[k], chain.n

        def block_pool(e, k):
            with e.Fori(0, B) as b:
                n0 = k * (B * NS) + b * NS
                for t in range(NS):
                    n, p = n0 + t, t % 2
                    e.wait_ge(g_w, 1 + n + 1)
                    e.wait_ge(g_tp, 1 + (n if t == 0 else n - 1))
                    if k == 0:
                        v = [a[:, p, :].rearrange("p (g q) -> p g q", g=4) for a in (pn, pe_)]
                        f = rs[:, p, 0:4].rearrange("p (g o) -> p g o", o=1).broadcast_to([P, 4, S])
                    else:
                        v = [a[:, p, :].rearrange("p (g k q) -> p g k q", g=4, k=4) for a in (pn, pe_)]
                        f = wt[:, p, :].rearrange("p (k g o) -> p g k o", k=4, o=1).broadcast_to([P, 4, 4, 64])
                    e.tensor_tensor(v[0], v[1], f, ALU.mult).then_inc(g_pn, 1)

        def ffn_pe(e, l):
            e.wait_ge(s_wf, (l + 1) * 48)
            def hidden(c):
                for i, (o, w) in enumerate(FCH):
                    if c:
                        e.wait_ge(f_gu, 1 + l * 12 + (c - 1) * 3 + i + 1)
                    x = H[:, c * CH:(c + 1) * CH]
                    e.matmul(PS[0:w, 2 * i, :], W1[:, o:o + w], x, start=True, stop=True)
                    e.matmul(PS[0:w, 2 * i + 1, :], W1[:, FI + o:FI + o + w], x,
                             start=True, stop=True).then_inc(f_hg, 1)

            def down(c):
                e.wait_ge(f_gu, 1 + l * 12 + 3 * (c + 1))
                if c >= 2:
                    e.wait_ge(f_res, 1 + l * 4 + c - 1)
                for i, (o, w) in enumerate(FCH):
                    j = e.matmul(PS[:, 6 + c % 2, :], W2[0:w, i, :], hg[0:w, c % 2, i, :],
                                 start=(i == 0), stop=(i == 2))
                j.then_inc(f_y, 1)

            hidden(0)
            for c in range(1, NCH):
                hidden(c)
                down(c - 1)
            down(NCH - 1)

        def ffn_act(e, l, lv):
            for c in range(NCH):
                for i, (o, w) in enumerate(FCH):
                    if c:
                        e.wait_ge(f_gu, 1 + l * 12 + (c - 1) * 3 + i + 1)
                    wait_apart(e, f_hg, 1 + l * 12 + 3 * c + i + 1)
                    e.activation(ga[0:w, i, :], PS[0:w, 2 * i + 1, :], ACT.Gelu,
                                 bias=CO[0:w, bass.ds(lv + C_B1G + i, 1)]).then_inc(f_ge, 1)

        def ffn_dve(e, l, lv):
            def residual(c):
                e.wait_ge(f_y, 1 + l * 4 + c + 1)
                r = R[:, c * CH:(c + 1) * CH]
                e.scalar_tensor_tensor(out=r, in0=PS[:, 6 + c % 2, :], scalar=CO[:, bass.ds(lv + C_B2, 1)],
                                       in1=r, op0=ALU.add, op1=ALU.add).then_inc(f_res, 1)
            for c in range(NCH):
                for i, (o, w) in enumerate(FCH):
                    e.wait_ge(f_ge, 1 + l * 12 + 3 * c + i + 1)
                    if c >= 2 and i == 0:
                        e.wait_ge(f_y, 1 + l * 4 + c - 1)
                    e.scalar_tensor_tensor(out=hg[0:w, c % 2, i, :], in0=PS[0:w, 2 * i, :],
                                           scalar=CO[0:w, bass.ds(lv + C_B1A + i, 1)], in1=ga[0:w, i, :],
                                           op0=ALU.add, op1=ALU.mult).then_inc(f_gu, 1)
                if c:
                    residual(c - 1)
            residual(NCH - 1)

        def quantize(e, chain, r, x, out, n):
            a, c, t = fa[0:r, 0:n], fc[0:r, 0:n], ft[0:r, 0:n]
            sc, rc = fs[0:r, 0:n // 16], fr[0:r, 0:n // 16]

            def blocks(v):
                return v.rearrange("p (b q) -> p b q", q=16)

            def spread(v):
                return v.rearrange("p (b o) -> p b o", o=1).broadcast_to([r, n // 16, 16])

            chain(e.scalar_tensor_tensor(out=a, in0=x, scalar=-1.0, in1=x, op0=ALU.mult, op1=ALU.max))
            e.tensor_scalar(fsn[0:r, 0:n], x, 0.0, 2.0, ALU.is_ge, ALU.mult)
            chain(e.tensor_reduce(sc, blocks(a), AX.X, ALU.max))
            chain(e.tensor_scalar(sc, sc, 1.0 / 6.0, 1e-12, ALU.mult, ALU.max))
            chain(e.reciprocal(rc, sc))
            chain(e.tensor_tensor(blocks(a), blocks(a), spread(rc), ALU.mult))
            e.tensor_scalar(c, a, 0.25, None, ALU.is_gt)
            chain(e.tensor_scalar(t, a, 5.0, 2.0, ALU.is_gt, ALU.mult))
            for m, v in ((0.75, c), (2.5, t), (1.25, c), (3.5, t), (1.75, c)):
                chain(e.scalar_tensor_tensor(out=v, in0=a, scalar=m, in1=v, op0=ALU.is_gt, op1=ALU.add))
            chain(e.scalar_tensor_tensor(out=c, in0=c, scalar=0.5, in1=t, op0=ALU.mult, op1=ALU.add))
            chain(e.scalar_tensor_tensor(out=c, in0=fsn[0:r, 0:n], scalar=-1.0, in1=c,
                                         op0=ALU.add, op1=ALU.mult))
            return e.tensor_tensor(blocks(out), blocks(c), spread(sc), ALU.mult)

        QC = 13
        W_TILES = [(k, i, w) for k in range(2) for i, (o, w) in enumerate(QCH)]

        def fp4w_dve(e):
            chain = Chain(e, s_v, W_CHAIN0)
            for k, i, w in W_TILES:
                quantize(e, chain, w, WG[0:w, k, i, :], WG[0:w, k, i, :], P).then_inc(q_dve, 1)
                e.wait_ge(q_dve, 1 + 3 * k + i + 1)
            quantize(e, chain, P, WD[:, :], WD[:, :], QI).then_inc(q_dve, 1)
            e.wait_ge(q_dve, 1 + 7)
            assert chain.n == 7 * QC

        def fp4w_pe(e):
            for k, i, w in W_TILES:
                e.wait_ge(q_dve, 1 + 3 * k + i + 1)
                o = QCH[i][0]
                e.transpose(PS[:, k, o:o + w], WG[0:w, k, i, :], MAT[0:w, 2, 0:w]).then_inc(q_pe, 1)
            e.wait_ge(q_dve, 1 + 7)
            for i, (o, w) in enumerate(QCH):
                e.transpose(PS[0:w, 2, i * P:(i + 1) * P], WD[:, o:o + w], IDN).then_inc(q_pe, 1)

        def fp4w_act(e):
            e.wait_ge(q_pe, 1 + 9)
            e.activation(WGT[:, :, :], PS[:, 0:2, 0:QI], ACT.Copy)
            for i, (o, w) in enumerate(QCH):
                j = e.activation(WDT[0:w, i, :], PS[0:w, 2, i * P:(i + 1) * P], ACT.Copy)
            j.then_inc(q_act, 1)

        def fp4_pe(e):
            e.wait_ge(q_act, 1 + 1)
            with e.Fori(0, B) as b:
                p0, a0, d0 = 9 + b * 5, 1 + b * 5, 7 + b * 3
                e.wait_ge(q_act, 1 + a0 + 1)
                e.wait_ge(q_dve, 1 + d0)
                for j in range(2):
                    i = e.transpose(PS[:, 0, j * P:(j + 1) * P], hT[:, j * P:(j + 1) * P], IDN)
                i.then_inc(q_pe, 1)
                e.wait_ge(q_dve, 1 + d0 + 1)
                for j in range(2):
                    i = e.transpose(PS[:, 1, j * P:(j + 1) * P], fh[:, j * P:(j + 1) * P], IDN)
                i.then_inc(q_pe, 1)
                e.wait_ge(q_act, 1 + a0 + 3)
                for j in range(2):
                    for k in range(2):
                        i = e.matmul(PS[:, 2 + 2 * k + j, 0:QI], hT[:, j * P:(j + 1) * P], WGT[:, k, :],
                                     start=True, stop=True)
                i.then_inc(q_pe, 1)
                e.wait_ge(q_dve, 1 + d0 + 2)
                for i, (o, w) in enumerate(QCH):
                    for j in range(2):
                        x = e.transpose(PS[0:w, (0, 1, 6)[i], j * P:(j + 1) * P],
                                        fh[:, j * QI + o:j * QI + o + w], IDN)
                x.then_inc(q_pe, 1)
                e.wait_ge(q_act, 1 + a0 + 5)
                for i, (o, w) in enumerate(QCH):
                    x = e.matmul(PS[:, 7, 0:S], WDT[0:w, i, :], h3[0:w, i, :],
                                 start=(i == 0), stop=(i == 2))
                x.then_inc(q_pe, 1)

        def fp4_act(e):
            with e.Fori(0, B) as b:
                p0, a0 = 9 + b * 5, 1 + b * 5
                e.wait_ge(q_pe, 1 + p0)
                e.activation(hT[:, :], H[:, bass.ds(b * S, S)], ACT.Copy).then_inc(q_act, 1)
                e.wait_ge(q_pe, 1 + p0 + 1)
                e.activation(fx[:, 0:S], PS[:, 0, 0:S], ACT.Copy).then_inc(q_act, 1)
                e.wait_ge(q_pe, 1 + p0 + 2)
                e.activation(hT[:, :], PS[:, 1, 0:S], ACT.Copy).then_inc(q_act, 1)
                e.wait_ge(q_pe, 1 + p0 + 3)
                e.activation(fg[:, :].rearrange("p (j n) -> p j n", j=2), PS[:, 2:4, 0:QI],
                             ACT.Silu).then_inc(q_act, 1)
                e.wait_ge(q_pe, 1 + p0 + 4)
                for i, (o, w) in enumerate(QCH):
                    x = e.activation(h3[0:w, i, :], PS[0:w, (0, 1, 6)[i], 0:S], ACT.Copy)
                x.then_inc(q_act, 1)

        def fp4_dve(e):
            with e.Fori(0, B) as b:
                p0, a0, d0 = 9 + b * 5, 1 + b * 5, 7 + b * 3
                chain = Chain(e, s_v, W_CHAIN0 + 7 * QC + b * (2 * QC + 1))
                e.wait_ge(q_act, 1 + a0 + 2)
                quantize(e, chain, P, fx[:, 0:S], fh[:, 0:S], S).then_inc(q_dve, 1)
                e.wait_ge(q_act, 1 + a0 + 4)
                chain(e.tensor_tensor(fx[:, :].rearrange("p (j n) -> p j n", j=2), PS[:, 4:6, 0:QI],
                                      fg[:, :].rearrange("p (j n) -> p j n", j=2), ALU.mult))
                quantize(e, chain, P, fx[:, :], fh[:, :], NQ).then_inc(q_dve, 1)
                e.wait_ge(q_pe, 1 + p0 + 5)
                x = X[:, bass.ds(b * S, S)]
                e.scalar_tensor_tensor(out=x, in0=PS[:, 7, 0:S], scalar=MOD[:, 1, 5, bass.ds(b, 1)],
                                       in1=x, op0=ALU.mult, op1=ALU.add).then_inc(q_dve, 1)
                assert chain.n == 2 * QC + 1

        M_CHAIN = 8
        B_CHAIN = (NS * 2 + 1, NS * (4 + 1 + 6 + 1 + 3 + 2) + 1)
        B_CHAIN0 = (M_CHAIN, M_CHAIN + B * B_CHAIN[0] + DEPTH)
        L_CHAIN0 = M_CHAIN + B * B_CHAIN[0]
        W_CHAIN0 = B_CHAIN0[1] + B * B_CHAIN[1]

        block = ctx.enter_context(nc.Block())

        @block.sync
        def _(e):
            for counter in FROM_ONE:
                e.sem_inc(counter, 1)
            e.dma_start(X[:, :], xT).then_inc(s_in, 16)
            for k in range(2):
                e.dma_start(CT[:, k, :], cT[k]).then_inc(s_in, 16)
                e.dma_start(WM[:, k, :], wmod[k]).then_inc(s_in, 16)
            e.dma_start(BO[:, 0:1], bo).then_inc(s_in, 16)
            e.dma_start(CO[:, :], cols).then_inc(s_in, 16)
            e.dma_start(TAB[:, :, :], tabs).then_inc(s_in, 16)
            e.dma_start(MSK[:, :], mask).then_inc(s_in, 16)
            e.dma_start(MAT[:, :, :], mats).then_inc(s_in, 16)
            e.dma_start(WB[:, :], w0).then_inc(s_wb, 16)
            e.dma_start(WA[:, :], wl[0]).then_inc(s_wa, 16)
            for i, (o, w) in enumerate(QCH):
                e.dma_start(WG[0:w, :, i, :], wgu[o:o + w, :, :]).then_inc(s_wq, 16)
            e.dma_start(WD[:, :], wd).then_inc(s_wq, 16)

            def ffn_weights(l):
                e.dma_start(W1[:, :], f1[bass.ds(l, 1)].rearrange("l p n -> (l p) n")).then_inc(s_wf, 16)
                e.dma_start(W2[:, 0:2, :], f2[bass.ds(l, 1), 0:256, :]
                            .rearrange("l (i p) n -> (l p) i n", p=P)).then_inc(s_wf, 16)
                e.dma_start(W2[0:FI - 256, 2, :], f2[bass.ds(l, 1), 256:FI, :]
                            .rearrange("l p n -> (l p) n")).then_inc(s_wf, 16)

            for k in range(LAYER0):
                barrier(e, k)
                if k == 2:
                    e.dma_start(WB[:, :], w1).then_inc(s_wb, 16)
            with e.Fori(0, DEPTH - 1) as l:
                ffn_weights(l)
                barrier(e, l * 3 + LAYER0)
                e.dma_start(WA[:, :], wl[bass.ds(l + 1, 1)].rearrange("l p n -> (l p) n")).then_inc(s_wa, 16)
                barrier(e, l * 3 + LAYER0 + 1)
                barrier(e, l * 3 + LAYER0 + 2)
            ffn_weights(DEPTH - 1)
            for k in range(3):
                barrier(e, AFTER - 3 + k)
            for k in range(4):
                barrier(e, AFTER + k)
            e.wait_ge(q_dve, 1 + 7 + 3 * B)
            e.dma_start(out, X[:, :]).then_inc(s_out, 16)
            e.wait_ge(s_out, 16)

        @block.tensor
        def _(e):
            e.wait_ge(s_m, 1)
            for k in range(2):
                for j in range(6):
                    i = e.matmul(PS[:, k, j * B:(j + 1) * B], WM[:, k, j * P:(j + 1) * P], CE[:, k, :],
                                 start=True, stop=True)
            i.then_inc(s_m, 1)
            barrier(e, 0)
            ln_pe(e, 0, X, False, 0)
            barrier(e, 1)
            block_pe(e, 0)
            barrier(e, 2)
            ln_pe(e, 1, X, False, 0)
            barrier(e, 3)
            with e.Fori(0, DEPTH) as l:
                local_pe(e, l)
                barrier(e, l * 3 + LAYER0)
                ln_pe(e, l + 2, R, True, l)
                barrier(e, l * 3 + LAYER0 + 1)
                ffn_pe(e, l)
                barrier(e, l * 3 + LAYER0 + 2)
            barrier(e, AFTER)
            ln_pe(e, DEPTH + 2, X, False, 0)
            barrier(e, AFTER + 1)
            block_pe(e, 1)
            barrier(e, AFTER + 2)
            ln_pe(e, DEPTH + 3, X, False, 0)
            barrier(e, AFTER + 3)
            fp4w_pe(e)
            fp4_pe(e)

        @block.scalar
        def _(e):
            e.preload_act_table_set("natural_log_exp_and_others")
            e.wait_ge(s_in, 16 * 10)
            e.activation(CE[:, :, :], CT[:, :, :], ACT.Exp, scale=-1.0).then_inc(s_c, 1)
            barrier(e, 0)
            ln_act(e, 0)
            barrier(e, 1)
            block_act(e, 0)
            barrier(e, 2)
            ln_act(e, 1)
            barrier(e, 3)
            with e.Fori(0, DEPTH) as l:
                e.preload_act_table_set("natural_log_exp_and_others")
                local_act(e, l)
                barrier(e, l * 3 + LAYER0)
                e.preload_act_table_set("natural_log_exp_and_others")
                ln_act(e, l + 2)
                barrier(e, l * 3 + LAYER0 + 1)
                ffn_act(e, l, l * NV)
                barrier(e, l * 3 + LAYER0 + 2)
            e.preload_act_table_set("natural_log_exp_and_others")
            barrier(e, AFTER)
            ln_act(e, DEPTH + 2)
            barrier(e, AFTER + 1)
            block_act(e, 1)
            barrier(e, AFTER + 2)
            ln_act(e, DEPTH + 3)
            barrier(e, AFTER + 3)
            fp4w_act(e)
            fp4_act(e)

        @block.gpsimd
        def _(e):
            chain = Chain(e, s_pz, 0)
            for r in (slice(0, DH), slice(DH, P)):
                chain(e.memset(qz[r, :, 1 - r.start // DH, :], 0.0))
            chain(e.memset(kT[:, :, 0:WIN], 0.0))
            barrier(e, 0)
            barrier(e, 1)
            block_pool(e, 0)
            barrier(e, 2)
            chain(e.memset(pt[:, :, :, :, :].rearrange("p a b c n -> p (a b c n)"), 0.0))
            chain(e.memset(xs[DH:P, 0:1], 0.0))
            barrier(e, 3)
            with e.Fori(0, DEPTH) as l:
                local_pool(e, l)
                barrier(e, l * 3 + LAYER0)
                barrier(e, l * 3 + LAYER0 + 1)
                barrier(e, l * 3 + LAYER0 + 2)
            barrier(e, AFTER)
            barrier(e, AFTER + 1)
            block_pool(e, 1)
            barrier(e, AFTER + 2)
            barrier(e, AFTER + 3)

        @block.vector
        def _(e):
            def mod(k, scale, offset):
                return lambda b: (MOD[:, k, scale, b:b + 1], MOD[:, k, offset, b:b + 1])

            e.memset(BO[:, 1:2], 0.0)
            for i, v in enumerate((NFLOOR, NBIAS, LN_EPS)):
                e.memset(KC[:, i:i + 1], v)
            e.wait_ge(s_in, 16 * 10)
            e.tensor_copy(MSKB[:, :], MSK[:, :])
            e.tensor_copy(IDB[:, :], IDN)
            chain = Chain(e, s_v, 0)
            e.wait_ge(s_c, 1)
            chain(e.tensor_scalar(CE[:, :, :], CE[:, :, :], 1.0, None, ALU.add))
            chain(e.reciprocal(CR[:, :, :], CE[:, :, :]))
            e.tensor_tensor(CE[:, :, :], CT[:, :, :], CR[:, :, :], ALU.mult).then_inc(s_m, 1)
            e.wait_ge(s_m, 2)
            chain(e.tensor_copy(MOD[:, :, :, :].rearrange("p k j b -> p k (j b)"), PS[:, 0:2, 0:6 * B]))
            for j in (1, 4):
                e.tensor_scalar(MOD[:, :, j, :], MOD[:, :, j, :], 1.0, None, ALU.add)
            for i, j in enumerate((2, 5)):
                g = MOD[:, :, j, :]
                sg, ab = MT[:, 0, i, :, :], MT[:, 1, i, :, :]
                e.tensor_scalar(sg, g, 0.0, 2.0, ALU.is_ge, ALU.mult)
                chain(e.scalar_tensor_tensor(out=ab, in0=g, scalar=-1.0, in1=g, op0=ALU.mult, op1=ALU.max))
                e.tensor_scalar(sg, sg, -1.0, None, ALU.add)
                chain(e.tensor_scalar(ab, ab, 0.25, None, ALU.max))
                i = e.tensor_tensor(g, sg, ab, ALU.mult)
            chain(i)
            assert chain.n == M_CHAIN
            barrier(e, 0)
            ln_dve(e, 0, X, H, False, mod(0, 1, 0))
            barrier(e, 1)
            block_dve(e, 0)
            barrier(e, 2)
            ln_dve(e, 1, X, R, False, mod(0, 4, 3))
            barrier(e, 3)
            with e.Fori(0, DEPTH) as l:
                lv = l * NV
                local_dve(e, l, lv, L_CHAIN0)
                barrier(e, l * 3 + LAYER0)
                ln_dve(e, l + 2, R, H, True,
                       lambda b: (CO[:, bass.ds(lv + C_G, 1)], CO[:, bass.ds(lv + C_B, 1)]))
                barrier(e, l * 3 + LAYER0 + 1)
                ffn_dve(e, l, lv)
                barrier(e, l * 3 + LAYER0 + 2)
            for b in range(B):
                x = X[:, b * S:(b + 1) * S]
                e.scalar_tensor_tensor(out=x, in0=R[:, b * S:(b + 1) * S], scalar=MOD[:, 0, 5, b:b + 1],
                                       in1=x, op0=ALU.mult, op1=ALU.add)
            barrier(e, AFTER)
            ln_dve(e, DEPTH + 2, X, H, False, mod(1, 1, 0))
            barrier(e, AFTER + 1)
            block_dve(e, 1)
            barrier(e, AFTER + 2)
            ln_dve(e, DEPTH + 3, X, H, False, mod(1, 4, 3))
            barrier(e, AFTER + 3)
            e.wait_ge(s_wq, 64)
            fp4w_dve(e)
            fp4_dve(e)


def _tables():
    half = np.arange(0, DH, 2, dtype=np.float32)
    inv = (np.float32(1.0) / np.float32(10000.0) ** (half / np.float32(DH))).astype(np.float32)
    tok = np.arange(S, dtype=np.float32)
    freq = np.concatenate([tok[:, None] * inv[None, :]] * 2, -1)
    base = ((half + np.float32(0.4 * DH)) / np.float32(1.4 * DH)).astype(np.float32)
    scale = (base[None, :] ** ((tok - S // 2) / (WIN // 2))[:, None]).astype(np.float32)
    scale = np.concatenate([scale, scale], -1)
    cos, sin = np.cos(freq), np.sin(freq)
    sign = np.where(np.arange(DH) < DH // 2, -1.0, 1.0).astype(np.float32)
    qk = np.float32(8.0)
    tabs = [cos * scale * qk, cos / scale, sin * scale * sign * qk, sin / scale * sign]
    return np.stack([np.tile(t.T, (2, 1)) for t in tabs], 1).astype(np.float32)


def _mask():
    i, j = np.arange(WIN)[:, None], np.arange(2 * WIN)[None, :]
    band = np.where((j < i) | (j > i + WIN), MASKED, 0.0)
    m = np.zeros((4, WIN, 2, 2, 2 * WIN), np.float32)
    m[:] = band[None, :, None, None, :]
    m[0, :, 0, :, :WIN] = MASKED
    return m.reshape(P, 256)


def _mats():
    ones = np.kron(np.eye(2), np.ones((DH, DH)))
    return np.stack([ones, np.full((P, P), 1.0 / P), np.eye(P)], 1).astype(np.float32)


def kernel(**inputs):
    import concourse.bacc as _bacc
    from concourse.bass_utils import run_bass_kernel_spmd as _run

    a = {k: np.asarray(v) for k, v in inputs.items()}

    def chunks(w):
        return w.reshape(-1, P, w.shape[-1]).transpose(1, 0, 2).reshape(P, -1)

    w0 = np.concatenate([a["L0_attn_W" + n].reshape(INNER, P).T for n in "qkv"]
                        + [chunks(a["L0_attn_Wo"].T)], 1)
    w1 = np.concatenate([a["L1_attn_W" + n] for n in "qkv"] + [chunks(a["L1_attn_Wo"])], 1)
    qk = a["L0_ffn_Wqkv"][:, :, :2 * INNER].reshape(DEPTH, P, 2, PAIRS, 2, 2, DH // 2)
    both = np.stack([qk, qk[:, :, :, :, :, ::-1]], 2).transpose(0, 1, 4, 2, 3, 5, 6, 7)
    wl = np.concatenate([both.reshape(DEPTH, P, 4 * INNER), a["L0_ffn_Wqkv"][:, :, 2 * INNER:],
                         np.stack([chunks(w) for w in a["L0_ffn_Wo"]])], 2)
    cols = np.zeros((P, DEPTH, NV), np.float32)
    cols[:, :, C_G], cols[:, :, C_B], cols[:, :, C_B2] = (a["L0_ffn_" + n].T for n in ("ln_g", "ln_b", "b2"))
    for i, (o, w) in enumerate(FCH):
        cols[:w, :, C_B1A + i] = a["L0_ffn_b1"][:, o:o + w].T
        cols[:w, :, C_B1G + i] = a["L0_ffn_b1"][:, FI + o:FI + o + w].T
    for c, n in ((C_QS, "q_scale"), (C_KS, "k_scale")):
        v = a["L0_ffn_" + n].T
        cols[:, :, c] = np.concatenate([v, v])
        v = np.concatenate([v[DH // 2:], v[:DH // 2]])
        cols[:, :, c + 1] = np.concatenate([v, v])
    arrays = dict(
        xT=a["L0_attn_x"].transpose(2, 0, 1).reshape(P, T),
        cT=np.stack([a["L0_c"].T, a["L1_c"].T]), wmod=np.stack([a["L0_wmod"], a["L1_wmod"]]),
        bo=a["L0_attn_bo"].reshape(P, 1), w0=w0, w1=w1, wl=wl, f1=a["L0_ffn_W1"], f2=a["L0_ffn_W2"],
        cols=cols.reshape(P, DEPTH * NV), tabs=_tables(), mask=_mask(), mats=_mats(),
        wgu=np.stack([a["L1_ffn_w_gate"], a["L1_ffn_w_up"]], 1), wd=a["L1_ffn_w_down"])
    nc = _bacc.Bacc("TRN2", target_bir_lowering=False, num_devices=1)
    arrays = {f"in_{k}": np.ascontiguousarray(v) for k, v in arrays.items()}
    args = [nc.dram_tensor(k, v.shape, mybir.dt.from_np(v.dtype), kind="ExternalInput").ap()
            for k, v in arrays.items()]
    o = nc.dram_tensor("out_x", (P, T), F32, kind="ExternalOutput").ap()
    build(nc, *args, o)
    r = _run(nc, [arrays], core_ids=[0])
    y = r.results[0]["out_x"]
    return np.ascontiguousarray(y.reshape(P, B, S).transpose(1, 2, 0))
```

```python
from contextlib import ExitStack

import numpy as np

import concourse.bass as bass
from concourse import mybir

ALU = mybir.AluOpType
ACT = mybir.ActivationFunctionType
AX = mybir.AxisListType
F32 = mybir.dt.float32
BF16 = mybir.dt.bfloat16

P = 128
B, S = 8, 256
T = B * S
DH = 64
PAIRS = 8
INNER = PAIRS * P
DEPTH = 6
WIN = 32
FI = 341
FCH = [(0, 128), (128, 128), (256, FI - 256)]
QI = 352
QCH = [(0, 128), (128, 128), (256, QI - 256)]
CH = 512
NCH = T // CH
SC0 = float(np.float32(1.0) / np.float32(0.04))
LN_EPS = 1e-5
NSCALE, NFLOOR, NBIAS = float(2.0 ** 24), float(2.0 ** -62), float(12 * np.log(2.0))
MASKED = -1.0e30
FIRST = 8

C_G, C_B, C_B2, C_B1A, C_B1G, C_QS, C_QSR, C_KS, C_KSR, NV = 0, 1, 2, 3, 6, 9, 10, 11, 12, 13


class Chain:

    def __init__(self, e, sem, base):
        self.e, self.sem, self.base, self.n = e, sem, base, 0

    def __call__(self, instruction):
        self.n += 1
        instruction.then_inc(self.sem, 1)
        self.e.wait_ge(self.sem, self.base + self.n)


def build(nc, xT, cT, wmod, bo, w0, w1, wl, f1, f2, cols, tabs, mask, mats, wgu, wd, out):
    ctx = ExitStack()
    with ctx:
        def sb(name, shape, dt=F32):
            return ctx.enter_context(nc.sbuf_tensor(name, shape, dt))

        def sem(name):
            return ctx.enter_context(nc.semaphore(name))

        X = sb("X", [P, T])
        R = sb("R", [P, T])
        H = sb("H", [P, T])
        WB = sb("WB", [P, 4 * INNER])
        WA = sb("WA", [P, 6 * INNER])
        W1 = sb("W1", [P, 2 * FI])
        W2 = sb("W2", [P, 3, P])
        CO = sb("CO", [P, DEPTH * NV])
        TAB = sb("TAB", [P, 4, S])
        LT = sb("LT", [P, 4, S])
        MSK = sb("MSK", [P, 256])
        MSKB = sb("MSKB", [P, 256], BF16)
        MAT = sb("MAT", [P, 3, P])
        IDB = sb("IDB", [P, P], BF16)
        CT = sb("CT", [P, 2, B])
        CE = sb("CE", [P, 2, B])
        CR = sb("CR", [P, 2, B])
        WM = sb("WM", [P, 2, 6 * P])
        MOD = sb("MOD", [P, 2, 6, B])
        MT = sb("MT", [P, 2, 2, 2, B])
        BO = sb("BO", [P, 2])
        KC = sb("KC", [P, 4])
        xs = sb("xs", [P, S])
        sq = sb("sq", [P, 2, 512])
        t1 = sb("t1", [P, 2, 512])
        t2 = sb("t2", [P, 2, 512])
        rl = sb("rl", [P, 2, 260])
        rn = sb("rn", [P, 2, 260])
        k1 = sb("k1", [P, 2, S])
        qz = sb("qz", [P, 2, 2, S])
        kT = sb("kT", [P, 2, WIN + S])
        vb = sb("vb", [P, PAIRS, 2, P])
        mx = sb("mx", [P, 2, 16])
        sm = sb("sm", [P, 2, 16])
        rq = sb("rq", [P, 4, 4])
        nb = sb("nb", [P, 2, 4])
        rs = sb("rs", [P, 2, 16])
        al = sb("al", [P, 2, 16])
        dl = sb("dl", [P, 2, 16])
        ls = sb("ls", [P, 2, 16])
        wt = sb("wt", [P, 2, 16])
        s1 = sb("s1", [P, 2, 1024])
        pe_ = sb("pe_", [P, 2, 1024])
        pn = sb("pn", [P, 2, 1024])
        pt = sb("pt", [P, 2, 2, 2, S])
        ot = sb("ot", [P, 2, S])
        yr = sb("yr", [P, S])
        xc = sb("xc", [P, T])
        xq = sb("xq", [P, T])
        hg = sb("hg", [P, 2, 3, CH])
        ga = sb("ga", [P, 3, CH])
        WG = sb("WG", [P, 2, 3, P])
        WD = sb("WD", [P, QI])
        WGT = sb("WGT", [P, 2, QI])
        WDT = sb("WDT", [P, 3, P])
        NQ = 2 * QI
        fa, fsn, fx, fc, ft, fh, fg = (WA[:, i * NQ:(i + 1) * NQ] for i in range(7))
        fs = sb("fs", [P, NQ // 16])
        fr = sb("fr", [P, NQ // 16])
        hT = sb("hT", [P, S])
        h3 = sb("h3", [P, 3, S])

        PS = ctx.enter_context(nc.psum_tensor("PS", [P, 8, 512], F32))

        s_in = sem("s_in")
        s_wb = sem("s_wb")
        s_wa = sem("s_wa")
        s_wf = sem("s_wf")
        s_wq = sem("s_wq")
        s_out = sem("s_out")
        s_pass = sem("s_pass")
        s_bar = sem("s_bar")
        s_v = sem("s_v")
        s_cs = sem("s_cs")
        s_cw = sem("s_cw")
        s_cr = sem("s_cr")
        s_c = sem("s_c")
        s_m = sem("s_m")
        s_xs = sem("s_xs")
        s_qk = sem("s_qk")
        s_rot = sem("s_rot")
        s_vp = sem("s_vp")
        s_sq = sem("s_sq")
        s_ssq = sem("s_ssq")
        s_t1 = sem("s_t1")
        s_t2 = sem("s_t2")
        s_ln = sem("s_ln")
        s_rn = sem("s_rn")
        s_add = sem("s_add")
        s_pl = sem("s_pl")
        s_pz = sem("s_pz")
        s_kn = sem("s_kn")
        s_vev = sem("s_vev")
        s_sc = sem("s_sc")
        s_mx = sem("s_mx")
        s_nb = sem("s_nb")
        s_exp = sem("s_exp")
        s_rs = sem("s_rs")
        s_pn = sem("s_pn")
        s_pt = sem("s_pt")
        s_av = sem("s_av")
        s_oev = sem("s_oev")
        s_wo = sem("s_wo")
        s_y = sem("s_y")
        s_res = sem("s_res")
        g_xs = sem("g_xs")
        g_qk = sem("g_qk")
        g_vp = sem("g_vp")
        g_qev = sem("g_qev")
        g_vev = sem("g_vev")
        g_sc = sem("g_sc")
        g_d = sem("g_d")
        g_mx = sem("g_mx")
        g_exp = sem("g_exp")
        g_w = sem("g_w")
        g_pn = sem("g_pn")
        g_tp = sem("g_tp")
        g_pta = sem("g_pta")
        g_ptv = sem("g_ptv")
        g_av = sem("g_av")
        g_oev = sem("g_oev")
        g_wo = sem("g_wo")
        g_y = sem("g_y")
        g_res = sem("g_res")
        n_x = sem("n_x")
        n_mu = sem("n_mu")
        n_xc = sem("n_xc")
        n_sq = sem("n_sq")
        n_var = sem("n_var")
        n_ln = sem("n_ln")
        n_rs = sem("n_rs")
        n_xn = sem("n_xn")
        f_hg = sem("f_hg")
        f_ge = sem("f_ge")
        f_gu = sem("f_gu")
        f_y = sem("f_y")
        f_res = sem("f_res")
        q_pe = sem("q_pe")
        q_act = sem("q_act")
        q_dve = sem("q_dve")

        COUNTERS = [f_ge, f_gu, f_hg, f_res, f_y, g_av, g_d, g_exp, g_mx,
                    g_oev, g_pn, g_pta, g_ptv, g_qev, g_qk, g_res, g_sc, g_tp,
                    g_vev, g_vp, g_w, g_wo, g_xs, n_ln, n_mu, n_rs, n_sq,
                    n_var, n_x, n_xc, n_xn, q_act, q_dve, q_pe, s_add, s_av,
                    s_exp, s_kn, s_ln, s_mx, s_nb, s_oev, s_pl, s_pn, s_pt,
                    s_qk, s_res, s_rn, s_rot, s_rs, s_sc, s_sq, s_ssq, s_t1,
                    s_t2, s_vev, s_vp, s_wo, s_xs]

        ONES, MEAN, IDN = MAT[:, 0, :], MAT[:, 1, :], MAT[:, 2, :]

        def wait_apart(e, sem, value):
            e.wait_ge(sem, value)
            e.sem_inc(s_pass, 1)

        def barrier(e, k):
            e.drain().then_inc(s_bar, 1)
            wait_apart(e, s_bar, (k + 1) * 5)

        LAYER0 = 4
        AFTER = LAYER0 + 3 * DEPTH

        def ln_dve(e, call, src, dst, shift, affine):
            c0 = call * NCH
            if shift:
                for c in range(NCH):
                    for hb in range(2):
                        a = c * CH + hb * S
                        e.tensor_copy(xq[0:DH, a:a + S], src[0:DH, a:a + S])
                        e.memset(xq[DH:P, a:a + 1], 0.0)
                        i = e.tensor_copy(xq[DH:P, a + 1:a + S], src[DH:P, a:a + S - 1])
                    i.then_inc(n_x, 1)
            for c in range(NCH):
                a = c * CH
                e.wait_ge(n_mu, FIRST + c0 + (c + 1))
                e.tensor_tensor(xc[:, a:a + CH], (xq if shift else src)[:, a:a + CH], PS[:, c, :],
                                ALU.subtract).then_inc(n_xc, 1)
            for c in range(NCH):
                a = c * CH
                e.wait_ge(n_rs, FIRST + c0 + (c + 1))
                e.tensor_tensor(xc[:, a:a + CH], xc[:, a:a + CH], xq[:, a:a + CH],
                                ALU.mult).then_inc(n_xn, 1)
                e.wait_ge(n_xn, FIRST + c0 + (c + 1))
                for hb in range(2):
                    g, o = affine(2 * c + hb)
                    e.tensor_scalar(dst[:, a + hb * S:a + hb * S + S], xc[:, a + hb * S:a + hb * S + S],
                                    g, o, ALU.mult, ALU.add)

        def ln_pe(e, call, src, shift, shifts):
            c0 = call * NCH
            for c in range(NCH):
                a = c * CH
                if shift:
                    e.wait_ge(n_x, FIRST + shifts * NCH + (c + 1))
                e.matmul(PS[:, c, :], MEAN, (xq if shift else src)[:, a:a + CH],
                         start=True, stop=True).then_inc(n_mu, 1)
            for c in range(NCH):
                e.wait_ge(n_sq, FIRST + c0 + (c + 1))
                e.matmul(PS[:, 4 + c, :], MEAN, xq[:, c * CH:(c + 1) * CH],
                         start=True, stop=True).then_inc(n_var, 1)

        def ln_act(e, call):
            c0 = call * NCH
            for c in range(NCH):
                a = c * CH
                e.wait_ge(n_xc, FIRST + c0 + (c + 1))
                e.activation(xq[:, a:a + CH], xc[:, a:a + CH], ACT.Square).then_inc(n_sq, 1)
            for c in range(NCH):
                a = c * CH
                e.wait_ge(n_var, FIRST + c0 + (c + 1))
                e.activation(xq[:, a:a + CH], PS[:, 4 + c, :], ACT.Ln, bias=KC[:, 2:3]).then_inc(n_ln, 1)
                e.wait_ge(n_ln, FIRST + c0 + (c + 1))
                e.activation(xq[:, a:a + CH], xq[:, a:a + CH], ACT.Exp, scale=-0.5).then_inc(n_rs, 1)

        NS = PAIRS

        def steps(e, base, stages):
            last = max(lag for _, lag in stages)
            for s in range(NS):
                for stage, lag in stages:
                    if s >= lag:
                        stage(s - lag, base + (s - lag), 0)
            with e.Fori(1, B) as b:
                for s in range(NS):
                    for stage, lag in stages:
                        stage((s - lag) % NS, base + b * NS + (s - lag), b - 1 if s < lag else b)
            for s in range(NS, NS + last):
                for stage, lag in stages:
                    if s - lag < NS:
                        stage(s - lag, base + ((B - 1) * NS + s - lag), B - 1)

        HPV = 5 * INNER

        def local_pe(e, l):
            wait_apart(e, s_wa, (l + 1) * 16)

            def project(t, n, b):
                p = t % 2
                if t == 0:
                    e.wait_ge(s_xs, FIRST + (l * B + b + 1) * 2)
                e.wait_ge(s_t1, FIRST + n - 1)
                w = t * 512
                e.matmul(PS[:, p, 0:S], WA[:, w:w + P], xs[:, :], start=True, stop=True)
                e.matmul(PS[:, p, S:2 * S], WA[:, w + P:w + 2 * P], xs[:, :],
                         start=True, stop=True).then_inc(s_qk, 1)

            def project_more(t, n, b):
                w = t * 512
                e.wait_ge(s_t2, FIRST + n)
                e.matmul(PS[:, 2, 0:S], WA[:, w + 2 * P:w + 3 * P], xs[:, :], start=True, stop=True)
                e.matmul(PS[:, 2, S:2 * S], WA[:, w + 3 * P:w + 4 * P], xs[:, :],
                         start=True, stop=True).then_inc(s_rot, 1)
                e.wait_ge(s_vev, FIRST + n)
                for j in range(2):
                    i = e.matmul(PS[:, 5, j * P:(j + 1) * P], xs[:, j * P:(j + 1) * P],
                                 WA[:, 4 * INNER + t * P:4 * INNER + (t + 1) * P],
                                 start=True, stop=True)
                i.then_inc(s_vp, 1)

            def norms(t, n, b):
                p = t % 2
                e.wait_ge(s_sq, FIRST + n + 1)
                e.wait_ge(s_ln, FIRST + n)
                e.matmul(PS[:, 3, 0:S], ONES, sq[:, p, S:2 * S], start=True, stop=True)
                for j in range(2):
                    i = e.matmul(PS[:, 3, S + 2 * j:S + 2 * j + 2], sq[:, p, j * P:(j + 1) * P],
                                 MAT[:, 0, 0:P:DH], start=True, stop=True)
                i.then_inc(s_ssq, 1)

            def scores(t, n, b):
                p = t % 2
                e.wait_ge(s_exp, FIRST + n)
                e.wait_ge(s_add, FIRST + n + 1)
                e.wait_ge(s_kn, FIRST + n + 1)
                e.matmul(PS[:, 4, 0:256], IDB[:, :], MSKB[:, :], start=True, stop=False,
                         skip_group_check=True)
                for j in range(2):
                    for h in range(2):
                        for u in range(4):
                            w = j * P + u * WIN
                            o = (2 * j + h) * 64
                            i = e.matmul(PS[u * WIN:(u + 1) * WIN, 4, o:o + 64],
                                         qz[:, p, h, w:w + WIN], kT[:, p, w:w + 64],
                                         start=False, stop=(j == h == 1), skip_group_check=True)
                i.then_inc(s_sc, 1)

            def values(t, n, b):
                p = t % 2
                e.wait_ge(s_pt, FIRST + n + 1)
                e.wait_ge(s_oev, FIRST + n)
                for h in range(2):
                    o = PS[h * DH:(h + 1) * DH, 6, :]
                    e.matmul(o[:, 0:S], vb[:, t, 0, h * DH:(h + 1) * DH], pt[:, p, 0, h, :],
                             start=True, stop=False, skip_group_check=True)
                    i = e.matmul(o[:, P:S], vb[:, t, 1, h * DH:(h + 1) * DH],
                                 pt[:, p, 1, h, 0:P], start=False, stop=True, skip_group_check=True)
                i.then_inc(s_av, 1)

            def project_out(t, n, b):
                p = t % 2
                e.wait_ge(s_oev, FIRST + n + 1)
                if t == 0:
                    e.wait_ge(s_res, FIRST + l * B + b)
                i = e.matmul(PS[:, 7, 0:S], WA[:, HPV + t * P:HPV + (t + 1) * P], ot[:, p, :],
                             start=(t == 0), stop=(t == NS - 1))
                i.then_inc(s_wo, 1)

            steps(e, l * (B * NS), [(values, 6), (project, 0), (project_more, 0), (scores, 2),
                                    (norms, 0), (project_out, 7)])

        def local_act(e, l):

            def squares(t, n, b):
                p = t % 2
                e.wait_ge(s_qk, FIRST + n + 1)
                e.wait_ge(s_ssq, FIRST + n - 1)
                e.activation(sq[:, p, :], PS[:, p, :], ACT.Square).then_inc(s_sq, 1)

            def evac_v(t, n, b):
                e.wait_ge(s_vp, FIRST + n + 1)
                e.wait_ge(s_av, FIRST + n - 7)
                e.activation(vb[:, t, :, :], PS[:, 5, 0:2 * P].rearrange("p (j d) -> p j d", j=2),
                             ACT.Copy).then_inc(s_vev, 1)

            def norms(t, n, b):
                p = t % 2
                e.wait_ge(s_ssq, FIRST + n + 1)
                e.wait_ge(s_rn, FIRST + n)
                e.activation(rl[:, p, :], PS[:, 3, 0:260], ACT.Ln, bias=KC[:, 0:1],
                             scale=NSCALE).then_inc(s_ln, 1)
                e.wait_ge(s_ln, FIRST + n + 1)
                e.wait_ge(s_kn, FIRST + n - 1)
                e.activation(rn[:, p, :], rl[:, p, :], ACT.Exp, bias=KC[:, 1:2],
                             scale=-0.5).then_inc(s_rn, 1)

            def exps(t, n, b):
                p = t % 2
                e.wait_ge(s_nb, FIRST + n + 1)
                e.wait_ge(s_pn, FIRST + n - 1)
                e.wait_ge(s_rs, FIRST + n - 1)
                for g in range(4):
                    i = e.activation(pe_[:, p, g * 64:(g + 1) * 64], PS[:, 4, g * 64:(g + 1) * 64],
                                     ACT.Exp, bias=nb[:, p, g:g + 1], scale=rq[:, t % 4, g:g + 1],
                                     accum_out=sm[:, p, g:g + 1])
                i.then_inc(s_exp, 1)

            def evac(t, n, b):
                p = t % 2
                e.wait_ge(s_av, FIRST + n + 1)
                e.wait_ge(s_wo, FIRST + n - 1)
                e.activation(ot[:, p, :], PS[:, 6, 0:S], ACT.Copy).then_inc(s_oev, 1)

            steps(e, l * (B * NS), [(evac, 7), (norms, 1), (exps, 3), (squares, 0), (evac_v, 0)])

        def local_dve(e, l, lv, lt_base):
            for i, col in enumerate((C_QS, C_KS, C_QSR, C_KSR)):
                k = e.tensor_scalar(LT[:, i, :], TAB[:, i, :], CO[:, bass.ds(lv + col, 1)], None, ALU.mult)
            k.then_inc(s_v, 1)
            wait_apart(e, s_v, lt_base + l + 1)

            def tokens(t, n, b):
                if t == 0:
                    e.wait_ge(s_vp, FIRST + n)
                    e.tensor_copy(xs[0:DH, :], R[0:DH, bass.ds(b * S, S)]).then_inc(s_xs, 1)
                    e.tensor_copy(xs[DH:P, 1:S], R[DH:P, bass.ds(b * S, S - 1)]).then_inc(s_xs, 1)

            def rotary(t, n, b):
                p = t % 2
                e.wait_ge(s_sq, FIRST + n + 1)
                e.wait_ge(s_add, FIRST + n - 1)
                e.tensor_tensor(t1[:, p, :], PS[:, p, :], LT[:, 0:2, :].rearrange("p a n -> p (a n)"),
                                ALU.mult).then_inc(s_t1, 1)

            def rotary_more(t, n, b):
                p = t % 2
                e.wait_ge(s_rot, FIRST + n + 1)
                e.tensor_tensor(t2[:, p, :], PS[:, 2, :], LT[:, 2:4, :].rearrange("p a n -> p (a n)"),
                                ALU.mult).then_inc(s_t2, 1)

            def keys(t, n, b):
                p = t % 2
                e.wait_ge(s_rn, FIRST + n + 1)
                e.wait_ge(s_exp, FIRST + n - 3)
                e.tensor_scalar(rq[:, t % 4, :], rn[:, p, S:S + 4], 1e12, None, ALU.min)
                e.wait_ge(s_add, FIRST + n + 1)
                e.wait_ge(s_sc, FIRST + n - 1)
                e.scalar_tensor_tensor(out=kT[:, p, WIN:], in0=rn[:, p, 0:S], scalar=1e12,
                                       in1=k1[:, p, :], op0=ALU.min, op1=ALU.mult).then_inc(s_kn, 1)

            def maxima(t, n, b):
                p = t % 2
                e.wait_ge(s_sc, FIRST + n + 1)
                e.tensor_reduce(mx[:, p, 0:4], PS[:, 4, 0:256].rearrange("p (g k) -> p g k", g=4),
                                AX.X, ALU.max).then_inc(s_mx, 1)
                e.wait_ge(s_mx, FIRST + n + 1)
                e.wait_ge(s_exp, FIRST + n - 1)
                e.scalar_tensor_tensor(out=nb[:, p, :], in0=mx[:, p, 0:4], scalar=-1.0,
                                       in1=rq[:, t % 4, :], op0=ALU.mult, op1=ALU.mult).then_inc(s_nb, 1)

            def sums(t, n, b):
                p = t % 2
                e.wait_ge(s_exp, FIRST + n + 1)
                e.wait_ge(s_pn, FIRST + n - 1)
                e.reciprocal(rs[:, p, 0:4], sm[:, p, 0:4]).then_inc(s_rs, 1)

            def turn(t, n, b):
                p = t % 2
                e.wait_ge(s_pn, FIRST + n + 1)
                e.wait_ge(s_av, FIRST + n - 1)
                v = pn[:, p, 0:256].rearrange("p (j h f k) -> p j h f k", j=2, h=2, f=2)
                for u in range(4):
                    a = u * WIN
                    e.transpose(pt[a:a + WIN, p, :, :, a:a + WIN], v[a:a + WIN, :, :, 1, :])
                    if u:
                        e.transpose(pt[a - WIN:a, p, :, :, a:a + WIN], v[a:a + WIN, :, :, 0, :])
                e.transpose(pt[P - WIN:P, p, 0, :, P:P + WIN],
                            v[0:WIN, 1, :, 0, :]).then_inc(s_pt, 1)

            def residual(t, n, b):
                if t == NS - 1:
                    e.wait_ge(s_wo, FIRST + n + 1)
                    e.tensor_tensor(R[:, bass.ds(b * S, S)], PS[:, 7, 0:S], R[:, bass.ds(b * S, S)],
                                    ALU.add).then_inc(s_res, 1)

            steps(e, l * (B * NS), [(tokens, 0), (sums, 4), (maxima, 3), (turn, 5), (rotary, 0),
                                    (rotary_more, 0), (keys, 1), (residual, 7)])

        def local_pool(e, l):
            def add(t, n, b):
                p = t % 2
                e.wait_ge(s_t1, FIRST + n + 1)
                e.wait_ge(s_t2, FIRST + n + 1)
                e.wait_ge(s_kn, FIRST + n - 1)
                e.wait_ge(s_sc, FIRST + n - 1)
                e.tensor_tensor(k1[:, p, :], t1[:, p, S:], t2[:, p, S:], ALU.add).then_inc(s_pl, 1)
                for h in range(2):
                    r = slice(h * DH, (h + 1) * DH)
                    i = e.tensor_tensor(qz[r, p, h, :], t1[r, p, 0:S], t2[r, p, 0:S], ALU.add)
                    if h == 0:
                        i.then_inc(s_pl, 1)
                        e.wait_ge(s_pl, FIRST + 2 * n + 2)
                i.then_inc(s_add, 1)
                e.wait_ge(s_add, FIRST + n + 1)

            def divide(t, n, b):
                p = t % 2
                e.wait_ge(s_rs, FIRST + n + 1)
                e.wait_ge(s_pt, FIRST + n - 1)
                e.tensor_tensor(pn[:, p, 0:256].rearrange("p (g k) -> p g k", g=4),
                                pe_[:, p, 0:256].rearrange("p (g k) -> p g k", g=4),
                                rs[:, p, 0:4].rearrange("p (g o) -> p g o", o=1)
                                .broadcast_to([P, 4, 64]), ALU.mult).then_inc(s_pn, 1)

            steps(e, l * (B * NS), [(add, 1), (divide, 4)])

        def block_pe(e, k):
            e.wait_ge(s_wb, (k + 1) * 16)

            def project(t, n, b):
                if t == 0:
                    e.wait_ge(g_xs, FIRST + k * B + b + 1)
                e.wait_ge(g_qev, FIRST + n)
                e.matmul(PS[:, 0, 0:S], WB[:, t * P:(t + 1) * P], xs[:, :], start=True, stop=True)
                e.matmul(PS[:, 0, S:2 * S], WB[:, INNER + t * P:INNER + (t + 1) * P], xs[:, :],
                         start=True, stop=True).then_inc(g_qk, 1)
                e.wait_ge(g_vev, FIRST + n)
                for j in range(2):
                    i = e.matmul(PS[:, 1, j * P:(j + 1) * P], xs[:, j * P:(j + 1) * P],
                                 WB[:, 2 * INNER + t * P:2 * INNER + (t + 1) * P],
                                 start=True, stop=True)
                i.then_inc(g_vp, 1)

            def scores(t, n, b):
                p = t % 2
                e.wait_ge(g_qev, FIRST + n + 1)
                e.wait_ge(g_d, FIRST + n)
                for j in range(2):
                    for h in range(2):
                        i = e.matmul(PS[:, 2 + j, h * S:(h + 1) * S], qz[:, p, h, j * P:(j + 1) * P],
                                     kT[:, p, WIN:], start=True, stop=True)
                i.then_inc(g_sc, 1)

            def turn(t, n, b):
                p = t % 2
                e.wait_ge(g_pn, FIRST + n + 1)
                e.wait_ge(g_pta, FIRST + n)
                e.wait_ge(g_ptv, FIRST + n)
                for h in range(2):
                    for kt in range(2):
                        for j in range(2):
                            o = kt * S + j * P
                            c = (2 * j + h) * S + kt * P
                            i = e.transpose(PS[:, 4 + h, o:o + P], pn[:, p, c:c + P], IDN)
                i.then_inc(g_tp, 1)

            def values(t, n, b):
                p = t % 2
                e.wait_ge(g_pta, FIRST + n + 1)
                e.wait_ge(g_ptv, FIRST + n + 1)
                e.wait_ge(g_oev, FIRST + n)
                for h in range(2):
                    for kt in range(2):
                        i = e.matmul(PS[h * DH:(h + 1) * DH, 6, 0:S],
                                     vb[:, t, kt, h * DH:(h + 1) * DH], pt[:, p, h, kt, :],
                                     start=(kt == 0), stop=(kt == 1), skip_group_check=True)
                i.then_inc(g_av, 1)

            def project_out(t, n, b):
                p = t % 2
                e.wait_ge(g_oev, FIRST + n + 1)
                if t == 0:
                    e.wait_ge(g_res, FIRST + k * B + b)
                i = e.matmul(PS[:, 7, 0:S], WB[:, 3 * INNER + t * P:3 * INNER + (t + 1) * P],
                             ot[:, p, :], start=(t == 0), stop=(t == NS - 1))
                i.then_inc(g_wo, 1)

            steps(e, k * (B * NS), [(values, 7), (project, 0), (scores, 1), (turn, 5), (project_out, 8)])

        def block_act(e, k):

            def evac_qkv(t, n, b):
                p = t % 2
                e.wait_ge(g_qk, FIRST + n + 1)
                e.wait_ge(g_sc, FIRST + n - 1)
                for h in range(2):
                    r = slice(h * DH, (h + 1) * DH)
                    e.activation(qz[r, p, h, :], PS[r, 0, 0:S], ACT.Copy)
                e.activation(kT[:, p, WIN:], PS[:, 0, S:2 * S], ACT.Copy).then_inc(g_qev, 1)
                e.wait_ge(g_vp, FIRST + n + 1)
                e.wait_ge(g_av, FIRST + n - 7)
                e.activation(vb[:, t, :, :], PS[:, 1, 0:2 * P].rearrange("p (j d) -> p j d", j=2),
                             ACT.Copy).then_inc(g_vev, 1)

            def exps(t, n, b):
                p = t % 2
                e.wait_ge(g_d if k else g_mx, FIRST + n + 1)
                e.wait_ge(g_pn, FIRST + n - 1)
                e.wait_ge(g_w, FIRST + n - 1)
                if k == 0:
                    for g in range(4):
                        i = e.activation(pe_[:, p, g * S:(g + 1) * S], s1[:, p, g * S:(g + 1) * S],
                                         ACT.Exp, bias=nb[:, p, g:g + 1], scale=SC0,
                                         accum_out=sm[:, p, g:g + 1])
                    i.then_inc(g_exp, 1)
                else:
                    e.activation(al[:, p, 4:16], dl[:, p, 4:16], ACT.Exp, scale=DH ** -0.5)
                    e.activation(pe_[:, p, :], s1[:, p, :], ACT.Exp,
                                 scale=DH ** -0.5).then_inc(g_exp, 1)

            def evac_pt(t, n, b):
                p = t % 2
                e.wait_ge(g_tp, FIRST + n + 1)
                e.wait_ge(g_av, FIRST + n - 1)
                e.activation(pt[:, p, 0, :, :].rearrange("p a n -> p (a n)"), PS[:, 4, :],
                             ACT.Copy).then_inc(g_pta, 1)
                if k:
                    e.activation(pt[:, p, 1, :, :].rearrange("p a n -> p (a n)"), PS[:, 5, :],
                                 ACT.Copy).then_inc(g_ptv, 1)

            def evac_o(t, n, b):
                p = t % 2
                e.wait_ge(g_av, FIRST + n + 1)
                e.wait_ge(g_wo, FIRST + n - 1)
                e.activation(ot[:, p, :], PS[:, 6, 0:S], ACT.Copy).then_inc(g_oev, 1)

            def tokens(t, n, b):
                if t == 0:
                    e.wait_ge(g_vp, FIRST + n)
                    e.activation(xs[:, :], H[:, bass.ds(b * S, S)], ACT.Copy).then_inc(g_xs, 1)

            steps(e, k * (B * NS), [(tokens, 0), (evac_o, 8), (evac_pt, 6), (exps, 3), (evac_qkv, 0)])

        def block_dve(e, k):
            SOFT, WGHT = (2, 4), (0, 13)
            before = k * B * NS

            def soft(t, n, b):
                p = t % 2
                chain = Chain(e, s_cs, before * SOFT[0] + (n - before) * SOFT[k])
                e.wait_ge(g_sc, FIRST + n + 1)
                e.wait_ge(g_exp, FIRST + n - 1)
                if k == 0:
                    sv = PS[:, 2:4, :]
                    s1v = s1[:, p, :].rearrange("p (a n) -> p a n", a=2)
                    chain(e.tensor_scalar(s1v, sv, 0.0, -1.0e9, ALU.is_equal, ALU.mult))
                    e.tensor_tensor(s1v, sv, s1v, ALU.add).then_inc(g_d, 1)
                    e.wait_ge(g_d, FIRST + n + 1)
                    chain(e.tensor_reduce(mx[:, p, 0:4], s1[:, p, :].rearrange("p (g q) -> p g q", g=4),
                                          AX.X, ALU.max))
                    e.tensor_scalar(nb[:, p, :], mx[:, p, 0:4], -SC0, None, ALU.mult).then_inc(g_mx, 1)
                else:
                    for j in range(2):
                        i = e.tensor_reduce(
                            mx[:, p, :].rearrange("p (k g) -> p g k", k=4)[:, 2 * j:2 * j + 2, :],
                            PS[:, 2 + j, :].rearrange("p (h k q) -> p h k q", h=2, k=4),
                            AX.X, ALU.max)
                    chain(i)
                    for i in range(1, 4):
                        chain(e.tensor_tensor(mx[:, p, 4 * i:4 * i + 4], mx[:, p, 4 * i - 4:4 * i],
                                              mx[:, p, 4 * i:4 * i + 4], ALU.max))
                    e.tensor_tensor(dl[:, p, 4:16], mx[:, p, 0:12], mx[:, p, 4:16], ALU.subtract)
                    for j in range(2):
                        m = mx[:, p, :].rearrange("p (k g o) -> p g k o", k=4, o=1)
                        i = e.tensor_tensor(
                            s1[:, p, j * 512:(j + 1) * 512].rearrange("p (h k q) -> p h k q", h=2, k=4),
                            PS[:, 2 + j, :].rearrange("p (h k q) -> p h k q", h=2, k=4),
                            m[:, 2 * j:2 * j + 2, :, :].broadcast_to([P, 2, 4, 64]), ALU.subtract)
                    i.then_inc(g_d, 1)
                assert chain.n == SOFT[k]

            def weights(t, n, b):
                p = t % 2
                e.wait_ge(g_exp, FIRST + n + 1)
                e.wait_ge(g_pn, FIRST + n - 1)
                if k == 0:
                    e.reciprocal(rs[:, p, 0:4], sm[:, p, 0:4]).then_inc(g_w, 1)
                    return
                chain = Chain(e, s_cw, (n - before) * WGHT[k])
                chain(e.tensor_reduce(ls[:, p, :].rearrange("p (k g) -> p g k", k=4),
                                      pe_[:, p, :].rearrange("p (g k q) -> p g k q", g=4, k=4),
                                      AX.X, ALU.add))
                for i in range(1, 4):
                    c, c1 = slice(4 * i, 4 * i + 4), slice(4 * i - 4, 4 * i)
                    chain(e.tensor_tensor(sm[:, p, c], al[:, p, c], ls[:, p, c1], ALU.mult))
                    chain(e.tensor_tensor(ls[:, p, c], ls[:, p, c], sm[:, p, c], ALU.add))
                chain(e.reciprocal(wt[:, p, :], ls[:, p, :]))
                for i in (2, 1, 0):
                    c, c1 = slice(4 * i, 4 * i + 4), slice(4 * i + 4, 4 * i + 8)
                    chain(e.tensor_tensor(rs[:, p, c], wt[:, p, c1], al[:, p, c1], ALU.mult))
                    j = e.tensor_tensor(wt[:, p, c], wt[:, p, c], rs[:, p, c], ALU.mult)
                    if i:
                        chain(j)
                    else:
                        j.then_inc(g_w, 1)
                assert chain.n == WGHT[k], chain.n

            def evac_pt(t, n, b):
                p = t % 2
                e.wait_ge(g_tp, FIRST + n + 1)
                e.wait_ge(g_av, FIRST + n - 1)
                e.tensor_copy(pt[:, p, 1, :, :].rearrange("p a n -> p (a n)"),
                              PS[:, 5, :]).then_inc(g_ptv, 1)

            def residual(t, n, b):
                if t == NS - 1:
                    e.wait_ge(g_wo, FIRST + n + 1)
                    Chain(e, s_cr, k * B + b)(
                        e.tensor_scalar(yr[:, :], PS[:, 7, 0:S], BO[:, k:k + 1],
                                        MOD[:, k, 2, bass.ds(b, 1)], ALU.add, ALU.mult))
                    e.tensor_tensor(X[:, bass.ds(b * S, S)], X[:, bass.ds(b * S, S)], yr[:, :],
                                    ALU.add).then_inc(g_res, 1)

            steps(e, k * (B * NS), [(weights, 4), (soft, 2)] + [(evac_pt, 6)] * (k == 0) + [(residual, 8)])

        def block_pool(e, k):
            def divide(t, n, b):
                p = t % 2
                e.wait_ge(g_w, FIRST + n + 1)
                e.wait_ge(g_tp, FIRST + n - 1)
                if k == 0:
                    v = [a[:, p, :].rearrange("p (g q) -> p g q", g=4) for a in (pn, pe_)]
                    f = rs[:, p, 0:4].rearrange("p (g o) -> p g o", o=1).broadcast_to([P, 4, S])
                else:
                    v = [a[:, p, :].rearrange("p (g k q) -> p g k q", g=4, k=4) for a in (pn, pe_)]
                    f = wt[:, p, :].rearrange("p (k g o) -> p g k o", k=4, o=1).broadcast_to([P, 4, 4, 64])
                e.tensor_tensor(v[0], v[1], f, ALU.mult).then_inc(g_pn, 1)

            steps(e, k * (B * NS), [(divide, 4)])

        def ffn_pe(e, l):
            e.wait_ge(s_wf, (l + 1) * 48)
            def hidden(c):
                for i, (o, w) in enumerate(FCH):
                    if c:
                        e.wait_ge(f_gu, FIRST + l * 12 + (c - 1) * 3 + i + 1)
                    x = H[:, c * CH:(c + 1) * CH]
                    e.matmul(PS[0:w, 2 * i, :], W1[:, o:o + w], x, start=True, stop=True)
                    e.matmul(PS[0:w, 2 * i + 1, :], W1[:, FI + o:FI + o + w], x,
                             start=True, stop=True).then_inc(f_hg, 1)

            def down(c):
                e.wait_ge(f_gu, FIRST + l * 12 + 3 * (c + 1))
                if c >= 2:
                    e.wait_ge(f_res, FIRST + l * 4 + c - 1)
                for i, (o, w) in enumerate(FCH):
                    j = e.matmul(PS[:, 6 + c % 2, :], W2[0:w, i, :], hg[0:w, c % 2, i, :],
                                 start=(i == 0), stop=(i == 2))
                j.then_inc(f_y, 1)

            hidden(0)
            for c in range(1, NCH):
                hidden(c)
                down(c - 1)
            down(NCH - 1)

        def ffn_act(e, l, lv):
            for c in range(NCH):
                for i, (o, w) in enumerate(FCH):
                    if c:
                        e.wait_ge(f_gu, FIRST + l * 12 + (c - 1) * 3 + i + 1)
                    wait_apart(e, f_hg, FIRST + l * 12 + 3 * c + i + 1)
                    e.activation(ga[0:w, i, :], PS[0:w, 2 * i + 1, :], ACT.Gelu,
                                 bias=CO[0:w, bass.ds(lv + C_B1G + i, 1)]).then_inc(f_ge, 1)

        def ffn_dve(e, l, lv):
            def residual(c):
                e.wait_ge(f_y, FIRST + l * 4 + c + 1)
                r = R[:, c * CH:(c + 1) * CH]
                e.scalar_tensor_tensor(out=r, in0=PS[:, 6 + c % 2, :], scalar=CO[:, bass.ds(lv + C_B2, 1)],
                                       in1=r, op0=ALU.add, op1=ALU.add).then_inc(f_res, 1)
            for c in range(NCH):
                for i, (o, w) in enumerate(FCH):
                    e.wait_ge(f_ge, FIRST + l * 12 + 3 * c + i + 1)
                    if c >= 2 and i == 0:
                        e.wait_ge(f_y, FIRST + l * 4 + c - 1)
                    e.scalar_tensor_tensor(out=hg[0:w, c % 2, i, :], in0=PS[0:w, 2 * i, :],
                                           scalar=CO[0:w, bass.ds(lv + C_B1A + i, 1)], in1=ga[0:w, i, :],
                                           op0=ALU.add, op1=ALU.mult).then_inc(f_gu, 1)
                if c:
                    residual(c - 1)
            residual(NCH - 1)

        def quantize(e, chain, r, x, out, n):
            a, c, t = fa[0:r, 0:n], fc[0:r, 0:n], ft[0:r, 0:n]
            sc, rc = fs[0:r, 0:n // 16], fr[0:r, 0:n // 16]

            def blocks(v):
                return v.rearrange("p (b q) -> p b q", q=16)

            def spread(v):
                return v.rearrange("p (b o) -> p b o", o=1).broadcast_to([r, n // 16, 16])

            chain(e.scalar_tensor_tensor(out=a, in0=x, scalar=-1.0, in1=x, op0=ALU.mult, op1=ALU.max))
            e.tensor_scalar(fsn[0:r, 0:n], x, 0.0, 2.0, ALU.is_ge, ALU.mult)
            chain(e.tensor_reduce(sc, blocks(a), AX.X, ALU.max))
            chain(e.tensor_scalar(sc, sc, 1.0 / 6.0, 1e-12, ALU.mult, ALU.max))
            chain(e.reciprocal(rc, sc))
            chain(e.tensor_tensor(blocks(a), blocks(a), spread(rc), ALU.mult))
            e.tensor_scalar(c, a, 0.25, None, ALU.is_gt)
            chain(e.tensor_scalar(t, a, 5.0, 2.0, ALU.is_gt, ALU.mult))
            for m, v in ((0.75, c), (2.5, t), (1.25, c), (3.5, t), (1.75, c)):
                chain(e.scalar_tensor_tensor(out=v, in0=a, scalar=m, in1=v, op0=ALU.is_gt, op1=ALU.add))
            chain(e.scalar_tensor_tensor(out=c, in0=c, scalar=0.5, in1=t, op0=ALU.mult, op1=ALU.add))
            chain(e.scalar_tensor_tensor(out=c, in0=fsn[0:r, 0:n], scalar=-1.0, in1=c,
                                         op0=ALU.add, op1=ALU.mult))
            return e.tensor_tensor(blocks(out), blocks(c), spread(sc), ALU.mult)

        QC = 13
        W_TILES = [(k, i, w) for k in range(2) for i, (o, w) in enumerate(QCH)]

        def fp4w_dve(e):
            chain = Chain(e, s_v, W_CHAIN0)
            for k, i, w in W_TILES:
                quantize(e, chain, w, WG[0:w, k, i, :], WG[0:w, k, i, :], P).then_inc(q_dve, 1)
                e.wait_ge(q_dve, FIRST + 3 * k + i + 1)
            quantize(e, chain, P, WD[:, :], WD[:, :], QI).then_inc(q_dve, 1)
            e.wait_ge(q_dve, FIRST + 7)
            assert chain.n == 7 * QC

        def fp4w_pe(e):
            for k, i, w in W_TILES:
                e.wait_ge(q_dve, FIRST + 3 * k + i + 1)
                o = QCH[i][0]
                e.transpose(PS[:, k, o:o + w], WG[0:w, k, i, :], MAT[0:w, 2, 0:w]).then_inc(q_pe, 1)
            e.wait_ge(q_dve, FIRST + 7)
            for i, (o, w) in enumerate(QCH):
                e.transpose(PS[0:w, 2, i * P:(i + 1) * P], WD[:, o:o + w], IDN).then_inc(q_pe, 1)

        def fp4w_act(e):
            e.wait_ge(q_pe, FIRST + 9)
            e.activation(WGT[:, :, :], PS[:, 0:2, 0:QI], ACT.Copy)
            for i, (o, w) in enumerate(QCH):
                j = e.activation(WDT[0:w, i, :], PS[0:w, 2, i * P:(i + 1) * P], ACT.Copy)
            j.then_inc(q_act, 1)

        def fp4_pe(e):
            e.wait_ge(q_act, FIRST + 1)
            with e.Fori(0, B) as b:
                p0, a0, d0 = 9 + b * 5, 1 + b * 5, 7 + b * 3
                e.wait_ge(q_act, FIRST + a0 + 1)
                e.wait_ge(q_dve, FIRST + d0)
                for j in range(2):
                    i = e.transpose(PS[:, 0, j * P:(j + 1) * P], hT[:, j * P:(j + 1) * P], IDN)
                i.then_inc(q_pe, 1)
                e.wait_ge(q_dve, FIRST + d0 + 1)
                for j in range(2):
                    i = e.transpose(PS[:, 1, j * P:(j + 1) * P], fh[:, j * P:(j + 1) * P], IDN)
                i.then_inc(q_pe, 1)
                e.wait_ge(q_act, FIRST + a0 + 3)
                for j in range(2):
                    for k in range(2):
                        i = e.matmul(PS[:, 2 + 2 * k + j, 0:QI], hT[:, j * P:(j + 1) * P], WGT[:, k, :],
                                     start=True, stop=True)
                i.then_inc(q_pe, 1)
                e.wait_ge(q_dve, FIRST + d0 + 2)
                for i, (o, w) in enumerate(QCH):
                    for j in range(2):
                        x = e.transpose(PS[0:w, (0, 1, 6)[i], j * P:(j + 1) * P],
                                        fh[:, j * QI + o:j * QI + o + w], IDN)
                x.then_inc(q_pe, 1)
                e.wait_ge(q_act, FIRST + a0 + 5)
                for i, (o, w) in enumerate(QCH):
                    x = e.matmul(PS[:, 7, 0:S], WDT[0:w, i, :], h3[0:w, i, :],
                                 start=(i == 0), stop=(i == 2))
                x.then_inc(q_pe, 1)

        def fp4_act(e):
            with e.Fori(0, B) as b:
                p0, a0 = 9 + b * 5, 1 + b * 5
                e.wait_ge(q_pe, FIRST + p0)
                e.activation(hT[:, :], H[:, bass.ds(b * S, S)], ACT.Copy).then_inc(q_act, 1)
                e.wait_ge(q_pe, FIRST + p0 + 1)
                e.activation(fx[:, 0:S], PS[:, 0, 0:S], ACT.Copy).then_inc(q_act, 1)
                e.wait_ge(q_pe, FIRST + p0 + 2)
                e.activation(hT[:, :], PS[:, 1, 0:S], ACT.Copy).then_inc(q_act, 1)
                e.wait_ge(q_pe, FIRST + p0 + 3)
                e.activation(fg[:, :].rearrange("p (j n) -> p j n", j=2), PS[:, 2:4, 0:QI],
                             ACT.Silu).then_inc(q_act, 1)
                e.wait_ge(q_pe, FIRST + p0 + 4)
                for i, (o, w) in enumerate(QCH):
                    x = e.activation(h3[0:w, i, :], PS[0:w, (0, 1, 6)[i], 0:S], ACT.Copy)
                x.then_inc(q_act, 1)

        def fp4_dve(e):
            with e.Fori(0, B) as b:
                p0, a0, d0 = 9 + b * 5, 1 + b * 5, 7 + b * 3
                chain = Chain(e, s_v, W_CHAIN0 + 7 * QC + b * (2 * QC + 1))
                e.wait_ge(q_act, FIRST + a0 + 2)
                quantize(e, chain, P, fx[:, 0:S], fh[:, 0:S], S).then_inc(q_dve, 1)
                e.wait_ge(q_act, FIRST + a0 + 4)
                chain(e.tensor_tensor(fx[:, :].rearrange("p (j n) -> p j n", j=2), PS[:, 4:6, 0:QI],
                                      fg[:, :].rearrange("p (j n) -> p j n", j=2), ALU.mult))
                quantize(e, chain, P, fx[:, :], fh[:, :], NQ).then_inc(q_dve, 1)
                e.wait_ge(q_pe, FIRST + p0 + 5)
                x = X[:, bass.ds(b * S, S)]
                e.scalar_tensor_tensor(out=x, in0=PS[:, 7, 0:S], scalar=MOD[:, 1, 5, bass.ds(b, 1)],
                                       in1=x, op0=ALU.mult, op1=ALU.add).then_inc(q_dve, 1)
                assert chain.n == 2 * QC + 1

        M_CHAIN = 8
        L_CHAIN0 = M_CHAIN
        W_CHAIN0 = M_CHAIN + DEPTH

        block = ctx.enter_context(nc.Block())

        @block.sync
        def _(e):
            for counter in COUNTERS:
                e.sem_inc(counter, FIRST)
            e.dma_start(X[:, :], xT).then_inc(s_in, 16)
            for k in range(2):
                e.dma_start(CT[:, k, :], cT[k]).then_inc(s_in, 16)
                e.dma_start(WM[:, k, :], wmod[k]).then_inc(s_in, 16)
            e.dma_start(BO[:, 0:1], bo).then_inc(s_in, 16)
            e.dma_start(CO[:, :], cols).then_inc(s_in, 16)
            e.dma_start(TAB[:, :, :], tabs).then_inc(s_in, 16)
            e.dma_start(MSK[:, :], mask).then_inc(s_in, 16)
            e.dma_start(MAT[:, :, :], mats).then_inc(s_in, 16)
            e.dma_start(WB[:, :], w0).then_inc(s_wb, 16)
            e.dma_start(WA[:, :], wl[0]).then_inc(s_wa, 16)
            for i, (o, w) in enumerate(QCH):
                e.dma_start(WG[0:w, :, i, :], wgu[o:o + w, :, :]).then_inc(s_wq, 16)
            e.dma_start(WD[:, :], wd).then_inc(s_wq, 16)

            def ffn_weights(l):
                e.dma_start(W1[:, :], f1[bass.ds(l, 1)].rearrange("l p n -> (l p) n")).then_inc(s_wf, 16)
                e.dma_start(W2[:, 0:2, :], f2[bass.ds(l, 1), 0:256, :]
                            .rearrange("l (i p) n -> (l p) i n", p=P)).then_inc(s_wf, 16)
                e.dma_start(W2[0:FI - 256, 2, :], f2[bass.ds(l, 1), 256:FI, :]
                            .rearrange("l p n -> (l p) n")).then_inc(s_wf, 16)

            for k in range(LAYER0):
                barrier(e, k)
                if k == 2:
                    e.dma_start(WB[:, :], w1).then_inc(s_wb, 16)
            with e.Fori(0, DEPTH - 1) as l:
                ffn_weights(l)
                barrier(e, l * 3 + LAYER0)
                e.dma_start(WA[:, :], wl[bass.ds(l + 1, 1)].rearrange("l p n -> (l p) n")).then_inc(s_wa, 16)
                barrier(e, l * 3 + LAYER0 + 1)
                barrier(e, l * 3 + LAYER0 + 2)
            ffn_weights(DEPTH - 1)
            for k in range(3):
                barrier(e, AFTER - 3 + k)
            for k in range(4):
                barrier(e, AFTER + k)
            e.wait_ge(q_dve, FIRST + 7 + 3 * B)
            e.dma_start(out, X[:, :]).then_inc(s_out, 16)
            e.wait_ge(s_out, 16)

        @block.tensor
        def _(e):
            e.wait_ge(s_m, 1)
            for k in range(2):
                for j in range(6):
                    i = e.matmul(PS[:, k, j * B:(j + 1) * B], WM[:, k, j * P:(j + 1) * P], CE[:, k, :],
                                 start=True, stop=True)
            i.then_inc(s_m, 1)
            barrier(e, 0)
            ln_pe(e, 0, X, False, 0)
            barrier(e, 1)
            block_pe(e, 0)
            barrier(e, 2)
            ln_pe(e, 1, X, False, 0)
            barrier(e, 3)
            with e.Fori(0, DEPTH) as l:
                local_pe(e, l)
                barrier(e, l * 3 + LAYER0)
                ln_pe(e, l + 2, R, True, l)
                barrier(e, l * 3 + LAYER0 + 1)
                ffn_pe(e, l)
                barrier(e, l * 3 + LAYER0 + 2)
            barrier(e, AFTER)
            ln_pe(e, DEPTH + 2, X, False, 0)
            barrier(e, AFTER + 1)
            block_pe(e, 1)
            barrier(e, AFTER + 2)
            ln_pe(e, DEPTH + 3, X, False, 0)
            barrier(e, AFTER + 3)
            fp4w_pe(e)
            fp4_pe(e)

        @block.scalar
        def _(e):
            e.preload_act_table_set("natural_log_exp_and_others")
            e.wait_ge(s_in, 16 * 10)
            e.activation(CE[:, :, :], CT[:, :, :], ACT.Exp, scale=-1.0).then_inc(s_c, 1)
            barrier(e, 0)
            ln_act(e, 0)
            barrier(e, 1)
            block_act(e, 0)
            barrier(e, 2)
            ln_act(e, 1)
            barrier(e, 3)
            with e.Fori(0, DEPTH) as l:
                e.preload_act_table_set("natural_log_exp_and_others")
                local_act(e, l)
                barrier(e, l * 3 + LAYER0)
                e.preload_act_table_set("natural_log_exp_and_others")
                ln_act(e, l + 2)
                barrier(e, l * 3 + LAYER0 + 1)
                ffn_act(e, l, l * NV)
                barrier(e, l * 3 + LAYER0 + 2)
            e.preload_act_table_set("natural_log_exp_and_others")
            barrier(e, AFTER)
            ln_act(e, DEPTH + 2)
            barrier(e, AFTER + 1)
            block_act(e, 1)
            barrier(e, AFTER + 2)
            ln_act(e, DEPTH + 3)
            barrier(e, AFTER + 3)
            fp4w_act(e)
            fp4_act(e)

        @block.gpsimd
        def _(e):
            chain = Chain(e, s_pz, 0)
            for r in (slice(0, DH), slice(DH, P)):
                chain(e.memset(qz[r, :, 1 - r.start // DH, :], 0.0))
            chain(e.memset(kT[:, :, 0:WIN], 0.0))
            barrier(e, 0)
            barrier(e, 1)
            block_pool(e, 0)
            barrier(e, 2)
            chain(e.memset(pt[:, :, :, :, :].rearrange("p a b c n -> p (a b c n)"), 0.0))
            chain(e.memset(xs[DH:P, 0:1], 0.0))
            barrier(e, 3)
            with e.Fori(0, DEPTH) as l:
                local_pool(e, l)
                barrier(e, l * 3 + LAYER0)
                barrier(e, l * 3 + LAYER0 + 1)
                barrier(e, l * 3 + LAYER0 + 2)
            barrier(e, AFTER)
            barrier(e, AFTER + 1)
            block_pool(e, 1)
            barrier(e, AFTER + 2)
            barrier(e, AFTER + 3)

        @block.vector
        def _(e):
            def mod(k, scale, offset):
                return lambda b: (MOD[:, k, scale, b:b + 1], MOD[:, k, offset, b:b + 1])

            e.memset(BO[:, 1:2], 0.0)
            for i, v in enumerate((NFLOOR, NBIAS, LN_EPS)):
                e.memset(KC[:, i:i + 1], v)
            e.wait_ge(s_in, 16 * 10)
            e.tensor_copy(MSKB[:, :], MSK[:, :])
            e.tensor_copy(IDB[:, :], IDN)
            chain = Chain(e, s_v, 0)
            e.wait_ge(s_c, 1)
            chain(e.tensor_scalar(CE[:, :, :], CE[:, :, :], 1.0, None, ALU.add))
            chain(e.reciprocal(CR[:, :, :], CE[:, :, :]))
            e.tensor_tensor(CE[:, :, :], CT[:, :, :], CR[:, :, :], ALU.mult).then_inc(s_m, 1)
            e.wait_ge(s_m, 2)
            chain(e.tensor_copy(MOD[:, :, :, :].rearrange("p k j b -> p k (j b)"), PS[:, 0:2, 0:6 * B]))
            for j in (1, 4):
                e.tensor_scalar(MOD[:, :, j, :], MOD[:, :, j, :], 1.0, None, ALU.add)
            for i, j in enumerate((2, 5)):
                g = MOD[:, :, j, :]
                sg, ab = MT[:, 0, i, :, :], MT[:, 1, i, :, :]
                e.tensor_scalar(sg, g, 0.0, 2.0, ALU.is_ge, ALU.mult)
                chain(e.scalar_tensor_tensor(out=ab, in0=g, scalar=-1.0, in1=g, op0=ALU.mult, op1=ALU.max))
                e.tensor_scalar(sg, sg, -1.0, None, ALU.add)
                chain(e.tensor_scalar(ab, ab, 0.25, None, ALU.max))
                i = e.tensor_tensor(g, sg, ab, ALU.mult)
            chain(i)
            assert chain.n == M_CHAIN
            barrier(e, 0)
            ln_dve(e, 0, X, H, False, mod(0, 1, 0))
            barrier(e, 1)
            block_dve(e, 0)
            barrier(e, 2)
            ln_dve(e, 1, X, R, False, mod(0, 4, 3))
            barrier(e, 3)
            with e.Fori(0, DEPTH) as l:
                lv = l * NV
                local_dve(e, l, lv, L_CHAIN0)
                barrier(e, l * 3 + LAYER0)
                ln_dve(e, l + 2, R, H, True,
                       lambda b: (CO[:, bass.ds(lv + C_G, 1)], CO[:, bass.ds(lv + C_B, 1)]))
                barrier(e, l * 3 + LAYER0 + 1)
                ffn_dve(e, l, lv)
                barrier(e, l * 3 + LAYER0 + 2)
            for b in range(B):
                x = X[:, b * S:(b + 1) * S]
                e.scalar_tensor_tensor(out=x, in0=R[:, b * S:(b + 1) * S], scalar=MOD[:, 0, 5, b:b + 1],
                                       in1=x, op0=ALU.mult, op1=ALU.add)
            barrier(e, AFTER)
            ln_dve(e, DEPTH + 2, X, H, False, mod(1, 1, 0))
            barrier(e, AFTER + 1)
            block_dve(e, 1)
            barrier(e, AFTER + 2)
            ln_dve(e, DEPTH + 3, X, H, False, mod(1, 4, 3))
            barrier(e, AFTER + 3)
            e.wait_ge(s_wq, 64)
            fp4w_dve(e)
            fp4_dve(e)


def _tables():
    half = np.arange(0, DH, 2, dtype=np.float32)
    inv = (np.float32(1.0) / np.float32(10000.0) ** (half / np.float32(DH))).astype(np.float32)
    tok = np.arange(S, dtype=np.float32)
    freq = np.concatenate([tok[:, None] * inv[None, :]] * 2, -1)
    base = ((half + np.float32(0.4 * DH)) / np.float32(1.4 * DH)).astype(np.float32)
    scale = (base[None, :] ** ((tok - S // 2) / (WIN // 2))[:, None]).astype(np.float32)
    scale = np.concatenate([scale, scale], -1)
    cos, sin = np.cos(freq), np.sin(freq)
    sign = np.where(np.arange(DH) < DH // 2, -1.0, 1.0).astype(np.float32)
    qk = np.float32(8.0)
    tabs = [cos * scale * qk, cos / scale, sin * scale * sign * qk, sin / scale * sign]
    return np.stack([np.tile(t.T, (2, 1)) for t in tabs], 1).astype(np.float32)


def _mask():
    i, j = np.arange(WIN)[:, None], np.arange(2 * WIN)[None, :]
    band = np.where((j < i) | (j > i + WIN), MASKED, 0.0)
    m = np.zeros((4, WIN, 2, 2, 2 * WIN), np.float32)
    m[:] = band[None, :, None, None, :]
    m[0, :, 0, :, :WIN] = MASKED
    return m.reshape(P, 256)


def _mats():
    ones = np.kron(np.eye(2), np.ones((DH, DH)))
    return np.stack([ones, np.full((P, P), 1.0 / P), np.eye(P)], 1).astype(np.float32)


def kernel(**inputs):
    import concourse.bacc as _bacc
    from concourse.bass_utils import run_bass_kernel_spmd as _run

    a = {k: np.asarray(v) for k, v in inputs.items()}

    def chunks(w):
        return w.reshape(-1, P, w.shape[-1]).transpose(1, 0, 2).reshape(P, -1)

    w0 = np.concatenate([a["L0_attn_W" + n].reshape(INNER, P).T for n in "qkv"]
                        + [chunks(a["L0_attn_Wo"].T)], 1)
    w1 = np.concatenate([a["L1_attn_W" + n] for n in "qkv"] + [chunks(a["L1_attn_Wo"])], 1)
    qk = a["L0_ffn_Wqkv"][:, :, :2 * INNER].reshape(DEPTH, P, 2, PAIRS, 2, 2, DH // 2)
    both = np.stack([qk, qk[:, :, :, :, :, ::-1]], 2).transpose(0, 1, 4, 2, 3, 5, 6, 7)
    wl = np.concatenate([both.reshape(DEPTH, P, 4 * INNER), a["L0_ffn_Wqkv"][:, :, 2 * INNER:],
                         np.stack([chunks(w) for w in a["L0_ffn_Wo"]])], 2)
    cols = np.zeros((P, DEPTH, NV), np.float32)
    cols[:, :, C_G], cols[:, :, C_B], cols[:, :, C_B2] = (a["L0_ffn_" + n].T for n in ("ln_g", "ln_b", "b2"))
    for i, (o, w) in enumerate(FCH):
        cols[:w, :, C_B1A + i] = a["L0_ffn_b1"][:, o:o + w].T
        cols[:w, :, C_B1G + i] = a["L0_ffn_b1"][:, FI + o:FI + o + w].T
    for c, n in ((C_QS, "q_scale"), (C_KS, "k_scale")):
        v = a["L0_ffn_" + n].T
        cols[:, :, c] = np.concatenate([v, v])
        v = np.concatenate([v[DH // 2:], v[:DH // 2]])
        cols[:, :, c + 1] = np.concatenate([v, v])
    arrays = dict(
        xT=a["L0_attn_x"].transpose(2, 0, 1).reshape(P, T),
        cT=np.stack([a["L0_c"].T, a["L1_c"].T]), wmod=np.stack([a["L0_wmod"], a["L1_wmod"]]),
        bo=a["L0_attn_bo"].reshape(P, 1), w0=w0, w1=w1, wl=wl, f1=a["L0_ffn_W1"], f2=a["L0_ffn_W2"],
        cols=cols.reshape(P, DEPTH * NV), tabs=_tables(), mask=_mask(), mats=_mats(),
        wgu=np.stack([a["L1_ffn_w_gate"], a["L1_ffn_w_up"]], 1), wd=a["L1_ffn_w_down"])
    nc = _bacc.Bacc("TRN2", target_bir_lowering=False, num_devices=1)
    arrays = {f"in_{k}": np.ascontiguousarray(v) for k, v in arrays.items()}
    args = [nc.dram_tensor(k, v.shape, mybir.dt.from_np(v.dtype), kind="ExternalInput").ap()
            for k, v in arrays.items()]
    o = nc.dram_tensor("out_x", (P, T), F32, kind="ExternalOutput").ap()
    build(nc, *args, o)
    r = _run(nc, [arrays], core_ids=[0])
    y = r.results[0]["out_x"]
    return np.ascontiguousarray(y.reshape(P, B, S).transpose(1, 2, 0))
```

```python
from contextlib import ExitStack

import numpy as np

import concourse.bass as bass
from concourse import mybir

ALU = mybir.AluOpType
ACT = mybir.ActivationFunctionType
AX = mybir.AxisListType
F32 = mybir.dt.float32
F32R = mybir.dt.float32r
BF16 = mybir.dt.bfloat16

P = 128
B, S = 8, 256
T = B * S
DH = 64
PAIRS = 8
INNER = PAIRS * P
DEPTH = 6
WIN = 32
FI = 341
FCH = [(0, 128), (128, 128), (256, FI - 256)]
QI = 352
QCH = [(0, 128), (128, 128), (256, QI - 256)]
CH = 512
NCH = T // CH
SC0 = float(np.float32(1.0) / np.float32(0.04))
LN_EPS = 1e-5
NSCALE, NFLOOR, NBIAS = float(2.0 ** 24), float(2.0 ** -62), float(12 * np.log(2.0))
MASKED = -1.0e30
BIG = float(np.finfo(np.float32).max)
FIRST = 8

C_G, C_B, C_B2, C_B1A, C_B1G, C_QS, C_QSR, C_KS, C_KSR, NV = 0, 1, 2, 3, 6, 9, 10, 11, 12, 13


class Chain:

    def __init__(self, e, sem, base):
        self.e, self.sem, self.base, self.n = e, sem, base, 0

    def __call__(self, instruction, behind=0):
        self.n += 1
        instruction.then_inc(self.sem, 1)
        self.e.wait_ge(self.sem, self.base + self.n - behind)


def build(nc, xT, cT, wmod, bo, w0, w1, wl, f1, f2, cols, tabs, mask, mats, wgu, wd, out):
    ctx = ExitStack()
    with ctx:
        def sb(name, shape, dt=F32):
            return ctx.enter_context(nc.sbuf_tensor(name, shape, dt))

        def sem(name):
            return ctx.enter_context(nc.semaphore(name))

        X = sb("X", [P, T])
        R = sb("R", [P, T])
        H = sb("H", [P, T])
        WB = sb("WB", [P, 4 * INNER])
        XH = sb("XH", [P, T], F32R)
        XL = sb("XL", [P, T], F32R)
        WS = sb("WS", [P, 4 * INNER])
        WH = sb("WH", [P, 4 * INNER], F32R)
        WL = sb("WL", [P, 4 * INNER], F32R)
        WA = sb("WA", [P, 2 * INNER])
        W1 = sb("W1", [P, 2 * FI])
        W2 = sb("W2", [P, 3, P])
        CO = sb("CO", [P, DEPTH * NV])
        TAB = sb("TAB", [P, 4, S])
        LT = sb("LT", [P, 4, S])
        MSK = sb("MSK", [P, 256])
        MSKB = sb("MSKB", [P, 256], BF16)
        MAT = sb("MAT", [P, 3, P])
        IDB = sb("IDB", [P, P], BF16)
        CT = sb("CT", [P, 2, B])
        CE = sb("CE", [P, 2, B])
        CR = sb("CR", [P, 2, B])
        MOD = sb("MOD", [P, 2, 6, B])
        MT = sb("MT", [P, 2, 2, 2, B])
        BO = sb("BO", [P, 2])
        KC = sb("KC", [P, 4])
        xs = sb("xs", [P, S])
        xc = sb("xc", [P, T])
        xq = sb("xq", [P, T])
        WM = xq[:, 0:12 * P].rearrange("p (k n) -> p k n", k=2)
        t1, t2, sq = (v.rearrange("p (a n) -> p a n", a=2)
                      for v in (xc[:, 0:1024], xc[:, 1024:2048], xq[:, 0:1024]))
        rl = sb("rl", [P, 2, 260])
        rn = sb("rn", [P, 2, 260])
        k1 = sb("k1", [P, 2, S])
        qz = sb("qz", [P, 2, 2, S])
        kT = sb("kT", [P, 2, WIN + S])
        vb = sb("vb", [P, PAIRS, 2, P])
        mx = sb("mx", [P, 2, 16])
        bm = sb("bm", [P, 2, 16])
        LIM = sb("LIM", [P, 16])
        sm = sb("sm", [P, 2, 16])
        rq = sb("rq", [P, 4, 4])
        nb = sb("nb", [P, 2, 4])
        rs = sb("rs", [P, 2, 16])
        dl = sb("dl", [P, 2, 16])
        al = sb("al", [P, 2, 16])
        ls = sb("ls", [P, 2, 16])
        wt = sb("wt", [P, 2, 16])
        SH = sb("SH", [P, 6 * 1024])

        def share(at, *shape):
            names = "abcd"[:len(shape)]
            return SH[:, at:at + int(np.prod(shape))].rearrange(
                f"p ({' '.join(names)}) -> p {' '.join(names)}", **dict(zip(names, shape)))

        s1 = share(0, 2, 1024)
        pe_ = share(2048, 2, 1024)
        pn = share(4096, 2, 1024)
        pt = sb("pt", [P, 2, 2, 2, S])
        ot = sb("ot", [P, 2, S])
        yr = sb("yr", [P, S])
        hg = share(0, 2, 3, CH)
        ga = share(6 * CH, 3, CH)
        WG = sb("WG", [P, 3, 2, P])
        WD = sb("WD", [P, QI])
        NQ = 6 * P
        fs = sb("fs", [P, NQ // 16])
        fr = sb("fr", [P, NQ // 16])
        fs2 = sb("fs2", [P, 2, NQ // 16])
        fa, fn = ([WS[:, (i + k) * NQ:(i + k + 1) * NQ] for k in range(2)] for i in (0, 2))
        fx, fq = ([W[:, k * NQ:(k + 1) * NQ] for k in range(2)] for W in (WA, WB))
        fc, ft, fg = WB[:, 2 * NQ:3 * NQ], WB[:, 3 * NQ:4 * NQ], WB[:, 4 * NQ:4 * NQ + 2 * QI]
        h3 = share(0, 2, 3, S)
        hT = share(6 * S, 2, S)
        WGT = share(8 * S, 2, QI)
        WDT = share(8 * S + 2 * QI, 3, P)

        PS = ctx.enter_context(nc.psum_tensor("PS", [P, 8, 512], F32))

        s_in = sem("s_in")
        s_wb = sem("s_wb")
        s_ws = sem("s_ws")
        s_split = sem("s_split")
        s_hi = sem("s_hi")
        s_xh = sem("s_xh")
        s_xl = sem("s_xl")
        s_wa = sem("s_wa")
        s_wf = sem("s_wf")
        s_wq = sem("s_wq")
        s_out = sem("s_out")
        s_pass = sem("s_pass")
        s_bar = sem("s_bar")
        s_v = sem("s_v")
        s_cs = sem("s_cs")
        s_cw = sem("s_cw")
        s_cr = sem("s_cr")
        s_cp = sem("s_cp")
        s_c = sem("s_c")
        s_m = sem("s_m")
        s_xs = sem("s_xs")
        s_qk = sem("s_qk")
        s_rot = sem("s_rot")
        s_vp = sem("s_vp")
        s_sq = sem("s_sq")
        s_ssq = sem("s_ssq")
        s_t1 = sem("s_t1")
        s_t2 = sem("s_t2")
        s_ln = sem("s_ln")
        s_rn = sem("s_rn")
        s_add = sem("s_add")
        s_pl = sem("s_pl")
        s_pz = sem("s_pz")
        s_kn = sem("s_kn")
        s_vev = sem("s_vev")
        s_sc = sem("s_sc")
        s_mx = sem("s_mx")
        s_nb = sem("s_nb")
        s_exp = sem("s_exp")
        s_rs = sem("s_rs")
        s_pn = sem("s_pn")
        s_pt = sem("s_pt")
        s_av = sem("s_av")
        s_oev = sem("s_oev")
        s_wo = sem("s_wo")
        s_res = sem("s_res")
        g_xs = sem("g_xs")
        g_qk = sem("g_qk")
        g_vp = sem("g_vp")
        g_qev = sem("g_qev")
        g_vev = sem("g_vev")
        g_sc = sem("g_sc")
        g_d = sem("g_d")
        g_mx = sem("g_mx")
        g_exp = sem("g_exp")
        g_w = sem("g_w")
        g_f = sem("g_f")
        g_pn = sem("g_pn")
        g_tp = sem("g_tp")
        g_pta = sem("g_pta")
        g_ptv = sem("g_ptv")
        g_av = sem("g_av")
        g_oev = sem("g_oev")
        g_wo = sem("g_wo")
        g_res = sem("g_res")
        n_x = sem("n_x")
        n_mu = sem("n_mu")
        n_xc = sem("n_xc")
        n_sq = sem("n_sq")
        n_var = sem("n_var")
        n_ln = sem("n_ln")
        n_rs = sem("n_rs")
        n_xn = sem("n_xn")
        n_h = sem("n_h")
        f_hg = sem("f_hg")
        f_ge = sem("f_ge")
        f_gu = sem("f_gu")
        f_y = sem("f_y")
        f_res = sem("f_res")
        q_x = sem("q_x")
        q_abs = sem("q_abs")
        q_sc = sem("q_sc")
        q_sp = sem("q_sp")
        q_q = sem("q_q")
        q_t = sem("q_t")
        q_ev = sem("q_ev")
        q_tok = sem("q_tok")
        q_gu = sem("q_gu")
        q_silu = sem("q_silu")
        q_mul = sem("q_mul")
        q_y = sem("q_y")
        q_res = sem("q_res")

        COUNTERS = [f_ge, f_gu, f_hg, f_res, f_y, g_av, g_d, g_exp, g_mx,
                    g_oev, g_pn, g_pta, g_ptv, g_qev, g_qk, g_res, g_sc, g_tp,
                    g_vev, g_vp, g_w, g_wo, g_xs, n_ln, n_mu, n_rs, n_sq,
                    n_h, n_var, n_x, n_xc, n_xn, g_f, q_x, q_abs, q_sc, q_sp, q_q, q_t,
                    q_ev, q_tok, q_gu, q_silu, q_mul, q_y, q_res, s_add, s_av,
                    s_exp, s_kn, s_ln, s_mx, s_nb, s_oev, s_pl, s_pn, s_pt,
                    s_qk, s_res, s_rn, s_rot, s_rs, s_sc, s_sq, s_ssq, s_t1,
                    s_t2, s_vev, s_vp, s_wo, s_xs]

        ONES, MEAN, IDN = MAT[:, 0, :], MAT[:, 1, :], MAT[:, 2, :]

        def wait_apart(e, sem, value):
            e.wait_ge(sem, value)
            e.sem_inc(s_pass, 1)

        def barrier(e, k):
            e.drain().then_inc(s_bar, 1)
            wait_apart(e, s_bar, (k + 1) * 5)

        LAYER0 = 4
        AFTER = LAYER0 + 2 * DEPTH

        def ln_dve(e, call, src, dst, shift, affine):
            c0 = call * NCH
            if shift:
                for c in range(NCH):
                    for hb in range(2):
                        a = c * CH + hb * S
                        e.tensor_copy(xq[0:DH, a:a + S], src[0:DH, a:a + S])
                        e.memset(xq[DH:P, a:a + 1], 0.0)
                        i = e.tensor_copy(xq[DH:P, a + 1:a + S], src[DH:P, a:a + S - 1])
                    i.then_inc(n_x, 1)
            for c in range(NCH):
                a = c * CH
                e.wait_ge(n_mu, FIRST + c0 + (c + 1))
                e.tensor_tensor(xc[:, a:a + CH], (xq if shift else src)[:, a:a + CH], PS[:, c, :],
                                ALU.subtract).then_inc(n_xc, 1)
            for c in range(NCH):
                a = c * CH
                e.wait_ge(n_rs, FIRST + c0 + (c + 1))
                e.tensor_tensor(xc[:, a:a + CH], xc[:, a:a + CH], xq[:, a:a + CH],
                                ALU.mult).then_inc(n_xn, 1)
                e.wait_ge(n_xn, FIRST + c0 + (c + 1))
                for hb in range(2):
                    g, o = affine(2 * c + hb)
                    i = e.tensor_scalar(dst[:, a + hb * S:a + hb * S + S], xc[:, a + hb * S:a + hb * S + S],
                                        g, o, ALU.mult, ALU.add)
                i.then_inc(n_h, 1)

        def ln_pe(e, call, src, shift, shifts):
            c0 = call * NCH
            for c in range(NCH):
                a = c * CH
                if shift:
                    e.wait_ge(n_x, FIRST + shifts * NCH + (c + 1))
                e.matmul(PS[:, c, :], MEAN, (xq if shift else src)[:, a:a + CH],
                         start=True, stop=True).then_inc(n_mu, 1)
            for c in range(NCH):
                e.wait_ge(n_sq, FIRST + c0 + (c + 1))
                e.matmul(PS[:, 4 + c, :], MEAN, xq[:, c * CH:(c + 1) * CH],
                         start=True, stop=True).then_inc(n_var, 1)

        def ln_act(e, call):
            c0 = call * NCH
            for c in range(NCH):
                a = c * CH
                e.wait_ge(n_xc, FIRST + c0 + (c + 1))
                e.activation(xq[:, a:a + CH], xc[:, a:a + CH], ACT.Square).then_inc(n_sq, 1)
            for c in range(NCH):
                a = c * CH
                e.wait_ge(n_var, FIRST + c0 + (c + 1))
                e.activation(xq[:, a:a + CH], PS[:, 4 + c, :], ACT.Ln, bias=KC[:, 2:3]).then_inc(n_ln, 1)
                e.wait_ge(n_ln, FIRST + c0 + (c + 1))
                e.activation(xq[:, a:a + CH], xq[:, a:a + CH], ACT.Exp, scale=-0.5).then_inc(n_rs, 1)

        NS = PAIRS

        def steps(e, base, stages, NS=PAIRS, B=B):
            last = max(lag for _, lag in stages)
            for s in range(NS):
                for stage, lag in stages:
                    if s >= lag:
                        stage(s - lag, base + (s - lag), 0)
            with e.Fori(1, B) as b:
                for s in range(NS):
                    for stage, lag in stages:
                        stage((s - lag) % NS, base + b * NS + (s - lag), b - 1 if s < lag else b)
            for s in range(NS, NS + last):
                for stage, lag in stages:
                    if s - lag < NS:
                        stage(s - lag, base + ((B - 1) * NS + s - lag), B - 1)

        HPV = INNER

        def local_pe(e, l):
            wait_apart(e, s_wa, (l + 1) * 16)
            wait_apart(e, s_split, l + 1)

            wait_apart(e, s_xl, (l + 1) * 2 * NCH)

            def exact(out, w, b):
                xh, xl = (x[:, bass.ds(b * S, S)] for x in (XH, XL))
                e.matmul(out, WH[:, w:w + P], xh, start=True, stop=False)
                e.matmul(out, WL[:, w:w + P], xh, start=False, stop=False)
                return e.matmul(out, WH[:, w:w + P], xl, start=False, stop=True)

            def project(t, n, b):
                p = t % 2
                e.wait_ge(s_t1, FIRST + n - 1)
                w = t * 512
                exact(PS[:, p, 0:S], w, b)
                exact(PS[:, p, S:2 * S], w + P, b).then_inc(s_qk, 1)

            def project_more(t, n, b):
                w = t * 512
                e.wait_ge(s_t2, FIRST + n)
                exact(PS[:, 2, 0:S], w + 2 * P, b)
                exact(PS[:, 2, S:2 * S], w + 3 * P, b).then_inc(s_rot, 1)
                if t == 0:
                    e.wait_ge(s_xs, FIRST + (l * B + b + 1) * 2)
                e.wait_ge(s_vev, FIRST + n)
                for j in range(2):
                    i = e.matmul(PS[:, 5, j * P:(j + 1) * P], xs[:, j * P:(j + 1) * P],
                                 WA[:, t * P:(t + 1) * P],
                                 start=True, stop=True)
                i.then_inc(s_vp, 1)

            def norms(t, n, b):
                p = t % 2
                e.wait_ge(s_sq, FIRST + n + 1)
                e.wait_ge(s_ln, FIRST + n)
                e.matmul(PS[:, 3, 0:S], ONES, sq[:, p, S:2 * S], start=True, stop=True)
                for j in range(2):
                    i = e.matmul(PS[:, 3, S + 2 * j:S + 2 * j + 2], sq[:, p, j * P:(j + 1) * P],
                                 MAT[:, 0, 0:P:DH], start=True, stop=True)
                i.then_inc(s_ssq, 1)

            def scores(t, n, b):
                p = t % 2
                e.wait_ge(s_exp, FIRST + n)
                e.wait_ge(s_add, FIRST + n + 1)
                e.wait_ge(s_kn, FIRST + n + 1)
                e.matmul(PS[:, 4, 0:256], IDB[:, :], MSKB[:, :], start=True, stop=False,
                         skip_group_check=True)
                for j in range(2):
                    for h in range(2):
                        for u in range(4):
                            w = j * P + u * WIN
                            o = (2 * j + h) * 64
                            i = e.matmul(PS[u * WIN:(u + 1) * WIN, 4, o:o + 64],
                                         qz[:, p, h, w:w + WIN], kT[:, p, w:w + 64],
                                         start=False, stop=(j == h == 1), skip_group_check=True)
                i.then_inc(s_sc, 1)

            def values(t, n, b):
                p = t % 2
                e.wait_ge(s_pt, FIRST + n + 1)
                e.wait_ge(s_oev, FIRST + n)
                for h in range(2):
                    o = PS[h * DH:(h + 1) * DH, 6, :]
                    e.matmul(o[:, 0:P + WIN], vb[:, t, 0, h * DH:(h + 1) * DH], pt[:, p, 0, h, 0:P + WIN],
                             start=True, stop=False, skip_group_check=True)
                    i = e.matmul(o[:, P:S], vb[:, t, 1, h * DH:(h + 1) * DH],
                                 pt[:, p, 1, h, 0:P], start=False, stop=True, skip_group_check=True)
                i.then_inc(s_av, 1)

            def project_out(t, n, b):
                p = t % 2
                e.wait_ge(s_oev, FIRST + n + 1)
                if t == 0:
                    e.wait_ge(s_res, FIRST + l * B + b)
                i = e.matmul(PS[:, 7, 0:S], WA[:, HPV + t * P:HPV + (t + 1) * P], ot[:, p, :],
                             start=(t == 0), stop=(t == NS - 1))
                i.then_inc(s_wo, 1)

            steps(e, l * (B * NS), [(values, 6), (project, 0), (project_more, 0), (scores, 2),
                                    (norms, 0), (project_out, 7)])

        def local_act(e, l):

            def tokens(t, n, b):
                if t == 0:
                    e.wait_ge(s_vp, FIRST + n)
                    e.activation(xs[0:DH, :], R[0:DH, bass.ds(b * S, S)], ACT.Copy).then_inc(s_xs, 1)
                    e.activation(xs[DH:P, 1:S], R[DH:P, bass.ds(b * S, S - 1)],
                                 ACT.Copy).then_inc(s_xs, 1)

            def squares(t, n, b):
                p = t % 2
                e.wait_ge(s_qk, FIRST + n + 1)
                e.wait_ge(s_ssq, FIRST + n - 1)
                e.activation(sq[:, p, :], PS[:, p, :], ACT.Square).then_inc(s_sq, 1)

            def evac_v(t, n, b):
                e.wait_ge(s_vp, FIRST + n + 1)
                e.wait_ge(s_av, FIRST + n - 7)
                e.activation(vb[:, t, :, :], PS[:, 5, 0:2 * P].rearrange("p (j d) -> p j d", j=2),
                             ACT.Copy).then_inc(s_vev, 1)

            def norms(t, n, b):
                p = t % 2
                e.wait_ge(s_ssq, FIRST + n + 1)
                e.wait_ge(s_rn, FIRST + n)
                e.activation(rl[:, p, :], PS[:, 3, 0:260], ACT.Ln, bias=KC[:, 0:1],
                             scale=NSCALE).then_inc(s_ln, 1)
                e.wait_ge(s_ln, FIRST + n + 1)
                e.wait_ge(s_kn, FIRST + n - 1)
                e.activation(rn[:, p, :], rl[:, p, :], ACT.Exp, bias=KC[:, 1:2],
                             scale=-0.5).then_inc(s_rn, 1)

            def exps(t, n, b):
                p = t % 2
                e.wait_ge(s_nb, FIRST + n + 1)
                e.wait_ge(s_pn, FIRST + n - 1)
                e.wait_ge(s_rs, FIRST + n - 1)
                for g in range(4):
                    i = e.activation(pe_[:, p, g * 64:(g + 1) * 64], PS[:, 4, g * 64:(g + 1) * 64],
                                     ACT.Exp, bias=nb[:, p, g:g + 1], scale=rq[:, t % 4, g:g + 1],
                                     accum_out=sm[:, p, g:g + 1])
                i.then_inc(s_exp, 1)

            def evac(t, n, b):
                p = t % 2
                e.wait_ge(s_av, FIRST + n + 1)
                e.wait_ge(s_wo, FIRST + n - 1)
                e.activation(ot[:, p, :], PS[:, 6, 0:S], ACT.Copy).then_inc(s_oev, 1)

            steps(e, l * (B * NS), [(tokens, 0), (evac, 7), (norms, 1), (exps, 3), (squares, 0), (evac_v, 0)])

        def split_tokens(e, l, c):
            a = c * CH

            def shifted(x, o):
                return x[DH:P, a:a + CH].rearrange("p (b n) -> p b n", n=S)[:, :, o:o + S - 1]

            e.tensor_copy(XH[0:DH, a:a + CH], R[0:DH, a:a + CH]).then_inc(s_xh, 1)
            e.tensor_copy(shifted(XH, 1), shifted(R, 0)).then_inc(s_xh, 1)
            wait_apart(e, s_xh, (l * NCH + c + 1) * 2)
            e.tensor_tensor(XL[0:DH, a:a + CH], R[0:DH, a:a + CH], XH[0:DH, a:a + CH],
                            ALU.subtract).then_inc(s_xl, 1)
            e.tensor_tensor(shifted(XL, 1), shifted(R, 0), shifted(XH, 1),
                            ALU.subtract).then_inc(s_xl, 1)

        def local_dve(e, l, lv, lt_base):
            for i, col in enumerate((C_QS, C_KS, C_QSR, C_KSR)):
                k = e.tensor_scalar(LT[:, i, :], TAB[:, i, :], CO[:, bass.ds(lv + col, 1)], None, ALU.mult)
            k.then_inc(s_v, 1)
            wait_apart(e, s_v, lt_base + l + 1)

            def rotary(t, n, b):
                p = t % 2
                e.wait_ge(s_sq, FIRST + n + 1)
                e.wait_ge(s_add, FIRST + n - 1)
                e.tensor_tensor(t1[:, p, :], PS[:, p, :], LT[:, 0:2, :].rearrange("p a n -> p (a n)"),
                                ALU.mult).then_inc(s_t1, 1)

            def rotary_more(t, n, b):
                p = t % 2
                e.wait_ge(s_rot, FIRST + n + 1)
                e.tensor_tensor(t2[:, p, :], PS[:, 2, :], LT[:, 2:4, :].rearrange("p a n -> p (a n)"),
                                ALU.mult).then_inc(s_t2, 1)

            def keys(t, n, b):
                p = t % 2
                e.wait_ge(s_rn, FIRST + n + 1)
                e.wait_ge(s_exp, FIRST + n - 3)
                e.tensor_scalar(rq[:, t % 4, :], rn[:, p, S:S + 4], 1e12, None, ALU.min)
                e.wait_ge(s_add, FIRST + n + 1)
                e.wait_ge(s_sc, FIRST + n - 1)
                e.scalar_tensor_tensor(out=kT[:, p, WIN:], in0=rn[:, p, 0:S], scalar=1e12,
                                       in1=k1[:, p, :], op0=ALU.min, op1=ALU.mult).then_inc(s_kn, 1)

            def maxima(t, n, b):
                p = t % 2
                e.wait_ge(s_sc, FIRST + n + 1)
                e.tensor_reduce(mx[:, p, 0:4], PS[:, 4, 0:256].rearrange("p (g k) -> p g k", g=4),
                                AX.X, ALU.max).then_inc(s_mx, 1)
                e.wait_ge(s_mx, FIRST + n + 1)
                e.wait_ge(s_exp, FIRST + n - 1)
                e.scalar_tensor_tensor(out=nb[:, p, :], in0=mx[:, p, 0:4], scalar=-1.0,
                                       in1=rq[:, t % 4, :], op0=ALU.mult, op1=ALU.mult).then_inc(s_nb, 1)

            def sums(t, n, b):
                p = t % 2
                e.wait_ge(s_exp, FIRST + n + 1)
                e.wait_ge(s_pn, FIRST + n - 1)
                e.reciprocal(rs[:, p, 0:4], sm[:, p, 0:4]).then_inc(s_rs, 1)

            def turn(t, n, b):
                p = t % 2
                e.wait_ge(s_pn, FIRST + n + 1)
                e.wait_ge(s_av, FIRST + n - 1)
                v = pn[:, p, 0:256].rearrange("p (j h f k) -> p j h f k", j=2, h=2, f=2)
                for u in range(4):
                    a = u * WIN
                    e.transpose(pt[a:a + WIN, p, :, :, a:a + WIN], v[a:a + WIN, :, :, 1, :])
                    if u:
                        e.transpose(pt[a - WIN:a, p, :, :, a:a + WIN], v[a:a + WIN, :, :, 0, :])
                e.transpose(pt[P - WIN:P, p, 0, :, P:P + WIN],
                            v[0:WIN, 1, :, 0, :]).then_inc(s_pt, 1)

            def residual(t, n, b):
                if t == NS - 1:
                    e.wait_ge(s_wo, FIRST + n + 1)
                    e.tensor_tensor(R[:, bass.ds(b * S, S)], PS[:, 7, 0:S], R[:, bass.ds(b * S, S)],
                                    ALU.add).then_inc(s_res, 1)

            steps(e, l * (B * NS), [(sums, 4), (maxima, 3), (turn, 5), (residual, 8),
                                    (rotary, 0), (rotary_more, 0), (keys, 1)])

        def local_pool(e, l):
            def add(t, n, b):
                p = t % 2
                e.wait_ge(s_t1, FIRST + n + 1)
                e.wait_ge(s_t2, FIRST + n + 1)
                e.wait_ge(s_kn, FIRST + n - 1)
                e.wait_ge(s_sc, FIRST + n - 1)
                e.tensor_tensor(k1[:, p, :], t1[:, p, S:], t2[:, p, S:], ALU.add).then_inc(s_pl, 1)
                for h in range(2):
                    r = slice(h * DH, (h + 1) * DH)
                    i = e.tensor_tensor(qz[r, p, h, :], t1[r, p, 0:S], t2[r, p, 0:S], ALU.add)
                    if h == 0:
                        i.then_inc(s_pl, 1)
                        e.wait_ge(s_pl, FIRST + 2 * n + 2)
                i.then_inc(s_add, 1)
                e.wait_ge(s_add, FIRST + n + 1)

            def divide(t, n, b):
                p = t % 2
                e.wait_ge(s_rs, FIRST + n + 1)
                e.wait_ge(s_pt, FIRST + n - 1)
                e.tensor_tensor(pn[:, p, 0:256].rearrange("p (g k) -> p g k", g=4),
                                pe_[:, p, 0:256].rearrange("p (g k) -> p g k", g=4),
                                rs[:, p, 0:4].rearrange("p (g o) -> p g o", o=1)
                                .broadcast_to([P, 4, 64]), ALU.mult).then_inc(s_pn, 1)

            steps(e, l * (B * NS), [(add, 1), (divide, 4)])

        def block_pe(e, k):
            e.wait_ge(s_wb, (k + 1) * 16)

            def project(t, n, b):
                if t == 0:
                    e.wait_ge(g_xs, FIRST + k * B + b + 1)
                e.wait_ge(g_qev, FIRST + n)
                e.matmul(PS[:, 0, 0:S], WB[:, t * P:(t + 1) * P], xs[:, :], start=True, stop=True)
                e.matmul(PS[:, 0, S:2 * S], WB[:, INNER + t * P:INNER + (t + 1) * P], xs[:, :],
                         start=True, stop=True).then_inc(g_qk, 1)
                e.wait_ge(g_vev, FIRST + n)
                for j in range(2):
                    i = e.matmul(PS[:, 1, j * P:(j + 1) * P], xs[:, j * P:(j + 1) * P],
                                 WB[:, 2 * INNER + t * P:2 * INNER + (t + 1) * P],
                                 start=True, stop=True)
                i.then_inc(g_vp, 1)

            def scores(t, n, b):
                p = t % 2
                e.wait_ge(g_qev, FIRST + n + 1)
                e.wait_ge(g_d, FIRST + n)
                for j in range(2):
                    for h in range(2):
                        i = e.matmul(PS[:, 2 + j, h * S:(h + 1) * S], qz[:, p, h, j * P:(j + 1) * P],
                                     kT[:, p, WIN:], start=True, stop=True)
                i.then_inc(g_sc, 1)

            def turn(t, n, b):
                p = t % 2
                e.wait_ge(g_pn, FIRST + n + 1)
                e.wait_ge(g_pta, FIRST + n)
                e.wait_ge(g_ptv, FIRST + n)
                for h in range(2):
                    for kt in range(2):
                        for j in range(2):
                            o = kt * S + j * P
                            c = (2 * j + h) * S + kt * P
                            i = e.transpose(PS[:, 4 + h, o:o + P], pn[:, p, c:c + P], IDN)
                i.then_inc(g_tp, 1)

            def values(t, n, b):
                p = t % 2
                e.wait_ge(g_pta, FIRST + n + 1)
                e.wait_ge(g_ptv, FIRST + n + 1)
                e.wait_ge(g_oev, FIRST + n)
                for h in range(2):
                    for kt in range(2):
                        i = e.matmul(PS[h * DH:(h + 1) * DH, 6, 0:S],
                                     vb[:, t, kt, h * DH:(h + 1) * DH], pt[:, p, h, kt, :],
                                     start=(kt == 0), stop=(kt == 1), skip_group_check=True)
                i.then_inc(g_av, 1)

            def project_out(t, n, b):
                p = t % 2
                e.wait_ge(g_oev, FIRST + n + 1)
                if t == 0:
                    e.wait_ge(g_res, FIRST + k * B + b)
                i = e.matmul(PS[:, 7, 0:S], WB[:, 3 * INNER + t * P:3 * INNER + (t + 1) * P],
                             ot[:, p, :], start=(t == 0), stop=(t == NS - 1))
                i.then_inc(g_wo, 1)

            steps(e, k * (B * NS), [(values, 7), (project_out, 8), (project, 0), (scores, 1), (turn, 5)])

        def block_act(e, k):

            def evac_qkv(t, n, b):
                p = t % 2
                e.wait_ge(g_qk, FIRST + n + 1)
                e.wait_ge(g_sc, FIRST + n - 1)
                for h in range(2):
                    r = slice(h * DH, (h + 1) * DH)
                    e.activation(qz[r, p, h, :], PS[r, 0, 0:S], ACT.Copy)
                e.activation(kT[:, p, WIN:], PS[:, 0, S:2 * S], ACT.Copy).then_inc(g_qev, 1)
                e.wait_ge(g_vp, FIRST + n + 1)
                e.wait_ge(g_av, FIRST + n - 7)
                e.activation(vb[:, t, :, :], PS[:, 1, 0:2 * P].rearrange("p (j d) -> p j d", j=2),
                             ACT.Copy).then_inc(g_vev, 1)

            def exps(t, n, b):
                p = t % 2
                e.wait_ge(g_d if k else g_mx, FIRST + n + 1)
                e.wait_ge(g_pn, FIRST + n - 1)
                e.wait_ge(g_w, FIRST + n - 1)
                if k == 0:
                    for g in range(4):
                        i = e.activation(pe_[:, p, g * S:(g + 1) * S], s1[:, p, g * S:(g + 1) * S],
                                         ACT.Exp, bias=nb[:, p, g:g + 1], scale=SC0,
                                         accum_out=sm[:, p, g:g + 1])
                    i.then_inc(g_exp, 1)
                else:
                    a, d = (v[:, p, :].rearrange("p (g k) -> p g k", k=4)[:, :, 1:4] for v in (al, dl))
                    e.activation(a, d, ACT.Exp, scale=DH ** -0.5)
                    e.activation(pe_[:, p, :], s1[:, p, :], ACT.Exp,
                                 scale=DH ** -0.5).then_inc(g_exp, 1)

            def evac_pt(t, n, b):
                p = t % 2
                e.wait_ge(g_tp, FIRST + n + 1)
                e.wait_ge(g_av, FIRST + n - 1)
                e.activation(pt[:, p, 0, :, :].rearrange("p a n -> p (a n)"), PS[:, 4, :],
                             ACT.Copy).then_inc(g_pta, 1)
                if k:
                    e.activation(pt[:, p, 1, :, :].rearrange("p a n -> p (a n)"), PS[:, 5, :],
                                 ACT.Copy).then_inc(g_ptv, 1)

            def evac_o(t, n, b):
                p = t % 2
                e.wait_ge(g_av, FIRST + n + 1)
                e.wait_ge(g_wo, FIRST + n - 1)
                e.activation(ot[:, p, :], PS[:, 6, 0:S], ACT.Copy).then_inc(g_oev, 1)

            def tokens(t, n, b):
                if t == 0:
                    e.wait_ge(g_vp, FIRST + n)
                    e.activation(xs[:, :], H[:, bass.ds(b * S, S)], ACT.Copy).then_inc(g_xs, 1)

            steps(e, k * (B * NS), [(tokens, 0), (evac_pt, 6), (exps, 3), (evac_qkv, 0), (evac_o, 7)])

        def block_dve(e, k):
            SOFT, WGHT = (2, 2), (0, 2)
            before = k * B * NS

            def soft(t, n, b):
                p = t % 2
                chain = Chain(e, s_cs, before * SOFT[0] + (n - before) * SOFT[k])
                e.wait_ge(g_sc, FIRST + n + 1)
                e.wait_ge(g_exp, FIRST + n - 1)
                if k == 0:
                    sv = PS[:, 2:4, :]
                    s1v = s1[:, p, :].rearrange("p (a n) -> p a n", a=2)
                    chain(e.tensor_scalar(s1v, sv, 0.0, -1.0e9, ALU.is_equal, ALU.mult))
                    e.tensor_tensor(s1v, sv, s1v, ALU.add).then_inc(g_d, 1)
                    e.wait_ge(g_d, FIRST + n + 1)
                    chain(e.tensor_reduce(mx[:, p, 0:4], s1[:, p, :].rearrange("p (g q) -> p g q", g=4),
                                          AX.X, ALU.max))
                    e.tensor_scalar(nb[:, p, :], mx[:, p, 0:4], -SC0, None, ALU.mult).then_inc(g_mx, 1)
                else:
                    for j in range(2):
                        i = e.tensor_reduce(bm[:, p, 8 * j:8 * j + 8],
                                            PS[:, 2 + j, :].rearrange("p (g q) -> p g q", g=8),
                                            AX.X, ALU.max)
                    chain(i)
                    chain(e.tensor_tensor_scan(mx[:, p, :], LIM[:, :], bm[:, p, :], 0.0, ALU.min, ALU.max))
                    m = mx[:, p, :].rearrange("p (g k) -> p g k", k=4)
                    e.tensor_tensor(dl[:, p, :].rearrange("p (g k) -> p g k", k=4)[:, :, 1:4],
                                    m[:, :, 0:3], m[:, :, 1:4], ALU.subtract)
                    for j in range(2):
                        i = e.tensor_tensor(
                            s1[:, p, j * 512:(j + 1) * 512].rearrange("p (g q) -> p g q", g=8),
                            PS[:, 2 + j, :].rearrange("p (g q) -> p g q", g=8),
                            mx[:, p, 8 * j:8 * j + 8].rearrange("p (g o) -> p g o", o=1)
                            .broadcast_to([P, 8, 64]), ALU.subtract)
                    i.then_inc(g_d, 1)
                assert chain.n == SOFT[k]

            def weights(t, n, b):
                p = t % 2
                e.wait_ge(g_exp, FIRST + n + 1)
                e.wait_ge(g_pn, FIRST + n - 1)
                if k == 0:
                    e.reciprocal(rs[:, p, 0:4], sm[:, p, 0:4]).then_inc(g_w, 1)
                    return
                chain = Chain(e, s_cw, (n - before) * WGHT[k])
                chain(e.tensor_reduce(sm[:, p, :], pe_[:, p, :].rearrange("p (g q) -> p g q", g=16),
                                      AX.X, ALU.add))
                chain(e.tensor_tensor_scan(ls[:, p, :], al[:, p, :], sm[:, p, :], 0.0, ALU.mult, ALU.add))
                e.reciprocal(wt[:, p, :], ls[:, p, :]).then_inc(g_w, 1)
                assert chain.n == WGHT[k], chain.n

            def evac_pt(t, n, b):
                p = t % 2
                e.wait_ge(g_tp, FIRST + n + 1)
                e.wait_ge(g_av, FIRST + n - 1)
                e.tensor_copy(pt[:, p, 1, :, :].rearrange("p a n -> p (a n)"),
                              PS[:, 5, :]).then_inc(g_ptv, 1)

            def residual(t, n, b):
                if t == NS - 1:
                    e.wait_ge(g_wo, FIRST + n + 1)
                    Chain(e, s_cr, k * B + b)(
                        e.tensor_scalar(yr[:, :], PS[:, 7, 0:S], BO[:, k:k + 1],
                                        MOD[:, k, 2, bass.ds(b, 1)], ALU.add, ALU.mult))
                    e.tensor_tensor(X[:, bass.ds(b * S, S)], X[:, bass.ds(b * S, S)], yr[:, :],
                                    ALU.add).then_inc(g_res, 1)

            steps(e, k * (B * NS), [(weights, 4), (soft, 2)] + [(evac_pt, 6)] * (k == 0) + [(residual, 8)])

        def block_pool(e, k):
            def divide(t, n, b):
                p = t % 2
                e.wait_ge(g_w, FIRST + n + 1)
                e.wait_ge(g_tp, FIRST + n - 1)
                if k == 0:
                    v = [a[:, p, :].rearrange("p (g q) -> p g q", g=4) for a in (pn, pe_)]
                    f = rs[:, p, 0:4].rearrange("p (g o) -> p g o", o=1).broadcast_to([P, 4, S])
                else:
                    chain = Chain(e, s_cp, (n - k * B * NS) * 3)
                    w, a, u = (v[:, p, :].rearrange("p (g k) -> p g k", k=4) for v in (wt, al, rs))
                    chain(e.tensor_tensor(u[:, :, 0:3], w[:, :, 0:3], a[:, :, 1:4], ALU.mult))
                    for i in (2, 1, 0):
                        j = e.tensor_tensor(w[:, :, i:i + 1], u[:, :, i:i + 1], w[:, :, i + 1:i + 2], ALU.mult)
                        if i:
                            chain(j)
                    j.then_inc(g_f, 1)
                    e.wait_ge(g_f, FIRST + n - k * B * NS + 1)
                    v = [a[:, p, :].rearrange("p (g q) -> p g q", g=16) for a in (pn, pe_)]
                    f = wt[:, p, :].rearrange("p (g o) -> p g o", o=1).broadcast_to([P, 16, 64])
                e.tensor_tensor(v[0], v[1], f, ALU.mult).then_inc(g_pn, 1)

            steps(e, k * (B * NS), [(divide, 4)])

        def ffn_pe(e, l):
            e.wait_ge(s_wf, (l + 1) * 48)
            n0 = (l + 2) * NCH

            def hidden(c):
                e.wait_ge(n_h, FIRST + n0 + c + 1)
                for i, (o, w) in enumerate(FCH):
                    if c == 0 and i == 2:
                        e.wait_ge(n_ln, FIRST + n0 + 2)
                    if c:
                        e.wait_ge(f_gu, FIRST + l * 12 + (c - 1) * 3 + i + 1)
                    x = H[:, c * CH:(c + 1) * CH]
                    e.matmul(PS[0:w, 2 * i, :], W1[:, o:o + w], x, start=True, stop=True)
                    e.matmul(PS[0:w, 2 * i + 1, :], W1[:, FI + o:FI + o + w], x,
                             start=True, stop=True).then_inc(f_hg, 1)

            def down(c):
                e.wait_ge(f_gu, FIRST + l * 12 + 3 * (c + 1))
                if c >= 2:
                    e.wait_ge(f_res, FIRST + l * 4 + c - 1)
                else:
                    e.wait_ge(n_ln, FIRST + n0 + NCH)
                for i, (o, w) in enumerate(FCH):
                    j = e.matmul(PS[:, 6 + c % 2, :], W2[0:w, i, :], hg[0:w, c % 2, i, :],
                                 start=(i == 0), stop=(i == 2))
                j.then_inc(f_y, 1)

            hidden(0)
            for c in range(1, NCH):
                hidden(c)
                down(c - 1)
            down(NCH - 1)

        def ffn_act(e, l, lv):
            for c in range(NCH):
                for i, (o, w) in enumerate(FCH):
                    if c:
                        e.wait_ge(f_gu, FIRST + l * 12 + (c - 1) * 3 + i + 1)
                    wait_apart(e, f_hg, FIRST + l * 12 + 3 * c + i + 1)
                    e.activation(ga[0:w, i, :], PS[0:w, 2 * i + 1, :], ACT.Gelu,
                                 bias=CO[0:w, bass.ds(lv + C_B1G + i, 1)]).then_inc(f_ge, 1)

        def ffn_dve(e, l, lv):
            def residual(c):
                e.wait_ge(f_y, FIRST + l * 4 + c + 1)
                r = R[:, c * CH:(c + 1) * CH]
                e.scalar_tensor_tensor(out=r, in0=PS[:, 6 + c % 2, :], scalar=CO[:, bass.ds(lv + C_B2, 1)],
                                       in1=r, op0=ALU.add, op1=ALU.add).then_inc(f_res, 1)
                e.wait_ge(f_res, FIRST + l * 4 + c + 1)
                split_tokens(e, l + 1, c)
            for c in range(NCH):
                for i, (o, w) in enumerate(FCH):
                    e.wait_ge(f_ge, FIRST + l * 12 + 3 * c + i + 1)
                    if c >= 2 and i == 0:
                        e.wait_ge(f_y, FIRST + l * 4 + c - 1)
                    e.scalar_tensor_tensor(out=hg[0:w, c % 2, i, :], in0=PS[0:w, 2 * i, :],
                                           scalar=CO[0:w, bass.ds(lv + C_B1A + i, 1)], in1=ga[0:w, i, :],
                                           op0=ALU.add, op1=ALU.mult).then_inc(f_gu, 1)
                if c:
                    residual(c - 1)
            residual(NCH - 1)

        HID = 6
        QC = 12
        WIDTH = [6 * P, QI] + [CH] * NCH

        def but_first(stage):
            return lambda t, n, b: None if isinstance(n, int) and n == HID else stage(t, n, b)

        def job_act(e, n, p, x, w):
            e.wait_ge(q_q, FIRST + n - 1)
            e.activation(fa[p][:, 0:w], x, ACT.Abs)
            e.activation(fn[p][:, 0:w], x, ACT.Sign).then_inc(q_abs, 1)

        def job_pool(e, n, p, w):
            e.wait_ge(q_sc, FIRST + n + 1)
            e.tensor_tensor(fn[p][:, 0:w].rearrange("p (b q) -> p b q", q=16),
                            fn[p][:, 0:w].rearrange("p (b q) -> p b q", q=16),
                            fs2[:, p, 0:w // 16].rearrange("p (b o) -> p b o", o=1)
                            .broadcast_to([P, w // 16, 16]), ALU.mult).then_inc(q_sp, 1)

        def job_dve(e, n, p, w):
            chain = Chain(e, s_v, W_CHAIN0 + n * QC)
            a, c, t = fa[p][:, 0:w], fc[:, 0:w], ft[:, 0:w]
            sc, rc = fs[:, 0:w // 16], fr[:, 0:w // 16]
            blocks = a.rearrange("p (b q) -> p b q", q=16)
            e.wait_ge(q_abs, FIRST + n + 1)
            chain(e.tensor_reduce(sc, blocks, AX.X, ALU.max))
            chain(e.tensor_scalar(sc, sc, 1.0 / 6.0, 1e-12, ALU.mult, ALU.max))
            e.tensor_scalar(fs2[:, p, 0:w // 16], sc, 0.5, None, ALU.mult).then_inc(q_sc, 1)
            chain(e.reciprocal(rc, sc))
            chain(e.tensor_tensor(blocks, blocks, rc.rearrange("p (b o) -> p b o", o=1)
                                  .broadcast_to([P, w // 16, 16]), ALU.mult))
            chain(e.tensor_scalar(c, a, 0.25, None, ALU.is_gt), 1)
            chain(e.tensor_scalar(t, a, 5.0, 2.0, ALU.is_gt, ALU.mult), 1)
            for m, v in ((0.75, c), (2.5, t), (1.25, c), (3.5, t), (1.75, c)):
                chain(e.scalar_tensor_tensor(out=v, in0=a, scalar=m, in1=v, op0=ALU.is_gt, op1=ALU.add),
                      0 if m == 1.75 else 1)
            chain(e.scalar_tensor_tensor(out=c, in0=t, scalar=2.0, in1=c, op0=ALU.mult, op1=ALU.add))
            e.wait_ge(q_sp, FIRST + n + 1)
            e.wait_ge(q_t, FIRST + n - 1)
            e.tensor_tensor(fq[p][:, 0:w], c, fn[p][:, 0:w], ALU.mult).then_inc(q_q, 1)
            chain.n += 1
            e.wait_ge(q_q, FIRST + n + 1)
            assert chain.n == QC + 1

        def fp4_pe(e):
            for c in range(NCH):
                for j in range(4):
                    o = c * CH + j * P
                    i = e.transpose(PS[:, c, j * P:(j + 1) * P], H[:, o:o + P], IDN)
                i.then_inc(q_x, 1)
            e.wait_ge(q_q, FIRST + 1)
            for k in range(2):
                for i, (o, w) in enumerate(QCH):
                    j = e.transpose(PS[:, 4 + k, o:o + w], fq[0][0:w, (2 * i + k) * P:(2 * i + k + 1) * P],
                                    MAT[0:w, 2, 0:w])
            j.then_inc(q_t, 1)
            e.wait_ge(q_q, FIRST + 2)
            for i, (o, w) in enumerate(QCH):
                j = e.transpose(PS[0:w, 6, i * P:(i + 1) * P], fq[1][:, o:o + w], IDN)
            j.then_inc(q_t, 1)
            def tokens(c):
                e.wait_ge(q_q, FIRST + 3 + c)
                e.wait_ge(q_ev, FIRST + c + 1)
                for j in range(4):
                    i = e.transpose(PS[:, 7 - c % 2, j * P:(j + 1) * P], fq[c % 2][:, j * P:(j + 1) * P], IDN)
                i.then_inc(q_t, 1)

            def hidden(t, n, b):
                e.wait_ge(q_tok, FIRST + n - HID + 1)
                e.wait_ge(q_mul, FIRST + n - HID)
                for k in range(2):
                    for j in range(2):
                        i = e.matmul(PS[:, 2 + 2 * k + j, 0:QI], hT[:, t, j * P:(j + 1) * P], WGT[:, k, :],
                                     start=True, stop=True)
                i.then_inc(q_gu, 1)

            def turn(t, n, b):
                e.wait_ge(q_q, FIRST + n + 1)
                e.wait_ge(q_ev, FIRST + n)
                for i, (o, w) in enumerate(QCH):
                    for j in range(2):
                        x = e.transpose(PS[0:w, i // 2, (2 * (i % 2) + j) * P:(2 * (i % 2) + j + 1) * P],
                                        fq[t][:, j * QI + o:j * QI + o + w], IDN)
                x.then_inc(q_t, 1)

            def down(t, n, b):
                e.wait_ge(q_ev, FIRST + n + 1)
                e.wait_ge(q_res, FIRST + n - HID)
                for i, (o, w) in enumerate(QCH):
                    x = e.matmul(PS[:, 7, 0:S], WDT[0:w, i, :], h3[0:w, t, i, :],
                                 start=(i == 0), stop=(i == 2))
                x.then_inc(q_y, 1)

            for c in range(NCH - 1):
                tokens(c)
            e.wait_ge(q_abs, FIRST + HID)
            hidden(0, HID, 0)
            tokens(NCH - 1)
            steps(e, HID, [(but_first(hidden), 0), (turn, 2), (down, 2)], 2, B // 2)

        def fp4_act(e):
            def take(n):
                e.wait_ge(q_t, FIRST + n + 1)
                if n == 0:
                    i = e.activation(WGT[:, :, :], PS[:, 4:6, 0:QI], ACT.Copy)
                elif n == 1:
                    for j, (o, w) in enumerate(QCH):
                        i = e.activation(WDT[0:w, j, :], PS[0:w, 6, j * P:(j + 1) * P], ACT.Copy)
                else:
                    i = e.activation(H[:, (n - 2) * CH:(n - 1) * CH], PS[:, 7 - n % 2, :], ACT.Copy)
                i.then_inc(q_ev, 1)

            def tokens(t, n, b):
                e.wait_ge(q_gu, FIRST + n - HID - 1)
                e.activation(hT[:, t, :], H[:, bass.ds(b * 2 * S + t * S, S)], ACT.Copy).then_inc(q_tok, 1)

            def silu(t, n, b):
                e.wait_ge(q_gu, FIRST + n - HID + 1)
                e.wait_ge(q_mul, FIRST + n - HID)
                e.activation(fg[:, :].rearrange("p (j n) -> p j n", j=2), PS[:, 2:4, 0:QI],
                             ACT.Silu).then_inc(q_silu, 1)

            def magnitudes(t, n, b):
                e.wait_ge(q_mul, FIRST + n - HID + 1)
                job_act(e, n, t, fx[t][:, 0:2 * QI], 2 * QI)

            def take_hidden(t, n, b):
                e.wait_ge(q_t, FIRST + n + 1)
                e.wait_ge(q_y, FIRST + n - HID - 1)
                e.activation(h3[:, t, 0:2, :].rearrange("p i n -> p (i n)"), PS[:, 0, :], ACT.Copy)
                w = QCH[2][1]
                e.activation(h3[0:w, t, 2, :], PS[0:w, 1, 0:S], ACT.Copy).then_inc(q_ev, 1)

            for n in range(HID + 2):
                if n < HID:
                    if n >= 2:
                        e.wait_ge(q_x, FIRST + n - 1)
                    x = (WG[:, :, :, :].rearrange("p i k n -> p (i k n)"), WD[:, :])[n] if n < 2 \
                        else PS[:, n - 2, :]
                    job_act(e, n, n % 2, x, WIDTH[n])
                if n >= 2:
                    take(n - 2)
                if n == HID:
                    e.wait_ge(q_ev, FIRST + 3)
                    tokens(0, HID, 0)
                    silu(0, HID, 0)
            e.wait_ge(q_ev, FIRST + HID)

            steps(e, HID, [(but_first(tokens), 0), (but_first(silu), 0), (magnitudes, 0),
                           (take_hidden, 2)], 2, B // 2)

        def fp4_pool(e):
            for n in range(HID):
                job_pool(e, n, n % 2, WIDTH[n])

            def scales(t, n, b):
                job_pool(e, n, t, 2 * QI)

            steps(e, HID, [(scales, 0)], 2, B // 2)

        def fp4_dve(e):
            for n in range(HID):
                job_dve(e, n, n % 2, WIDTH[n])

            def product(t, n, b):
                e.wait_ge(q_silu, FIRST + n - HID + 1)
                e.wait_ge(q_abs, FIRST + n - 1)
                e.tensor_tensor(fx[t][:, 0:2 * QI].rearrange("p (j n) -> p j n", j=2), PS[:, 4:6, 0:QI],
                                fg[:, :].rearrange("p (j n) -> p j n", j=2), ALU.mult).then_inc(q_mul, 1)

            def quantize(t, n, b):
                job_dve(e, n, t, 2 * QI)

            def residual(t, n, b):
                e.wait_ge(q_y, FIRST + n - HID + 1)
                x = X[:, bass.ds(b * 2 * S + t * S, S)]
                e.scalar_tensor_tensor(out=x, in0=PS[:, 7, 0:S], scalar=MOD[:, 1, 5, bass.ds(b * 2 + t, 1)],
                                       in1=x, op0=ALU.mult, op1=ALU.add).then_inc(q_res, 1)

            steps(e, HID, [(product, 0), (quantize, 1), (residual, 2)], 2, B // 2)

        M_CHAIN = 8
        L_CHAIN0 = M_CHAIN
        W_CHAIN0 = M_CHAIN + DEPTH

        block = ctx.enter_context(nc.Block())

        @block.sync
        def _(e):
            for counter in COUNTERS:
                e.sem_inc(counter, FIRST)
            e.dma_start(X[:, :], xT).then_inc(s_in, 16)
            for k in range(2):
                e.dma_start(CT[:, k, :], cT[k]).then_inc(s_in, 16)
                e.dma_start(WM[:, k, :], wmod[k]).then_inc(s_in, 16)
            e.dma_start(BO[:, 0:1], bo).then_inc(s_in, 16)
            e.dma_start(CO[:, :], cols).then_inc(s_in, 16)
            e.dma_start(TAB[:, :, :], tabs).then_inc(s_in, 16)
            e.dma_start(MSK[:, :], mask).then_inc(s_in, 16)
            e.dma_start(MAT[:, :, :], mats).then_inc(s_in, 16)
            e.dma_start(WB[:, :], w0).then_inc(s_wb, 16)
            e.dma_start(WS[:, :], wl[0, :, 0:4 * INNER]).then_inc(s_ws, 16)
            e.dma_start(WA[:, :], wl[0, :, 4 * INNER:]).then_inc(s_wa, 16)
            for i, (o, w) in enumerate(QCH):
                e.dma_start(WG[0:w, i, :, :], wgu[o:o + w, :, :]).then_inc(s_wq, 16)
            e.dma_start(WD[:, :], wd).then_inc(s_wq, 16)

            def ffn_weights(l):
                e.dma_start(W1[:, :], f1[bass.ds(l, 1)].rearrange("l p n -> (l p) n")).then_inc(s_wf, 16)
                e.dma_start(W2[:, 0:2, :], f2[bass.ds(l, 1), 0:256, :]
                            .rearrange("l (i p) n -> (l p) i n", p=P)).then_inc(s_wf, 16)
                e.dma_start(W2[0:FI - 256, 2, :], f2[bass.ds(l, 1), 256:FI, :]
                            .rearrange("l p n -> (l p) n")).then_inc(s_wf, 16)

            for k in range(LAYER0):
                barrier(e, k)
                if k == 2:
                    e.dma_start(WB[:, :], w1).then_inc(s_wb, 16)
            with e.Fori(0, DEPTH - 1) as l:
                ffn_weights(l)
                wait_apart(e, s_split, l + 1)
                e.dma_start(WS[:, :], wl[bass.ds(l + 1, 1), :, 0:4 * INNER]
                            .rearrange("l p n -> (l p) n")).then_inc(s_ws, 16)
                barrier(e, l * 2 + LAYER0)
                e.dma_start(WA[:, :], wl[bass.ds(l + 1, 1), :, 4 * INNER:]
                            .rearrange("l p n -> (l p) n")).then_inc(s_wa, 16)
                barrier(e, l * 2 + LAYER0 + 1)
            ffn_weights(DEPTH - 1)
            for k in range(2):
                barrier(e, AFTER - 2 + k)
            for k in range(4):
                barrier(e, AFTER + k)
            e.wait_ge(q_res, FIRST + B)
            e.dma_start(out, X[:, :]).then_inc(s_out, 16)
            e.wait_ge(s_out, 16)

        @block.tensor
        def _(e):
            e.wait_ge(s_m, 1)
            for k in range(2):
                for j in range(6):
                    i = e.matmul(PS[:, k, j * B:(j + 1) * B], WM[:, k, j * P:(j + 1) * P], CE[:, k, :],
                                 start=True, stop=True)
            i.then_inc(s_m, 1)
            barrier(e, 0)
            ln_pe(e, 0, X, False, 0)
            barrier(e, 1)
            block_pe(e, 0)
            barrier(e, 2)
            ln_pe(e, 1, X, False, 0)
            barrier(e, 3)
            with e.Fori(0, DEPTH) as l:
                local_pe(e, l)
                barrier(e, l * 2 + LAYER0)
                ln_pe(e, l + 2, R, True, l)
                ffn_pe(e, l)
                barrier(e, l * 2 + LAYER0 + 1)
            barrier(e, AFTER)
            ln_pe(e, DEPTH + 2, X, False, 0)
            barrier(e, AFTER + 1)
            block_pe(e, 1)
            barrier(e, AFTER + 2)
            ln_pe(e, DEPTH + 3, X, False, 0)
            barrier(e, AFTER + 3)
            fp4_pe(e)

        @block.scalar
        def _(e):
            e.preload_act_table_set("natural_log_exp_and_others")
            e.wait_ge(s_in, 16 * 10)
            e.activation(CE[:, :, :], CT[:, :, :], ACT.Exp, scale=-1.0).then_inc(s_c, 1)
            barrier(e, 0)
            ln_act(e, 0)
            barrier(e, 1)
            block_act(e, 0)
            barrier(e, 2)
            ln_act(e, 1)
            barrier(e, 3)
            with e.Fori(0, DEPTH) as l:
                e.preload_act_table_set("natural_log_exp_and_others")
                local_act(e, l)
                barrier(e, l * 2 + LAYER0)
                e.preload_act_table_set("natural_log_exp_and_others")
                ln_act(e, l + 2)
                ffn_act(e, l, l * NV)
                barrier(e, l * 2 + LAYER0 + 1)
            e.preload_act_table_set("natural_log_exp_and_others")
            barrier(e, AFTER)
            ln_act(e, DEPTH + 2)
            barrier(e, AFTER + 1)
            block_act(e, 1)
            barrier(e, AFTER + 2)
            ln_act(e, DEPTH + 3)
            barrier(e, AFTER + 3)
            e.wait_ge(s_wq, 64)
            fp4_act(e)

        @block.gpsimd
        def _(e):
            def split(l):
                wait_apart(e, s_ws, (l + 1) * 16)
                e.tensor_copy(WH[:, :], WS[:, :]).then_inc(s_hi, 1)
                e.wait_ge(s_hi, l + 1)
                e.tensor_tensor(WL[:, :], WS[:, :], WH[:, :], ALU.subtract).then_inc(s_split, 1)

            chain = Chain(e, s_pz, 0)
            for r in (slice(0, DH), slice(DH, P)):
                chain(e.memset(qz[r, :, 1 - r.start // DH, :], 0.0))
            chain(e.memset(kT[:, :, 0:WIN], 0.0))
            chain(e.memset(al[:, :, :], 0.0))
            chain(e.memset(LIM[:, :], BIG))
            chain(e.memset(LIM[:, 0:16:4], -BIG))
            chain(e.memset(WG[QCH[2][1]:P, 2, :, :], 0.0))
            barrier(e, 0)
            barrier(e, 1)
            split(0)
            block_pool(e, 0)
            barrier(e, 2)
            chain(e.memset(pt[:, :, :, :, :].rearrange("p a b c n -> p (a b c n)"), 0.0))
            chain(e.memset(xs[DH:P, 0:1], 0.0))
            for x in (XH[:, :].bitcast(F32), XL[:, :].bitcast(F32)):
                chain(e.memset(x[DH:P, 0:T:S], 0.0))
            barrier(e, 3)
            with e.Fori(0, DEPTH - 1) as l:
                local_pool(e, l)
                barrier(e, l * 2 + LAYER0)
                split(l + 1)
                barrier(e, l * 2 + LAYER0 + 1)
            local_pool(e, DEPTH - 1)
            for k in range(2):
                barrier(e, AFTER - 2 + k)
            barrier(e, AFTER)
            barrier(e, AFTER + 1)
            block_pool(e, 1)
            barrier(e, AFTER + 2)
            barrier(e, AFTER + 3)
            fp4_pool(e)

        @block.vector
        def _(e):
            def mod(k, scale, offset):
                return lambda b: (MOD[:, k, scale, b:b + 1], MOD[:, k, offset, b:b + 1])

            e.memset(BO[:, 1:2], 0.0)
            for i, v in enumerate((NFLOOR, NBIAS, LN_EPS)):
                e.memset(KC[:, i:i + 1], v)
            e.wait_ge(s_in, 16 * 10)
            e.tensor_copy(MSKB[:, :], MSK[:, :])
            e.tensor_copy(IDB[:, :], IDN)
            chain = Chain(e, s_v, 0)
            e.wait_ge(s_c, 1)
            chain(e.tensor_scalar(CE[:, :, :], CE[:, :, :], 1.0, None, ALU.add))
            chain(e.reciprocal(CR[:, :, :], CE[:, :, :]))
            e.tensor_tensor(CE[:, :, :], CT[:, :, :], CR[:, :, :], ALU.mult).then_inc(s_m, 1)
            e.wait_ge(s_m, 2)
            chain(e.tensor_copy(MOD[:, :, :, :].rearrange("p k j b -> p k (j b)"), PS[:, 0:2, 0:6 * B]))
            for j in (1, 4):
                e.tensor_scalar(MOD[:, :, j, :], MOD[:, :, j, :], 1.0, None, ALU.add)
            for i, j in enumerate((2, 5)):
                g = MOD[:, :, j, :]
                sg, ab = MT[:, 0, i, :, :], MT[:, 1, i, :, :]
                e.tensor_scalar(sg, g, 0.0, 2.0, ALU.is_ge, ALU.mult)
                chain(e.scalar_tensor_tensor(out=ab, in0=g, scalar=-1.0, in1=g, op0=ALU.mult, op1=ALU.max))
                e.tensor_scalar(sg, sg, -1.0, None, ALU.add)
                chain(e.tensor_scalar(ab, ab, 0.25, None, ALU.max))
                i = e.tensor_tensor(g, sg, ab, ALU.mult)
            chain(i)
            assert chain.n == M_CHAIN
            barrier(e, 0)
            ln_dve(e, 0, X, H, False, mod(0, 1, 0))
            barrier(e, 1)
            block_dve(e, 0)
            barrier(e, 2)
            ln_dve(e, 1, X, R, False, mod(0, 4, 3))
            barrier(e, 3)
            for c in range(NCH):
                split_tokens(e, 0, c)
            with e.Fori(0, DEPTH) as l:
                lv = l * NV
                local_dve(e, l, lv, L_CHAIN0)
                barrier(e, l * 2 + LAYER0)
                ln_dve(e, l + 2, R, H, True,
                       lambda b: (CO[:, bass.ds(lv + C_G, 1)], CO[:, bass.ds(lv + C_B, 1)]))
                ffn_dve(e, l, lv)
                barrier(e, l * 2 + LAYER0 + 1)
            for b in range(B):
                x = X[:, b * S:(b + 1) * S]
                e.scalar_tensor_tensor(out=x, in0=R[:, b * S:(b + 1) * S], scalar=MOD[:, 0, 5, b:b + 1],
                                       in1=x, op0=ALU.mult, op1=ALU.add)
            barrier(e, AFTER)
            ln_dve(e, DEPTH + 2, X, H, False, mod(1, 1, 0))
            barrier(e, AFTER + 1)
            block_dve(e, 1)
            barrier(e, AFTER + 2)
            ln_dve(e, DEPTH + 3, X, H, False, mod(1, 4, 3))
            barrier(e, AFTER + 3)
            fp4_dve(e)


def _tables():
    half = np.arange(0, DH, 2, dtype=np.float32)
    inv = (np.float32(1.0) / np.float32(10000.0) ** (half / np.float32(DH))).astype(np.float32)
    tok = np.arange(S, dtype=np.float32)
    freq = np.concatenate([tok[:, None] * inv[None, :]] * 2, -1)
    base = ((half + np.float32(0.4 * DH)) / np.float32(1.4 * DH)).astype(np.float32)
    scale = (base[None, :] ** ((tok - S // 2) / (WIN // 2))[:, None]).astype(np.float32)
    scale = np.concatenate([scale, scale], -1)
    cos, sin = np.cos(freq), np.sin(freq)
    sign = np.where(np.arange(DH) < DH // 2, -1.0, 1.0).astype(np.float32)
    qk = np.float32(8.0)
    tabs = [cos * scale * qk, cos / scale, sin * scale * sign * qk, sin / scale * sign]
    return np.stack([np.tile(t.T, (2, 1)) for t in tabs], 1).astype(np.float32)


def _mask():
    i, j = np.arange(WIN)[:, None], np.arange(2 * WIN)[None, :]
    band = np.where((j < i) | (j > i + WIN), MASKED, 0.0)
    m = np.zeros((4, WIN, 2, 2, 2 * WIN), np.float32)
    m[:] = band[None, :, None, None, :]
    m[0, :, 0, :, :WIN] = MASKED
    return m.reshape(P, 256)


def _mats():
    ones = np.kron(np.eye(2), np.ones((DH, DH)))
    return np.stack([ones, np.full((P, P), 1.0 / P), np.eye(P)], 1).astype(np.float32)


def kernel(**inputs):
    import concourse.bacc as _bacc
    from concourse.bass_utils import run_bass_kernel_spmd as _run

    a = {k: np.asarray(v) for k, v in inputs.items()}

    def chunks(w):
        return w.reshape(-1, P, w.shape[-1]).transpose(1, 0, 2).reshape(P, -1)

    w0 = np.concatenate([a["L0_attn_W" + n].reshape(INNER, P).T for n in "qkv"]
                        + [chunks(a["L0_attn_Wo"].T)], 1)
    w1 = np.concatenate([a["L1_attn_W" + n] for n in "qkv"] + [chunks(a["L1_attn_Wo"])], 1)
    qk = a["L0_ffn_Wqkv"][:, :, :2 * INNER].reshape(DEPTH, P, 2, PAIRS, 2, 2, DH // 2)
    both = np.stack([qk, qk[:, :, :, :, :, ::-1]], 2).transpose(0, 1, 4, 2, 3, 5, 6, 7)
    wl = np.concatenate([both.reshape(DEPTH, P, 4 * INNER), a["L0_ffn_Wqkv"][:, :, 2 * INNER:],
                         np.stack([chunks(w) for w in a["L0_ffn_Wo"]])], 2)
    cols = np.zeros((P, DEPTH, NV), np.float32)
    cols[:, :, C_G], cols[:, :, C_B], cols[:, :, C_B2] = (a["L0_ffn_" + n].T for n in ("ln_g", "ln_b", "b2"))
    for i, (o, w) in enumerate(FCH):
        cols[:w, :, C_B1A + i] = a["L0_ffn_b1"][:, o:o + w].T
        cols[:w, :, C_B1G + i] = a["L0_ffn_b1"][:, FI + o:FI + o + w].T
    for c, n in ((C_QS, "q_scale"), (C_KS, "k_scale")):
        v = a["L0_ffn_" + n].T
        cols[:, :, c] = np.concatenate([v, v])
        v = np.concatenate([v[DH // 2:], v[:DH // 2]])
        cols[:, :, c + 1] = np.concatenate([v, v])
    arrays = dict(
        xT=a["L0_attn_x"].transpose(2, 0, 1).reshape(P, T),
        cT=np.stack([a["L0_c"].T, a["L1_c"].T]), wmod=np.stack([a["L0_wmod"], a["L1_wmod"]]),
        bo=a["L0_attn_bo"].reshape(P, 1), w0=w0, w1=w1, wl=wl, f1=a["L0_ffn_W1"], f2=a["L0_ffn_W2"],
        cols=cols.reshape(P, DEPTH * NV), tabs=_tables(), mask=_mask(), mats=_mats(),
        wgu=np.stack([a["L1_ffn_w_gate"], a["L1_ffn_w_up"]], 1), wd=a["L1_ffn_w_down"])
    nc = _bacc.Bacc("TRN2", target_bir_lowering=False, num_devices=1)
    arrays = {f"in_{k}": np.ascontiguousarray(v) for k, v in arrays.items()}
    args = [nc.dram_tensor(k, v.shape, mybir.dt.from_np(v.dtype), kind="ExternalInput").ap()
            for k, v in arrays.items()]
    o = nc.dram_tensor("out_x", (P, T), F32, kind="ExternalOutput").ap()
    build(nc, *args, o)
    r = _run(nc, [arrays], core_ids=[0])
    y = r.results[0]["out_x"]
    return np.ascontiguousarray(y.reshape(P, B, S).transpose(1, 2, 0))
```
